# Optimizing a Trainium2 kernel written in Bass

```python
import numpy as np
import jax
import jax.numpy as jnp

def _softmax(x, axis=-1):
    return jax.nn.softmax(x, axis=axis)

def _gelu(x):
    return jax.nn.gelu(x, approximate=True)

def _silu(x):
    return jax.nn.silu(x)

def _sigmoid(x):
    return jax.nn.sigmoid(x)

def _layernorm(x, axis=-1, eps=1e-05):
    m = jnp.mean(x, axis=axis, keepdims=True)
    v = jnp.var(x, axis=axis, keepdims=True)
    return (x - m) / jnp.sqrt(v + eps)

def _scatter_add(tgt, idx, src, axis=0):
    return tgt.at[idx].add(src)

def _segment_sum(src, seg, n):
    return jax.ops.segment_sum(src, seg, n)
kernel_name = 'mk_xattn_ffn_d4_seqx_r8_385ab8'

def setup_inputs(seed: int=0):
    np.random.seed(seed)
    _w = jnp.asarray

    def _rec_inputs():
        import jax
        import jax.numpy as jnp
        _rk = jax.random.key(seed)
        x = -0.0002928 + 1 * jax.random.normal(jax.random.fold_in(_rk, 1), (4, 512, 128), jnp.float32)
        _lenS = 512 - jax.random.randint(jax.random.fold_in(_rk, 7), (4,), 0, max(1, 512 // 4) + 1, jnp.int32)
        _lenS2 = 32 - jax.random.randint(jax.random.fold_in(_rk, 8), (4,), 0, max(1, 32 // 4) + 1, jnp.int32)
        _ctx_1024P = jax.random.normal(jax.random.fold_in(_rk, 11), (4, 16, 128), jnp.float32)
        _ctx_1024c = jax.random.dirichlet(jax.random.fold_in(_rk, 511), 0.3 * jnp.ones((16,), jnp.float32), (4, 32))
        _ctx_1024t = jnp.einsum('bsk,bkd->bsd', _ctx_1024c, _ctx_1024P)
        _ctx_1024t = _ctx_1024t * jax.lax.rsqrt(jnp.mean(jnp.square(_ctx_1024t)) + 1e-12) * 0.953939
        ctx_1024 = -1.39393e-06 + 0.999914 * (_ctx_1024t + 0.3 * jax.random.normal(jax.random.fold_in(_rk, 611), (4, 32, 128), jnp.float32))
        _validS = jnp.arange(512)[None, :] < _lenS[:, None]
        _validS2 = jnp.arange(32)[None, :] < _lenS2[:, None]
        _causal = jnp.tril(jnp.ones((512, 512), dtype=bool))
        mask_BxSxS2_ik1 = jnp.where(jnp.broadcast_to(_validS2[:, None, :], (4, 512, 32)), 1, 0).astype(jnp.int32)
        mask_BxS2_bk0 = jnp.logical_not(jnp.broadcast_to(_validS2[:, :], (4, 32)))
        return (x, ctx_1024, mask_BxSxS2_ik1, mask_BxS2_bk0)
    x, ctx_1024, mask_BxSxS2_ik1, mask_BxS2_bk0 = _rec_inputs()

    def _L0_xattn_setup():
        import jax, jax.numpy as jnp
        import numpy as np
        NUM_HEADS = 16
        D_MODEL = 128
        DEPTH = D_MODEL // NUM_HEADS
        B, S = (2, 256)

        def _split_heads(x):
            b, s, _ = x.shape
            return x.reshape(b, s, NUM_HEADS, DEPTH).transpose(0, 2, 1, 3)
        key = jax.random.key(seed)
        ks = jax.random.split(key, 11)
        s = 1.0 / np.sqrt(D_MODEL)
        return {'query': jax.random.normal(ks[0], (B, S, D_MODEL), dtype=jnp.float32), 'key': jax.random.normal(ks[1], (B, S, D_MODEL), dtype=jnp.float32), 'value': jax.random.normal(ks[2], (B, S, D_MODEL), dtype=jnp.float32), 'Wq': jax.random.normal(ks[3], (D_MODEL, D_MODEL), dtype=jnp.float32) * s, 'bq': jnp.zeros((D_MODEL,), dtype=jnp.float32), 'Wk': jax.random.normal(ks[4], (D_MODEL, D_MODEL), dtype=jnp.float32) * s, 'bk': jnp.zeros((D_MODEL,), dtype=jnp.float32), 'Wv': jax.random.normal(ks[5], (D_MODEL, D_MODEL), dtype=jnp.float32) * s, 'bv': jnp.zeros((D_MODEL,), dtype=jnp.float32), 'Wo': jax.random.normal(ks[6], (D_MODEL, D_MODEL), dtype=jnp.float32) * s, 'bo': jnp.zeros((D_MODEL,), dtype=jnp.float32)}
    _L0_xattn_all = _L0_xattn_setup()
    _L0_xattn_in = {k: v for k, v in _L0_xattn_all.items() if k in ('Wq', 'bq', 'Wk', 'bk', 'Wv', 'bv', 'Wo', 'bo')}
    del _L0_xattn_all

    def _L0_ffn_setup():
        import math
        import jax, jax.numpy as jnp
        import numpy as np
        D_MODEL = 128
        D_HIDDEN = 256
        N_EXPERTS = 8
        TOP_K = 2
        CAPACITY_FACTOR = 1.25

        def _moe_forward(x, w_router, w_gate, w_down):
            B, T, D = x.shape
            N = B * T
            xf = x.reshape(N, D)
            logits = xf.astype(jnp.float32) @ w_router.T
            gates = jax.nn.softmax(logits, axis=-1)
            topk_gates, topk_idx = jax.lax.top_k(gates, TOP_K)
            expert_mask = jax.nn.one_hot(topk_idx, N_EXPERTS, dtype=jnp.int32).sum(axis=1)
            capacity = math.ceil(N / N_EXPERTS * CAPACITY_FACTOR)
            position_in_expert = jnp.cumsum(expert_mask, axis=0) - 1
            expert_mask = expert_mask * (position_in_expert < capacity)
            keep = jnp.take_along_axis(expert_mask, topk_idx, axis=1) > 0
            topk_gates = topk_gates * keep
            topk_gates = topk_gates / (topk_gates.sum(axis=-1, keepdims=True) + 1e-06)
            hidden = jax.nn.silu(xf @ w_gate.T)
            combine = (topk_gates[:, :, None] * jax.nn.one_hot(topk_idx, N_EXPERTS, dtype=topk_gates.dtype)).sum(axis=1)
            y = jnp.zeros((N, D), dtype=x.dtype)
            for e in range(N_EXPERTS):
                y = y + combine[:, e:e + 1] * (hidden @ w_down[e].T)
            return y.reshape(B, T, D)
        key = jax.random.key(seed)
        k0, k1, k2, k3 = jax.random.split(key, 4)
        B, T = (2, 256)
        x = jax.random.normal(k0, (B, T, D_MODEL), dtype=jnp.float32)
        w_router = jax.random.normal(k1, (N_EXPERTS, D_MODEL), dtype=jnp.float32) * 0.02
        w_gate = jax.random.normal(k2, (D_HIDDEN, D_MODEL), dtype=jnp.float32) * 0.02
        w_down = jax.random.normal(k3, (N_EXPERTS, D_MODEL, D_HIDDEN), dtype=jnp.float32) * 0.02
        return {'x': x, 'w_router': w_router, 'w_gate': w_gate, 'w_down': w_down}
    _L0_ffn_all = _L0_ffn_setup()
    _L0_ffn_in = {k: v for k, v in _L0_ffn_all.items() if k in ('w_router', 'w_gate', 'w_down')}
    del _L0_ffn_all

    def _L1_xattn_setup():
        import jax, jax.numpy as jnp
        import numpy as np
        B, S, E, A = (4, 256, 128, 128)
        key = jax.random.key(seed)
        ks = jax.random.split(key, 10)
        bound = 1.0 / np.sqrt(E)
        return {'query': jax.random.normal(ks[0], (B, S, E), dtype=jnp.float32), 'key': jax.random.normal(ks[1], (B, S, E), dtype=jnp.float32), 'value': jax.random.normal(ks[2], (B, S, E), dtype=jnp.float32), 'mask': jax.random.randint(ks[3], (B, S, S), 0, 2, dtype=jnp.int32), 'Wq': jax.random.uniform(ks[4], (A, E), jnp.float32, -bound, bound), 'bq': jax.random.uniform(ks[5], (A,), jnp.float32, -bound, bound), 'Wk': jax.random.uniform(ks[6], (A, E), jnp.float32, -bound, bound), 'bk': jax.random.uniform(ks[7], (A,), jnp.float32, -bound, bound), 'Wv': jax.random.uniform(ks[8], (A, E), jnp.float32, -bound, bound), 'bv': jax.random.uniform(ks[9], (A,), jnp.float32, -bound, bound)}
    _L1_xattn_all = _L1_xattn_setup()
    _L1_xattn_in = {k: v for k, v in _L1_xattn_all.items() if k in ('Wq', 'bq', 'Wk', 'bk', 'Wv', 'bv')}
    del _L1_xattn_all

    def _L1_ffn_setup():
        import jax, jax.numpy as jnp
        import numpy as np
        D_MODEL, FF_DIM = (128, 256)
        N_SHARED, N_ROUTED, TOP_K = (1, 8, 2)
        BATCH, SEQ = (2, 256)
        key = jax.random.key(seed)
        ks = jax.random.split(key, 8)
        init = lambda k, shape: jax.random.normal(k, shape, jnp.float32) * 0.02
        x = jax.random.normal(ks[0], (BATCH, SEQ, D_MODEL), jnp.float32)
        Wg = init(ks[1], (D_MODEL, N_ROUTED))
        Ws1 = init(ks[2], (D_MODEL, FF_DIM))
        Ws3 = init(ks[3], (D_MODEL, FF_DIM))
        Ws2 = init(ks[4], (FF_DIM, D_MODEL))
        We1 = init(ks[5], (N_ROUTED, D_MODEL, FF_DIM))
        We3 = init(ks[6], (N_ROUTED, D_MODEL, FF_DIM))
        We2 = init(ks[7], (N_ROUTED, FF_DIM, D_MODEL))
        return {'x': x, 'Wg': Wg, 'Ws1': Ws1, 'Ws3': Ws3, 'Ws2': Ws2, 'We1': We1, 'We3': We3, 'We2': We2}
    _L1_ffn_all = _L1_ffn_setup()
    _L1_ffn_in = {k: v for k, v in _L1_ffn_all.items() if k in ('Wg', 'Ws1', 'Ws3', 'Ws2', 'We1', 'We3', 'We2')}
    del _L1_ffn_all

    def _L2_xattn_setup():
        import jax, jax.numpy as jnp
        import numpy as np
        DIM = 128
        HEADS = 16
        HEAD_DIM = DIM // HEADS
        B, N, S = (4, 512, 64)
        key = jax.random.key(seed)
        ks = jax.random.split(key, 9)
        scale = DIM ** (-0.5)
        return {'x': jax.random.normal(ks[0], (B, N, DIM), dtype=jnp.float32), 'context': jax.random.normal(ks[1], (B, S, DIM), dtype=jnp.float32), 'context_mask': jax.random.uniform(ks[2], (B, S)) < 0.2, 'q_w': jax.random.normal(ks[3], (DIM, DIM), dtype=jnp.float32) * scale, 'q_b': jnp.zeros((DIM,), dtype=jnp.float32), 'kv_w': jax.random.normal(ks[4], (DIM, 2 * DIM), dtype=jnp.float32) * scale, 'kv_b': jnp.zeros((2 * DIM,), dtype=jnp.float32), 'proj_w': jax.random.normal(ks[5], (DIM, DIM), dtype=jnp.float32) * scale, 'proj_b': jnp.zeros((DIM,), dtype=jnp.float32)}
    _L2_xattn_all = _L2_xattn_setup()
    _L2_xattn_in = {k: v for k, v in _L2_xattn_all.items() if k in ('q_w', 'q_b', 'kv_w', 'kv_b', 'proj_w', 'proj_b')}
    del _L2_xattn_all

    def _L2_ffn_setup():
        import jax, jax.numpy as jnp
        import numpy as np
        LN_EPS = 1e-05

        def layer_norm(x, g, b):
            mu = jnp.mean(x, axis=-1, keepdims=True)
            var = jnp.mean(jnp.square(x - mu), axis=-1, keepdims=True)
            return (x - mu) * jax.lax.rsqrt(var + LN_EPS) * g + b

        def ternary_quant(w):
            scale = 1.0 / jnp.clip(jnp.mean(jnp.abs(w)), 1e-05)
            wq = jnp.clip(jnp.round(w * scale), -1.0, 1.0) / scale
            return w + jax.lax.stop_gradient(wq - w)
        key = jax.random.key(seed)
        ks = jax.random.split(key, 3)
        dim, hidden = (128, 512)
        B, S = (8, 128)
        x = jax.random.normal(ks[0], (B, S, dim), dtype=jnp.float32)
        w1 = jax.random.normal(ks[1], (hidden, dim), dtype=jnp.float32) * 0.02
        w2 = jax.random.normal(ks[2], (dim, hidden), dtype=jnp.float32) * 0.02
        return {'x': x, 'ln1_g': jnp.ones((dim,), jnp.float32), 'ln1_b': jnp.zeros((dim,), jnp.float32), 'w1': w1, 'b1': jnp.zeros((hidden,), jnp.float32), 'ln2_g': jnp.ones((hidden,), jnp.float32), 'ln2_b': jnp.zeros((hidden,), jnp.float32), 'w2': w2, 'b2': jnp.zeros((dim,), jnp.float32)}
    _L2_ffn_all = _L2_ffn_setup()
    _L2_ffn_in = {k: v for k, v in _L2_ffn_all.items() if k in ('ln1_g', 'ln1_b', 'w1', 'b1', 'ln2_g', 'ln2_b', 'w2', 'b2')}
    del _L2_ffn_all

    def _L3_xattn_setup():
        import jax, jax.numpy as jnp
        import numpy as np
        D_MODEL = 128
        N_HEADS = 16
        D_K = D_MODEL // N_HEADS

        def _split_heads(x):
            B, S, _ = x.shape
            return x.reshape(B, S, N_HEADS, D_K).transpose(0, 2, 1, 3)
        key = jax.random.key(seed)
        ks = jax.random.split(key, 11)
        B, S = (4, 256)
        scale = 1.0 / np.sqrt(D_MODEL)
        inp = {'q': jax.random.normal(ks[0], (B, S, D_MODEL), dtype=jnp.float32), 'k': jax.random.normal(ks[1], (B, S, D_MODEL), dtype=jnp.float32), 'v': jax.random.normal(ks[2], (B, S, D_MODEL), dtype=jnp.float32), 'w_q': jax.random.normal(ks[3], (D_MODEL, D_MODEL), dtype=jnp.float32) * scale, 'b_q': jnp.zeros((D_MODEL,), dtype=jnp.float32), 'w_k': jax.random.normal(ks[4], (D_MODEL, D_MODEL), dtype=jnp.float32) * scale, 'b_k': jnp.zeros((D_MODEL,), dtype=jnp.float32), 'w_v': jax.random.normal(ks[5], (D_MODEL, D_MODEL), dtype=jnp.float32) * scale, 'b_v': jnp.zeros((D_MODEL,), dtype=jnp.float32), 'w_o': jax.random.normal(ks[6], (D_MODEL, D_MODEL), dtype=jnp.float32) * scale, 'b_o': jnp.zeros((D_MODEL,), dtype=jnp.float32)}
        return inp
    _L3_xattn_all = _L3_xattn_setup()
    _L3_xattn_in = {k: v for k, v in _L3_xattn_all.items() if k in ('w_q', 'b_q', 'w_k', 'b_k', 'w_v', 'b_v', 'w_o', 'b_o')}
    del _L3_xattn_all

    def _L3_ffn_setup():
        import jax, jax.numpy as jnp
        import numpy as np
        D = 128
        H = 512
        E = 12
        K = 3
        B, S = (1, 256)
        key = jax.random.key(seed)
        ks = jax.random.split(key, 6)
        scale = 0.02
        x = jax.random.normal(ks[0], (B, S, D), dtype=jnp.float32)
        Wg = jax.random.normal(ks[1], (D, E), dtype=jnp.float32) * scale
        Wup = jax.random.normal(ks[2], (E, D, H), dtype=jnp.float32) * scale
        bup = jax.random.normal(ks[3], (E, H), dtype=jnp.float32) * scale
        Wdown = jax.random.normal(ks[4], (E, H, D), dtype=jnp.float32) * scale
        bdown = jax.random.normal(ks[5], (E, D), dtype=jnp.float32) * scale
        return {'x': x, 'Wg': Wg, 'Wup': Wup, 'bup': bup, 'Wdown': Wdown, 'bdown': bdown}
    _L3_ffn_all = _L3_ffn_setup()
    _L3_ffn_in = {k: v for k, v in _L3_ffn_all.items() if k in ('Wg', 'Wup', 'bup', 'Wdown', 'bdown')}
    del _L3_ffn_all
    return {'x': x, 'ctx_1024': ctx_1024, 'mask_BxSxS2_ik1': mask_BxSxS2_ik1, 'mask_BxS2_bk0': mask_BxS2_bk0, 'L0_xattn_Wq': _L0_xattn_in['Wq'], 'L0_xattn_bq': _L0_xattn_in['bq'], 'L0_xattn_Wk': _L0_xattn_in['Wk'], 'L0_xattn_bk': _L0_xattn_in['bk'], 'L0_xattn_Wv': _L0_xattn_in['Wv'], 'L0_xattn_bv': _L0_xattn_in['bv'], 'L0_xattn_Wo': _L0_xattn_in['Wo'], 'L0_xattn_bo': _L0_xattn_in['bo'], 'L0_ffn_w_router': _L0_ffn_in['w_router'], 'L0_ffn_w_gate': _L0_ffn_in['w_gate'], 'L0_ffn_w_down': _L0_ffn_in['w_down'], 'L1_xattn_Wq': _L1_xattn_in['Wq'], 'L1_xattn_bq': _L1_xattn_in['bq'], 'L1_xattn_Wk': _L1_xattn_in['Wk'], 'L1_xattn_bk': _L1_xattn_in['bk'], 'L1_xattn_Wv': _L1_xattn_in['Wv'], 'L1_xattn_bv': _L1_xattn_in['bv'], 'L1_ffn_Wg': _L1_ffn_in['Wg'], 'L1_ffn_Ws1': _L1_ffn_in['Ws1'], 'L1_ffn_Ws3': _L1_ffn_in['Ws3'], 'L1_ffn_Ws2': _L1_ffn_in['Ws2'], 'L1_ffn_We1': _L1_ffn_in['We1'], 'L1_ffn_We3': _L1_ffn_in['We3'], 'L1_ffn_We2': _L1_ffn_in['We2'], 'L2_xattn_q_w': _L2_xattn_in['q_w'], 'L2_xattn_q_b': _L2_xattn_in['q_b'], 'L2_xattn_kv_w': _L2_xattn_in['kv_w'], 'L2_xattn_kv_b': _L2_xattn_in['kv_b'], 'L2_xattn_proj_w': _L2_xattn_in['proj_w'], 'L2_xattn_proj_b': _L2_xattn_in['proj_b'], 'L2_ffn_ln1_g': _L2_ffn_in['ln1_g'], 'L2_ffn_ln1_b': _L2_ffn_in['ln1_b'], 'L2_ffn_w1': _L2_ffn_in['w1'], 'L2_ffn_b1': _L2_ffn_in['b1'], 'L2_ffn_ln2_g': _L2_ffn_in['ln2_g'], 'L2_ffn_ln2_b': _L2_ffn_in['ln2_b'], 'L2_ffn_w2': _L2_ffn_in['w2'], 'L2_ffn_b2': _L2_ffn_in['b2'], 'L3_xattn_w_q': _L3_xattn_in['w_q'], 'L3_xattn_b_q': _L3_xattn_in['b_q'], 'L3_xattn_w_k': _L3_xattn_in['w_k'], 'L3_xattn_b_k': _L3_xattn_in['b_k'], 'L3_xattn_w_v': _L3_xattn_in['w_v'], 'L3_xattn_b_v': _L3_xattn_in['b_v'], 'L3_xattn_w_o': _L3_xattn_in['w_o'], 'L3_xattn_b_o': _L3_xattn_in['b_o'], 'L3_ffn_Wg': _L3_ffn_in['Wg'], 'L3_ffn_Wup': _L3_ffn_in['Wup'], 'L3_ffn_bup': _L3_ffn_in['bup'], 'L3_ffn_Wdown': _L3_ffn_in['Wdown'], 'L3_ffn_bdown': _L3_ffn_in['bdown']}

def reference(x, ctx_1024, mask_BxSxS2_ik1, mask_BxS2_bk0, L0_xattn_Wq, L0_xattn_bq, L0_xattn_Wk, L0_xattn_bk, L0_xattn_Wv, L0_xattn_bv, L0_xattn_Wo, L0_xattn_bo, L0_ffn_w_router, L0_ffn_w_gate, L0_ffn_w_down, L1_xattn_Wq, L1_xattn_bq, L1_xattn_Wk, L1_xattn_bk, L1_xattn_Wv, L1_xattn_bv, L1_ffn_Wg, L1_ffn_Ws1, L1_ffn_Ws3, L1_ffn_Ws2, L1_ffn_We1, L1_ffn_We3, L1_ffn_We2, L2_xattn_q_w, L2_xattn_q_b, L2_xattn_kv_w, L2_xattn_kv_b, L2_xattn_proj_w, L2_xattn_proj_b, L2_ffn_ln1_g, L2_ffn_ln1_b, L2_ffn_w1, L2_ffn_b1, L2_ffn_ln2_g, L2_ffn_ln2_b, L2_ffn_w2, L2_ffn_b2, L3_xattn_w_q, L3_xattn_b_q, L3_xattn_w_k, L3_xattn_b_k, L3_xattn_w_v, L3_xattn_b_v, L3_xattn_w_o, L3_xattn_b_o, L3_ffn_Wg, L3_ffn_Wup, L3_ffn_bup, L3_ffn_Wdown, L3_ffn_bdown):
    import jax
    import jax.numpy as jnp

    def _L0_xattn_ref(query, key, value, Wq, bq, Wk, bk, Wv, bv, Wo, bo):
        import jax, jax.numpy as jnp
        import numpy as np
        NUM_HEADS = 16
        D_MODEL = 128
        DEPTH = D_MODEL // NUM_HEADS
        B, S = (2, 256)

        def _split_heads(x):
            b, s, _ = x.shape
            return x.reshape(b, s, NUM_HEADS, DEPTH).transpose(0, 2, 1, 3)
        q = _split_heads(query @ Wq + bq)
        k = _split_heads(key @ Wk + bk)
        v = _split_heads(value @ Wv + bv)
        scores = jnp.einsum('bhqd,bhkd->bhqk', q, k)
        attn = jax.nn.softmax(scores, axis=-1)
        out = jnp.einsum('bhqk,bhkd->bhqd', attn, v)
        out = out.transpose(0, 2, 1, 3).reshape(query.shape[0], -1, D_MODEL)
        return out @ Wo + bo

    def _L0_ffn_ref(x, w_router, w_gate, w_down):
        import math
        import jax, jax.numpy as jnp
        import numpy as np
        D_MODEL = 128
        D_HIDDEN = 256
        N_EXPERTS = 8
        TOP_K = 2
        CAPACITY_FACTOR = 1.25

        def _moe_forward(x, w_router, w_gate, w_down):
            B, T, D = x.shape
            N = B * T
            xf = x.reshape(N, D)
            logits = xf.astype(jnp.float32) @ w_router.T
            gates = jax.nn.softmax(logits, axis=-1)
            topk_gates, topk_idx = jax.lax.top_k(gates, TOP_K)
            expert_mask = jax.nn.one_hot(topk_idx, N_EXPERTS, dtype=jnp.int32).sum(axis=1)
            capacity = math.ceil(N / N_EXPERTS * CAPACITY_FACTOR)
            position_in_expert = jnp.cumsum(expert_mask, axis=0) - 1
            expert_mask = expert_mask * (position_in_expert < capacity)
            keep = jnp.take_along_axis(expert_mask, topk_idx, axis=1) > 0
            topk_gates = topk_gates * keep
            topk_gates = topk_gates / (topk_gates.sum(axis=-1, keepdims=True) + 1e-06)
            hidden = jax.nn.silu(xf @ w_gate.T)
            combine = (topk_gates[:, :, None] * jax.nn.one_hot(topk_idx, N_EXPERTS, dtype=topk_gates.dtype)).sum(axis=1)
            y = jnp.zeros((N, D), dtype=x.dtype)
            for e in range(N_EXPERTS):
                y = y + combine[:, e:e + 1] * (hidden @ w_down[e].T)
            return y.reshape(B, T, D)
        return _moe_forward(x, w_router, w_gate, w_down)

    def _L1_xattn_ref(query, key, value, mask, Wq, bq, Wk, bk, Wv, bv):
        import jax, jax.numpy as jnp
        import numpy as np
        B, S, E, A = (4, 256, 128, 128)
        scale = jnp.sqrt(jnp.asarray(A, dtype=jnp.float32))
        q = jnp.einsum('bse,ae->bsa', query, Wq) + bq
        k = jnp.einsum('bse,ae->bsa', key, Wk) + bk
        v = jnp.einsum('bse,ae->bsa', value, Wv) + bv
        scores = jnp.einsum('bqa,bka->bqk', q, k) / scale
        scores = jnp.where(mask == 0, jnp.float32(-10000000000.0), scores)
        attn = jax.nn.softmax(scores, axis=-1)
        return jnp.einsum('bqk,bka->bqa', attn, v)

    def _L1_ffn_ref(x, Wg, Ws1, Ws3, Ws2, We1, We3, We2):
        import jax, jax.numpy as jnp
        import numpy as np
        D_MODEL, FF_DIM = (128, 256)
        N_SHARED, N_ROUTED, TOP_K = (1, 8, 2)
        BATCH, SEQ = (2, 256)
        B, S, d = x.shape
        E = Wg.shape[1]
        xf = x.reshape(-1, d)
        T = xf.shape[0]
        gates = jax.nn.sigmoid(xf @ Wg)
        vals, idx = jax.lax.top_k(gates, TOP_K)
        vals = vals / vals.sum(axis=-1, keepdims=True)
        w = jnp.zeros((T, E), x.dtype).at[jnp.arange(T)[:, None], idx].add(vals)
        shared = jax.nn.silu(xf @ Ws1) * (xf @ Ws3) @ Ws2
        h = jax.nn.silu(jnp.einsum('td,edf->tef', xf, We1)) * jnp.einsum('td,edf->tef', xf, We3)
        routed = jnp.einsum('tef,efd,te->td', h, We2, w)
        out = (shared + routed) / (N_SHARED + TOP_K)
        return out.reshape(B, S, d)

    def _L2_xattn_ref(x, context, context_mask, q_w, q_b, kv_w, kv_b, proj_w, proj_b):
        import jax, jax.numpy as jnp
        import numpy as np
        DIM = 128
        HEADS = 16
        HEAD_DIM = DIM // HEADS
        B, N, S = (4, 512, 64)
        b, n, c = x.shape
        s = context.shape[1]
        h, d = (HEADS, HEAD_DIM)
        scale = d ** (-0.5)
        q = (x @ q_w + q_b).reshape(b, n, h, d)
        kv = (context @ kv_w + kv_b).reshape(b, s, 2, h, d)
        k = kv[:, :, 0]
        v = kv[:, :, 1]
        attn = jnp.einsum('bnhd,bshd->bhns', q, k) * scale
        attn = jnp.where(context_mask[:, None, None, :], -jnp.inf, attn)
        attn = jax.nn.softmax(attn, axis=-1)
        out = jnp.einsum('bhns,bshd->bnhd', attn, v).reshape(b, n, c)
        return out @ proj_w + proj_b

    def _L2_ffn_ref(x, ln1_g, ln1_b, w1, b1, ln2_g, ln2_b, w2, b2):
        import jax, jax.numpy as jnp
        import numpy as np
        LN_EPS = 1e-05

        def layer_norm(x, g, b):
            mu = jnp.mean(x, axis=-1, keepdims=True)
            var = jnp.mean(jnp.square(x - mu), axis=-1, keepdims=True)
            return (x - mu) * jax.lax.rsqrt(var + LN_EPS) * g + b

        def ternary_quant(w):
            scale = 1.0 / jnp.clip(jnp.mean(jnp.abs(w)), 1e-05)
            wq = jnp.clip(jnp.round(w * scale), -1.0, 1.0) / scale
            return w + jax.lax.stop_gradient(wq - w)
        h = layer_norm(x, ln1_g, ln1_b)
        h = jnp.einsum('bsd,hd->bsh', h, ternary_quant(w1)) + b1
        h = jax.nn.gelu(h, approximate=False)
        h = layer_norm(h, ln2_g, ln2_b)
        out = jnp.einsum('bsh,dh->bsd', h, ternary_quant(w2)) + b2
        return out

    def _L3_xattn_ref(q, k, v, w_q, b_q, w_k, b_k, w_v, b_v, w_o, b_o):
        import jax, jax.numpy as jnp
        import numpy as np
        D_MODEL = 128
        N_HEADS = 16
        D_K = D_MODEL // N_HEADS

        def _split_heads(x):
            B, S, _ = x.shape
            return x.reshape(B, S, N_HEADS, D_K).transpose(0, 2, 1, 3)
        qh = _split_heads(q @ w_q.T + b_q)
        kh = _split_heads(k @ w_k.T + b_k)
        vh = _split_heads(v @ w_v.T + b_v)
        scores = jnp.einsum('bhqd,bhkd->bhqk', qh, kh) / np.sqrt(D_K)
        attn = jax.nn.softmax(scores, axis=-1)
        out = jnp.einsum('bhqk,bhkd->bhqd', attn, vh)
        B, H, S, Dk = out.shape
        out = out.transpose(0, 2, 1, 3).reshape(B, S, H * Dk)
        return out @ w_o.T + b_o

    def _L3_ffn_ref(x, Wg, Wup, bup, Wdown, bdown):
        import jax, jax.numpy as jnp
        import numpy as np
        D = 128
        H = 512
        E = 12
        K = 3
        B, S = (1, 256)
        gate_logits = jnp.einsum('bsd,de->bse', x, Wg)
        topw, sel = jax.lax.top_k(gate_logits, K)
        topw = jax.nn.softmax(topw.astype(jnp.float32), axis=-1).astype(x.dtype)
        cw = jnp.einsum('bsk,bske->bse', topw, jax.nn.one_hot(sel, E, dtype=x.dtype))
        h = jax.nn.gelu(jnp.einsum('bsd,edh->ebsh', x, Wup) + bup[:, None, None, :], approximate=False)
        y = jnp.einsum('ebsh,ehd->ebsd', h, Wdown) + bdown[:, None, None, :]
        return jnp.einsum('bse,ebsd->bsd', cw, y)
    x = x + _L0_xattn_ref(_layernorm(x, axis=-1), ctx_1024, ctx_1024, L0_xattn_Wq, L0_xattn_bq, L0_xattn_Wk, L0_xattn_bk, L0_xattn_Wv, L0_xattn_bv, L0_xattn_Wo, L0_xattn_bo)
    x = x + _L0_ffn_ref(_layernorm(x, axis=-1), L0_ffn_w_router, L0_ffn_w_gate, L0_ffn_w_down)
    x = x + _L1_xattn_ref(_layernorm(x, axis=-1), ctx_1024, ctx_1024, mask_BxSxS2_ik1, L1_xattn_Wq, L1_xattn_bq, L1_xattn_Wk, L1_xattn_bk, L1_xattn_Wv, L1_xattn_bv)
    x = x + _L1_ffn_ref(_layernorm(x, axis=-1), L1_ffn_Wg, L1_ffn_Ws1, L1_ffn_Ws3, L1_ffn_Ws2, L1_ffn_We1, L1_ffn_We3, L1_ffn_We2)
    x = x + _L2_xattn_ref(_layernorm(x, axis=-1), ctx_1024, mask_BxS2_bk0, L2_xattn_q_w, L2_xattn_q_b, L2_xattn_kv_w, L2_xattn_kv_b, L2_xattn_proj_w, L2_xattn_proj_b)
    x = x + _L2_ffn_ref(_layernorm(x, axis=-1), L2_ffn_ln1_g, L2_ffn_ln1_b, L2_ffn_w1, L2_ffn_b1, L2_ffn_ln2_g, L2_ffn_ln2_b, L2_ffn_w2, L2_ffn_b2)
    x = x + _L3_xattn_ref(_layernorm(x, axis=-1), ctx_1024, ctx_1024, L3_xattn_w_q, L3_xattn_b_q, L3_xattn_w_k, L3_xattn_b_k, L3_xattn_w_v, L3_xattn_b_v, L3_xattn_w_o, L3_xattn_b_o)
    x = x + _L3_ffn_ref(_layernorm(x, axis=-1), L3_ffn_Wg, L3_ffn_Wup, L3_ffn_bup, L3_ffn_Wdown, L3_ffn_bdown)
    return x

_drawn_inputs = setup_inputs


def setup_inputs(seed=0):
    import zlib

    import numpy as np

    out = dict(_drawn_inputs(seed))
    spreads = {'L0_xattn_bq': (0.0, 0.1),
     'L0_xattn_bk': (0.0, 2.0),
     'L0_xattn_bv': (0.0, 0.1),
     'L0_xattn_bo': (0.0, 0.1),
     'L2_xattn_q_b': (0.0, 0.484),
     'L2_xattn_kv_b': (0.0, 0.1),
     'L2_xattn_proj_b': (0.0, 0.1),
     'L2_ffn_ln1_g': (1.0, 0.6),
     'L2_ffn_ln1_b': (0.0, 0.474),
     'L2_ffn_b1': (0.0, 0.1),
     'L2_ffn_ln2_g': (1.0, 0.6),
     'L2_ffn_ln2_b': (0.0, 0.467),
     'L2_ffn_b2': (0.0, 0.1),
     'L3_xattn_b_q': (0.0, 0.506),
     'L3_xattn_b_k': (0.0, 2.0),
     'L3_xattn_b_v': (0.0, 0.1),
     'L3_xattn_b_o': (0.0, 0.1)}
    factors = {'L0_ffn_w_router': 3.36,
     'L0_ffn_w_gate': 3.197,
     'L0_ffn_w_down': 3.183,
     'L1_xattn_bq': 8.0,
     'L1_xattn_bk': 64.0,
     'L1_ffn_Wg': 8.0,
     'L1_ffn_Ws1': 8.0,
     'L1_ffn_Ws3': 8.0,
     'L1_ffn_Ws2': 8.0,
     'L1_ffn_We1': 8.0,
     'L1_ffn_We3': 8.0,
     'L1_ffn_We2': 8.0,
     'L3_ffn_Wg': 3.058,
     'L3_ffn_Wup': 2.893,
     'L3_ffn_bup': 8.0,
     'L3_ffn_Wdown': 2.844,
     'L3_ffn_bdown': 7.698}
    for name, (base, spread) in spreads.items():
        noise = np.random.default_rng([zlib.crc32(name.encode()), seed]).standard_normal(out[name].shape)
        drawn = base * np.exp(spread * noise) if base else spread * noise
        out[name] = jnp.asarray(drawn.astype(out[name].dtype))
    for name, factor in factors.items():
        out[name] = (out[name] * factor).astype(out[name].dtype)
    return out
```

```python
import concourse.bass as bass
import numpy as np
from concourse import mybir
from contextlib import ExitStack

F32 = mybir.dt.float32
F16 = mybir.dt.float16
BF16 = mybir.dt.bfloat16
I32 = mybir.dt.int32
U32 = mybir.dt.uint32
U8 = mybir.dt.uint8
ALU = mybir.AluOpType
ACT = mybir.ActivationFunctionType
AX = mybir.AxisListType.X

P = 128
BATCHES, SEQ, KEYS = 4, 512, 32
TILES = SEQ // P
NTILES = BATCHES * TILES
HEADS, DEPTH = 16, 8
QUADS = 4
VCOLS = 36
E0, E1, E3 = 8, 8, 12
S1 = E1 + 1
CAPACITY = -(-BATCHES * SEQ * 5 // (E0 * 4))
WSCALE = 64.0
EPS = 1e-5
MAGIC = float(0x5F3759DF)

W_GATE = 0
W_DOWN0 = W_GATE + 256
W_1 = W_DOWN0 + 2 * E0 * P
W_3 = W_1 + S1 * 256
W_2 = W_3 + S1 * 256
W_UP = W_2 + S1 * 256
W_DOWN3 = W_UP + E3 * 512
W_COLS = W_DOWN3 + E3 * 512
PIECE = 384
PIECES = W_COLS // PIECE
PIECES_L0 = -(-W_1 // PIECE)
PIECES_L1 = -(-W_UP // PIECE)

Q, K, V, O = 0, 1, 2, 3
ATT_AT = {0: 0, 1: 4, 2: 7, 3: 11}
C_BQ = {0: 0, 1: 2, 2: 4, 3: 6}
C_BK = {0: 1, 1: 3, 2: 5, 3: 7}
C_G1, C_B1, C_G2, C_B2, C_BUP = 8, 9, 10, 14, 18
C_COLS = C_BUP + 4 * E3
R_BV = {0: 0, 1: 128, 2: 256, 3: 384}
R_BO = {0: 512, 2: 640, 3: 768}
R_B2, R_B1 = 896, 1024
R_COLS = 1536
K_ID, K_TRI, K_HEAD, K_QUAD, K_IOTA = 0, 128, 256, 272, 276
K_COLS = K_IOTA + 12
STAGES = 8


class Chain:

    def __init__(self, eng, sem, per, rnd):
        self.eng, self.sem, self.per, self.rnd, self.at = eng, sem, per, rnd, 0

    def then(self, ins):
        self.at += 1
        ins.then_inc(self.sem, 1)
        self.eng.wait_ge(self.sem, self.rnd * self.per + self.at)

    def done(self):
        assert self.at == self.per, (self.at, self.per)


def bcast(ap, axis, count):
    shape = list(ap.shape)
    shape.insert(axis, count)
    return ap.unsqueeze(axis).to_broadcast(shape)


def build(nc, x, ctx, attw, cols, rows, router, moe_w, mlp_w, bdown, mask1, mask2, consts, out):
    stack = ExitStack()
    with stack:
        def sb(name, shape, dt=F32):
            return stack.enter_context(nc.sbuf_tensor(name, shape, dt))

        def sem(name):
            return stack.enter_context(nc.semaphore(name))

        def sems(prefix, *names):
            return {n: sem(f"{prefix}_{n}") for n in names}

        X = sb("X", [P, NTILES, P])
        ctxT = sb("ctxT", [P, BATCHES, QUADS, KEYS])
        aw = sb("aw", [P, 15, P])
        col = sb("col", [P, C_COLS])
        row = sb("row", [P, R_COLS])
        wr = sb("wr", [P, E0 + E1 + E3])
        raw = [sb(f"raw{i}", [P, PIECE]) for i in range(2)]
        scaled = [sb(f"scaled{i}", [P, PIECE]) for i in range(2)]
        scale64 = sb("scale64", [P, 1])
        WH = sb("WH", [P, W_COLS], F16)
        WL = sb("WL", [P, W_COLS], F16)
        mw = sb("mw", [P, 2, 512])
        bd = sb("bd", [E3, P])
        m1 = sb("m1", [P, NTILES, KEYS], I32)
        m2 = sb("m2", [1, BATCHES, KEYS], U8)
        kc = sb("kc", [P, K_COLS])
        ident = kc[:, K_ID:K_ID + P]
        headm = kc[:, K_HEAD:K_HEAD + HEADS]
        quadm = kc[:, K_QUAD:K_QUAD + QUADS]
        iota = kc[:, K_IOTA:K_IOTA + 12]
        tri16 = sb("tri16", [P, P], F16)
        ones16 = sb("ones16", [P, P], F16)
        ones = sb("ones", [P, P])
        onesb = sb("onesb", [1, P], BF16)
        m2b = sb("m2b", [1, BATCHES, HEADS, KEYS], BF16)
        kT = sb("kT", [P, 4, BATCHES, KEYS])
        kbd02 = sb("kbd02", [P, BATCHES, HEADS, KEYS])
        kbd = {0: kbd02, 2: kbd02, 3: sb("kbd3", [P, BATCHES, HEADS, KEYS])}
        vbd = {l: sb(f"vbd{l}", [P, BATCHES, QUADS, VCOLS]) for l in (0, 2, 3)}
        v1 = sb("v1", [KEYS, BATCHES, P])
        xn = sb("xn", [P, TILES, P])
        xnT = sb("xnT", [P, SEQ])
        xh = sb("xh", [P, BATCHES, SEQ], F16)
        xl = sb("xl", [P, BATCHES, SEQ], F16)
        qT = sb("qT", [P, SEQ])
        big = sb("big", [P, 2, 4, SEQ])
        sub = [big[:, 0, j, :].rearrange("p (h k) -> p h k", k=KEYS) for j in range(2)]
        prob = [big[:, 0, 2 + j, :] for j in range(2)]
        probT = [big[:, 1, j, :].rearrange("p (c t) -> p c t", t=P) for j in range(2)]
        hh = sb("hh", [P, 2, 4, SEQ], F16)
        hl = sb("hl", [P, 2, 4, SEQ], F16)
        mx = sb("mx", [P, 2, HEADS])
        rinv = sb("rinv", [P, QUADS, 4])
        o = sb("o", [P, TILES, P])
        vrep = o
        oT = sb("oT", [P, SEQ])
        cwT = oT[0:E3, :]
        p1T = oT[0:KEYS, :]
        stats = sb("stats", [P, TILES, 6])
        mean = sb("mean", [P, TILES])
        var = sb("var", [P, TILES])
        rstd = sb("rstd", [P, TILES])
        tmp4 = sb("tmp4", [P, TILES])
        gate = sb("gate", [P, TILES, 12])
        gtmp2 = sb("logit3", [P, TILES, 12])
        gexp = sb("gexp", [P, TILES, 12])
        gtmp = sb("gtmp", [P, TILES, 12])
        pick = sb("pick", [P, TILES, 12])
        top = sb("top", [P, TILES, 8])
        topi = sb("topi", [P, TILES, 8], U32)
        gsum = sb("gsum", [P, TILES])
        gden = sb("gden", [P, TILES])
        gmax = sb("gmax", [P, TILES])
        mask16 = sb("mask16", [P, TILES, E0], F16)
        before = sb("before", [P, TILES + 1, E0], F16)
        cw0 = sb("cw0", [P, NTILES, E0])
        cw1 = sb("cw1", [P, NTILES, S1])
        cw3 = sb("cw3", [P, NTILES, E3])
        allow, penal, s1a, s1b = (big[:, 1, 2, i * P:(i + 1) * P].rearrange("p (t k) -> p t k", k=KEYS)
                                  for i in range(4))
        qsum = sb("qsum", [P, 2])
        qs = sb("qs", [P, 4, 2])
        wq = mw

        pb = [stack.enter_context(nc.psum_tensor(f"pb{i}", [P, 512], F32)) for i in range(8)]

        hl_f = [hl[:, j, 0:2, :].bitcast(F32).rearrange("p a b -> p (a b)").rearrange("p (c t) -> p c t", t=P)
                for j in range(2)]

        ld = sems("ld", "x", "att", "small", "const", "mlp", "m1", "m2", "bd", "stored")
        ld_w = [sem(f"ld_w{i}") for i in range(2)]
        w = sems("w", "raw_used")
        pre = sems("pre", "kT_mm", "kT", "v_mm", "v", "const", "kbd", "vbd", "dve", "abs", "abs_mm", "quant")
        shared = ("ln", "xn", "xT_mm", "xT", "q_mm", "q", "scores", "subbed", "exped", "pT_mm", "pT", "av",
                  "dve", "x")
        many = ("dve2", "normed", "oT_mm", "oT", "proj")
        heads_sems = sems("heads", *shared, *many)
        A = {0: heads_sems, 1: sems("single", *shared), 2: heads_sems, 3: heads_sems}
        ROUND0 = {0: 0, 1: 0, 2: BATCHES, 3: 2 * BATCHES}
        common = ("ln", "xn", "xT_mm", "xT", "xh", "xl", "route_mm", "gexp", "dve", "cw", "up", "act", "hh",
                  "split", "down", "x")
        own = {0: ("dve2", "acc", "counted", "count_mm"), 1: ("prod",),
               3: ("counted", "cwT_mm", "cwT", "bias_mm", "bias")}
        F = {l: sems(f"f{l}", *common, *own[l]) for l in (0, 1, 3)}
        M = sems("m", "ln", "xn", "ln2", "xn2", "xT_mm", "xT", "up", "upb", "gelu", "dve", "n", "nT_mm", "nT", "down", "b2", "x")

        block = stack.enter_context(nc.Block())

        XADD = {"a0": (A[0]["x"], 1, 0), "f0": (F[0]["x"], TILES, 0), "a1": (A[1]["x"], 1, 0), "f1": (F[1]["x"], S1, 0),
                "a2": (A[2]["x"], 1, ROUND0[2]), "f2": (M["x"], 1, 0), "a3": (A[3]["x"], 1, ROUND0[3]),
                "f3": (F[3]["x"], E3, 0)}
        ORDER = ["a0", "f0", "a1", "f1", "a2", "f2", "a3", "f3"]

        def stage_wait(eng, stage, b):
            n = ORDER.index(stage)
            if n == 0:
                eng.wait_ge(ld["x"], 16)
            else:
                s, k, done = XADD[ORDER[n - 1]]
                eng.wait_ge(s, (b + 1) * k + done)

        def last_stage_wait(eng, b):
            s, k, done = XADD[ORDER[STAGES - 1]]
            eng.wait_ge(s, (b + 1) * k + done)

        def stage_over(eng, stage):
            n = ORDER.index(stage)
            if n:
                s, k, done = XADD[ORDER[n - 1]]
                eng.wait_ge(s, BATCHES * k + done)

        @block.sync
        def _(sp):
            sp.dma_start(ctxT[:, :, :, :], ctx).then_inc(ld["small"], 16)
            sp.dma_start(col[:, :], cols).then_inc(ld["small"], 16)
            sp.dma_start(kc[:, :], consts).then_inc(ld["const"], 16)
            sp.dma_start(X[:, :, :], x.rearrange("(t p) d -> p t d", p=P)).then_inc(ld["x"], 16)
            sp.dma_start(aw[:, :, :], attw).then_inc(ld["att"], 16)
            sp.dma_start(row[:, :], rows.to_broadcast([P, R_COLS])).then_inc(ld["small"], 16)
            sp.dma_start(wr[:, :], router).then_inc(ld["small"], 16)
            for n in range(PIECES):
                if n >= 2:
                    sp.wait_ge(w["raw_used"], n - 1)
                if n == PIECES_L0:
                    sp.dma_start(mw[:, :, :], mlp_w).then_inc(ld["mlp"], 16)
                    sp.dma_start(m1[:, :, :], mask1.rearrange("(t p) k -> p t k", p=P)).then_inc(ld["m1"], 16)
                    sp.dma_start(m2[:, :, :], mask2).then_inc(ld["m2"], 16)
                    sp.dma_start(bd[:, :], bdown).then_inc(ld["bd"], 16)
                sp.dma_start(raw[n % 2][:, :], moe_w[:, n * PIECE:(n + 1) * PIECE]).then_inc(ld_w[n % 2], 16)
            for b in range(BATCHES):
                last_stage_wait(sp, b)
                sp.dma_start(out[b * SEQ:(b + 1) * SEQ, :].rearrange("(t p) d -> p t d", p=P),
                             X[:, b * TILES:(b + 1) * TILES, :]).then_inc(ld["stored"], 16)
            sp.wait_ge(ld["stored"], 16 * BATCHES)

        @block.gpsimd
        def _(pool):
            nc.gpsimd.memset(ones[:, :], 1.0).then_inc(pre["const"], 1)
            nc.gpsimd.memset(ones16[:, :], 1.0).then_inc(pre["const"], 1)
            nc.gpsimd.memset(onesb[:, :], 1.0).then_inc(pre["const"], 1)
            pool.wait_ge(ld["const"], 16)
            nc.gpsimd.tensor_copy(tri16[:, :], kc[:, K_TRI:K_TRI + P]).then_inc(pre["const"], 1)
            nc.gpsimd.memset(before[:, 0, :], 0.0).then_inc(pre["const"], 1)
            nc.gpsimd.memset(cw1[:, :, E1], 1.0 / (3.0 * WSCALE)).then_inc(pre["const"], 1)
            nc.gpsimd.memset(scale64[:, :], WSCALE).then_inc(pre["const"], 1)
            pool.wait_ge(pre["const"], 7)
            def keys_apart(l):
                pool.wait_ge(pre["kT"], 4)
                for b in range(BATCHES):
                    ins = nc.gpsimd.tensor_tensor(kbd[l][:, b, :, :], bcast(kT[:, l, b, :], 1, HEADS),
                                                  bcast(headm, 2, KEYS), ALU.mult)
                ins.then_inc(pre["kbd"], 1)

            keys_apart(0)
            keys_apart(3)

            def cut(n, at):
                dst = bass.ds((2 * at + n) * PIECE, PIECE)
                factor = scale64[:, :].to_broadcast([P, PIECE])
                pool.wait_ge(ld_w[n], 16 * (at + 1))
                nc.gpsimd.tensor_tensor(scaled[n][:, :], raw[n][:, :], factor, ALU.mult)
                nc.gpsimd.tensor_tensor(WH[:, dst], raw[n][:, :], factor, ALU.mult)
                pool.drain()
                nc.gpsimd.tensor_tensor(WL[:, dst], scaled[n][:, :], WH[:, dst], ALU.subtract)\
                    .then_inc(w["raw_used"], 1)

            with pool.Fori(0, PIECES // 2) as i:
                cut(0, i)
                cut(1, i)
            pool.wait_ge(A[0]["x"], BATCHES)
            keys_apart(2)

        @block.scalar
        def _(act):
            A_ = nc.scalar.activation

            act.wait_ge(ld["small"], 64)
            for n, l in enumerate((0, 1, 2, 3)):
                act.wait_ge(pre["kT_mm"], n + 1)
                A_(kT[:, l, :, :], pb[n % 2][:, 0:P].rearrange("p (b k) -> p b k", k=KEYS), ACT.Identity,
                   bias=col[:, C_BK[l]:C_BK[l] + 1]).then_inc(pre["kT"], 1)

            def att_prep(l, b):
                s, r0 = A[l], ROUND0[l]
                act.wait_ge(s["xT_mm"], (b + r0) + 1)
                A_(xnT[:, :], pb[6][:, :], ACT.Copy).then_inc(s["xT"], 1)
                act.wait_ge(s["q_mm"], (b + r0) + 1)
                A_(qT[:, :], pb[6][:, :], ACT.Identity, bias=col[:, C_BQ[l]:C_BQ[l] + 1]).then_inc(s["q"], 1)

            def heads(l):
                s, r0 = A[l], ROUND0[l]
                scale = 1.0 if l == 0 else float(np.float32(DEPTH ** -0.5))

                def ex(b, t):
                    act.wait_ge(s["subbed"], TILES * (b + r0) + t + 1)
                    A_(prob[t % 2], sub[t % 2].rearrange("p h k -> p (h k)"), ACT.Exp, scale=scale)\
                        .then_inc(s["exped"], 1)

                def copy(b, t):
                    act.wait_ge(s["pT_mm"], TILES * (b + r0) + t + 1)
                    if t >= 2:
                        act.wait_ge(s["av"], TILES * (b + r0) + t - 1)
                    A_(probT[t % 2].rearrange("p c t -> p (c t)"), pb[2 + t % 2][:, :], ACT.Copy)\
                        .then_inc(s["pT"], 1)

                def body(b, more):
                    ex(b, 1)
                    copy(b, 0)
                    ex(b, 2)
                    copy(b, 1)
                    ex(b, 3)
                    if more:
                        att_prep(l, b + 1)
                    copy(b, 2)
                    copy(b, 3)
                    if more:
                        ex(b + 1, 0)
                    act.wait_ge(s["oT_mm"], (b + r0) + 1)
                    A_(oT[:, :], pb[7][:, :], ACT.Copy).then_inc(s["oT"], 1)

                att_prep(l, 0)
                ex(0, 0)
                with act.Fori(0, BATCHES - 1) as b:
                    body(b, True)
                body(BATCHES - 1, False)

            def single():
                s = A[1]

                def body(b, more):
                    act.wait_ge(s["subbed"], b + 1)
                    A_(s1a[:, :, :], s1b[:, :, :], ACT.Exp).then_inc(s["exped"], 1)
                    if more:
                        att_prep(1, b + 1)
                    act.wait_ge(s["pT_mm"], b + 1)
                    A_(p1T[:, :], pb[1][0:KEYS, :], ACT.Copy).then_inc(s["pT"], 1)

                att_prep(1, 0)
                with act.Fori(0, BATCHES - 1) as b:
                    body(b, True)
                body(BATCHES - 1, False)

            def ffn_prep(l, b):
                s = F[l]
                act.wait_ge(s["xT_mm"], b + 1)
                A_(xnT[:, :], pb[6][:, :], ACT.Copy).then_inc(s["xT"], 1)
                A_(xh[:, b, :], pb[6][:, :], ACT.Copy).then_inc(s["xh"], 1)

            def route_exp(l, b, scale):
                s = F[l]
                if l == 1:
                    act.wait_ge(s["route_mm"], b + 1)
                    A_(gexp[:, :, 0:E1], pb[7][:, 0:TILES * E1].rearrange("p (t e) -> p t e", e=E1), ACT.Exp,
                       scale=-1.0).then_inc(s["gexp"], 1)
                else:
                    n = E0 if l == 0 else E3
                    act.wait_ge(s["counted"], b + 1)
                    A_(gexp[:, :, 0:n], gate[:, :, 0:n], ACT.Exp).then_inc(s["gexp"], 1)

            def moe0():
                s = F[0]

                def body(b, more):
                    for c in range(2):
                        act.wait_ge(s["up"], 2 * b + c + 1)
                        A_(big[:, 0, c, :], pb[c][:, :], ACT.Silu, scale=1.0 / WSCALE).then_inc(s["act"], 1)
                    act.wait_ge(s["act"], 2 * b + 2)
                    A_(hh[:, 0, 0:2, :], big[:, 0, 0:2, :], ACT.Copy).then_inc(s["hh"], 1)
                    if more:
                        ffn_prep(0, b + 1)
                        route_exp(0, b + 1, 1.0)

                ffn_prep(0, 0)
                route_exp(0, 0, 1.0)
                with act.Fori(0, BATCHES - 1) as b:
                    body(b, True)
                body(BATCHES - 1, False)

            def moe1():
                s = F[1]

                def one(b, e, j):
                    for c in range(2):
                        act.wait_ge(s["up"], 4 * (S1 * b + e) + c + 1)
                        A_(big[:, j, c, :], pb[c][:, :], ACT.Silu, scale=1.0 / WSCALE).then_inc(s["act"], 1)

                def body(b, more):
                    one(b, 0, 0)
                    for lo, hi in ((0, 2), (2, 4)):
                        with act.Fori(lo, hi) as p:
                            one(b, 2 * p + 1, 1)
                            one(b, 2 * p + 2, 0)
                        if lo == 0 and more:
                            ffn_prep(1, b + 1)
                            route_exp(1, b + 1, -1.0)

                ffn_prep(1, 0)
                route_exp(1, 0, -1.0)
                with act.Fori(0, BATCHES - 1) as b:
                    body(b, True)
                body(BATCHES - 1, False)

            def moe3():
                s = F[3]

                def one(b, e, j):
                    for c in range(4):
                        act.wait_ge(s["up"], 4 * (E3 * b + e) + c + 1)
                        A_(big[:, j, c, :], pb[c][:, :], ACT.Gelu, scale=1.0 / WSCALE,
                           bias=col[:, bass.ds(C_BUP + 4 * e + c, 1)]).then_inc(s["act"], 1)

                def copy_cwT(b):
                    act.wait_ge(s["cwT_mm"], b + 1)
                    A_(cwT[:, :], pb[7][0:E3, :], ACT.Copy).then_inc(s["cwT"], 1)

                def body(b, more):
                    with act.Fori(0, 3) as p:
                        one(b, 2 * p + 1, 1)
                        one(b, 2 * p + 2, 0)
                    if more:
                        ffn_prep(3, b + 1)
                        route_exp(3, b + 1, 1.0)
                    with act.Fori(3, 5) as p:
                        one(b, 2 * p + 1, 1)
                        one(b, 2 * p + 2, 0)
                    if more:
                        copy_cwT(b + 1)
                    one(b, E3 - 1, 1)
                    if more:
                        one(b + 1, 0, 0)

                ffn_prep(3, 0)
                route_exp(3, 0, 1.0)
                copy_cwT(0)
                one(0, 0, 0)
                with act.Fori(0, BATCHES - 1) as b:
                    body(b, True)
                body(BATCHES - 1, False)

            def mlp():
                s = M

                def prep(b):
                    act.wait_ge(s["xT_mm"], b + 1)
                    A_(xnT[:, :], pb[6][:, :], ACT.Identity, scale=col[:, C_G1:C_G1 + 1],
                       bias=col[:, C_B1:C_B1 + 1]).then_inc(s["xT"], 1)

                def body(b, more):
                    for t in range(TILES):
                        act.wait_ge(s["upb"], TILES * b + t + 1)
                        A_(big[:, 1, t, :], big[:, 0, t, :], ACT.Gelu).then_inc(s["gelu"], 1)
                    if more:
                        prep(b + 1)
                    for t in range(TILES):
                        act.wait_ge(s["nT_mm"], TILES * b + t + 1)
                        if t >= 2:
                            act.wait_ge(s["down"], TILES * b + t - 1)
                        for c in range(4):
                            ins = A_(hl_f[t % 2][:, c, :], pb[2 + t % 2][:, c * P:(c + 1) * P], ACT.Identity,
                                     scale=col[:, C_G2 + c:C_G2 + c + 1], bias=col[:, C_B2 + c:C_B2 + c + 1])
                        ins.then_inc(s["nT"], 1)

                prep(0)
                with act.Fori(0, BATCHES - 1) as b:
                    body(b, True)
                body(BATCHES - 1, False)

            for n, stage in enumerate((lambda: heads(0), moe0, single, moe1, lambda: heads(2), mlp,
                                       lambda: heads(3), moe3)):
                if n < STAGES:
                    stage()

        @block.tensor
        def _(pe):
            mm = nc.tensor.matmul

            def pairs(dst, stat, mov, start, stop):
                (sh, sl), (mh, ml) = stat, mov
                mm(dst, sh, mh, start=start, stop=False)
                mm(dst, sl, mh, start=False, stop=False)
                return mm(dst, sh, ml, start=False, stop=stop)

            pe.wait_ge(ld["small"], 64)
            pe.wait_ge(ld["att"], 16)
            for n, l in enumerate((0, 1, 2, 3)):
                if n >= 2:
                    pe.wait_ge(pre["kT"], n - 1)
                mm(pb[n % 2][:, 0:P], aw[:, ATT_AT[l] + K, :], ctxT[:, :, 0, :], start=True, stop=True)\
                    .then_inc(pre["kT_mm"], 1)
            for n, l in enumerate((0, 1, 2, 3)):
                if n >= 2:
                    pe.wait_ge(pre["v"], n - 1)
                for b in range(BATCHES):
                    if l == 1:
                        ins = mm(pb[2 + n % 2][0:KEYS, b * P:(b + 1) * P], ctxT[:, b, 0, :],
                                 aw[:, ATT_AT[l] + V, :], start=True, stop=True)
                    else:
                        ins = mm(pb[2 + n % 2][:, b * P:(b + 1) * P],
                                 ctxT[:, b, :, :].rearrange("p r k -> p (r k)"),
                                 aw[:, ATT_AT[l] + V, :], start=True, stop=True)
                ins.then_inc(pre["v_mm"], 1)

            def transposes(bank, src, s_ready, s_done, b):
                pe.wait_ge(s_ready, b + 1)
                for t in range(TILES):
                    ins = nc.tensor.transpose(pb[bank][:, t * P:(t + 1) * P], src[:, t, :], ident)
                ins.then_inc(s_done, 1)

            def att_prep(l, b):
                s, r0 = A[l], ROUND0[l]
                transposes(6, xn, s["xn"], s["xT_mm"], b + r0)
                pe.wait_ge(s["xT"], (b + r0) + 1)
                mm(pb[6][:, :], aw[:, ATT_AT[l] + Q, :], xnT[:, :], start=True, stop=True).then_inc(s["q_mm"], 1)

            def heads(l):
                s, r0 = A[l], ROUND0[l]

                def scores(b, t, first=None):
                    if t == 0:
                        pe.wait_ge(s["q"], (b + r0) + 1)
                        if first:
                            pe.wait_ge(pre["kbd"], {0: 1, 3: 2, 2: 3}[l])
                    if t >= 2:
                        pe.wait_ge(s["subbed"], TILES * (b + r0) + t - 1)
                    ins = mm(pb[t % 2][:, :], qT[:, t * P:(t + 1) * P],
                             kbd[l][:, b, :, :].rearrange("p h k -> p (h k)"), start=True, stop=l != 2)
                    if l == 2:
                        ins = mm(pb[t % 2][:, :], onesb[:, :], m2b[:, b, :, :].rearrange("p h k -> p (h k)"),
                                 start=False, stop=True)
                    ins.then_inc(s["scores"], 1)

                def turn(b, t):
                    pe.wait_ge(s["exped"], TILES * (b + r0) + t + 1)
                    for c in range(QUADS):
                        ins = nc.tensor.transpose(pb[2 + t % 2][:, c * P:(c + 1) * P],
                                                  prob[t % 2][:, c * P:(c + 1) * P], ident)
                    ins.then_inc(s["pT_mm"], 1)

                def values(b, t):
                    pe.wait_ge(s["pT"], TILES * (b + r0) + t + 1)
                    if t >= 2:
                        pe.wait_ge(s["normed"], TILES * (b + r0) + t - 1)
                    for c in range(QUADS):
                        ins = mm(pb[4 + t % 2][:, c * VCOLS:(c + 1) * VCOLS], probT[t % 2][:, c, :],
                                 vbd[l][:, b, c, :], start=True, stop=True)
                    ins.then_inc(s["av"], 1)

                def body(b, more):
                    turn(b, 0)
                    scores(b, 2)
                    turn(b, 1)
                    values(b, 0)
                    scores(b, 3)
                    turn(b, 2)
                    values(b, 1)
                    if more:
                        att_prep(l, b + 1)
                    turn(b, 3)
                    values(b, 2)
                    if more:
                        scores2(b + 1, 0)
                    values(b, 3)
                    if more:
                        scores2(b + 1, 1)
                    transposes7(b)
                    pe.wait_ge(s["oT"], (b + r0) + 1)
                    for t in range(TILES):
                        dst = pb[7][:, t * P:(t + 1) * P]
                        mm(dst, oT[:, t * P:(t + 1) * P], aw[:, ATT_AT[l] + O, :], start=True, stop=False)
                        ins = mm(dst, ones[0:1, :], row[0:1, R_BO[l]:R_BO[l] + P], start=False, stop=True)
                    ins.then_inc(s["proj"], 1)

                def scores2(b, t):
                    pe.wait_ge(s["subbed"], TILES * (b + r0) + t - 1)
                    scores(b, t)

                def transposes7(b):
                    pe.wait_ge(s["normed"], TILES * (b + r0) + TILES)
                    for t in range(TILES):
                        ins = nc.tensor.transpose(pb[7][:, t * P:(t + 1) * P], o[:, t, :], ident)
                    ins.then_inc(s["oT_mm"], 1)

                if l == 0:
                    pe.wait_ge(pre["vbd"], 1)
                stage_over(pe, f"a{l}")
                att_prep(l, 0)
                scores(0, 0, True)
                scores(0, 1)
                with pe.Fori(0, BATCHES - 1) as b:
                    body(b, True)
                body(BATCHES - 1, False)

            def single():
                s = A[1]

                def body(b, more):
                    pe.wait_ge(s["q"], b + 1)
                    for t in range(TILES):
                        ins = mm(pb[0][:, t * KEYS:(t + 1) * KEYS], qT[:, t * P:(t + 1) * P],
                                 kT[:, 1, b, :], start=True, stop=True)
                    ins.then_inc(s["scores"], 1)
                    if more:
                        att_prep(1, b + 1)
                    pe.wait_ge(s["exped"], b + 1)
                    for t in range(TILES):
                        ins = nc.tensor.transpose(pb[1][0:KEYS, t * P:(t + 1) * P], s1a[:, t, :], ident)
                    ins.then_inc(s["pT_mm"], 1)
                    pe.wait_ge(s["pT"], b + 1)
                    for t in range(TILES):
                        ins = mm(pb[2][:, t * P:(t + 1) * P], p1T[:, t * P:(t + 1) * P], v1[:, b, :],
                                 start=True, stop=True)
                    ins.then_inc(s["av"], 1)

                stage_over(pe, "a1")
                att_prep(1, 0)
                with pe.Fori(0, BATCHES - 1) as b:
                    body(b, True)
                body(BATCHES - 1, False)

            def ffn_prep(l, b):
                s = F[l]
                n, at = ((E0, 0), (E1, E0), None, (E3, E0 + E1))[l]
                transposes(6, xn, s["xn"], s["xT_mm"], b)
                pe.wait_ge(s["xT"], b + 1)
                for t in range(TILES):
                    ins = mm(pb[7][:, t * n:(t + 1) * n], xnT[:, t * P:(t + 1) * P], wr[:, at:at + n],
                             start=True, stop=True)
                ins.then_inc(s["route_mm"], 1)

            def moe0():
                s = F[0]
                gate_w = [(WH[:, W_GATE + c * P:W_GATE + (c + 1) * P], WL[:, W_GATE + c * P:W_GATE + (c + 1) * P])
                          for c in range(2)]

                def count(b):
                    pe.wait_ge(s["cw"], 2 * b + 1)
                    for t in range(TILES):
                        dst = pb[7][:, t * E0:(t + 1) * E0]
                        mm(dst, tri16[:, :], mask16[:, t, :], start=True, stop=False)
                        ins = mm(dst, ones16[:, :], before[:, t, :], start=False, stop=True)
                    ins.then_inc(s["count_mm"], 1)

                def up(b):
                    pe.wait_ge(s["xh"], b + 1)
                    pe.wait_ge(s["xl"], b + 1)
                    for c in range(2):
                        pairs(pb[c][:, :], gate_w[c], (xh[:, b, :], xl[:, b, :]), True, True).then_inc(s["up"], 1)

                def down(b, t):
                    if t == 0:
                        pe.wait_ge(s["hh"], b + 1)
                        pe.wait_ge(s["split"], b + 1)
                    if t >= 2:
                        pe.wait_ge(s["x"], TILES * b + t - 1)
                    for n in range(2):
                        for c in range(2):
                            at = W_DOWN0 + c * E0 * P + n * 512
                            tok = slice(t * P, (t + 1) * P)
                            ins = pairs(pb[2 + 2 * (t % 2) + n][:, :], (hh[:, 0, c, tok], hl[:, 0, c, tok]),
                                        (WH[:, at:at + 512], WL[:, at:at + 512]), c == 0, c == 1)
                    ins.then_inc(s["down"], 1)

                def body(b, more):
                    up(b)
                    if more:
                        ffn_prep(0, b + 1)
                    down(b, 0)
                    down(b, 1)
                    if more:
                        count(b + 1)
                    down(b, 2)
                    down(b, 3)

                stage_over(pe, "f0")
                pe.wait_ge(w["raw_used"], PIECES_L0)
                pe.wait_ge(pre["const"], 6)
                ffn_prep(0, 0)
                count(0)
                with pe.Fori(0, BATCHES - 1) as b:
                    body(b, True)
                body(BATCHES - 1, False)

            def wpair(at, n=P):
                return WH[:, bass.ds(at, n)], WL[:, bass.ds(at, n)]

            def moe1():
                s = F[1]

                def up(b, e, j, guard=True):
                    g = S1 * b + e
                    if guard:
                        pe.wait_ge(s["act"], 2 * g)
                        pe.wait_ge(s["prod"], g)
                    for i, base in enumerate((W_1, W_3)):
                        for c in range(2):
                            pairs(pb[2 * i + c][:, :], wpair(base + e * 256 + c * P),
                                  (xh[:, b, :], xl[:, b, :]), True, True).then_inc(s["up"], 1)

                def down(b, e, j):
                    g = S1 * b + e
                    pe.wait_ge(s["split"], g + 1)
                    for t in range(TILES):
                        tok = slice(t * P, (t + 1) * P)
                        for c in range(2):
                            ins = pairs(pb[4 + j][:, tok], (hh[:, j, c, tok], hl[:, j, c, tok]),
                                        wpair(W_2 + e * 256 + c * P), c == 0, c == 1)
                    ins.then_inc(s["down"], 1)

                def body(b, more):
                    for lo, hi in ((0, 2), (2, 4)):
                        with pe.Fori(lo, hi) as p:
                            up(b, 2 * p + 1, 1)
                            down(b, 2 * p, 0)
                            up(b, 2 * p + 2, 0)
                            down(b, 2 * p + 1, 1)
                        if lo == 0 and more:
                            ffn_prep(1, b + 1)
                    down(b, S1 - 1, 0)
                    if more:
                        pe.wait_ge(s["xh"], b + 2)
                        pe.wait_ge(s["xl"], b + 2)
                        up(b + 1, 0, 0)

                stage_over(pe, "f1")
                pe.wait_ge(w["raw_used"], PIECES_L1)
                ffn_prep(1, 0)
                pe.wait_ge(s["xh"], 1)
                pe.wait_ge(s["xl"], 1)
                up(0, 0, 0, guard=False)
                with pe.Fori(0, BATCHES - 1) as b:
                    body(b, True)
                body(BATCHES - 1, False)

            def moe3():
                s = F[3]

                def up(b, e, j, guard=True):
                    g = E3 * b + e
                    for c in range(4):
                        if guard:
                            pe.wait_ge(s["act"], 4 * g - 3 + c)
                        pairs(pb[c][:, :], wpair(W_UP + e * 512 + c * P),
                              (xh[:, b, :], xl[:, b, :]), True, True).then_inc(s["up"], 1)

                def down(b, e, j):
                    g = E3 * b + e
                    pe.wait_ge(s["split"], g + 1)
                    for t in range(TILES):
                        tok = slice(t * P, (t + 1) * P)
                        for c in range(4):
                            ins = pairs(pb[4 + j][:, tok], (hh[:, j, c, tok], hl[:, j, c, tok]),
                                        wpair(W_DOWN3 + e * 512 + c * P), c == 0, c == 3)
                    ins.then_inc(s["down"], 1)

                def bias(b):
                    pe.wait_ge(s["cw"], b + 1)
                    for t in range(TILES):
                        ins = nc.tensor.transpose(pb[7][0:E3, t * P:(t + 1) * P], gate[:, t, :], ident)
                    ins.then_inc(s["cwT_mm"], 1)
                    pe.wait_ge(s["cwT"], b + 1)
                    pe.wait_ge(pre["quant"], 3)
                    for t in range(TILES):
                        ins = mm(pb[6][:, t * P:(t + 1) * P], cwT[:, t * P:(t + 1) * P], bd[:, :],
                                 start=True, stop=True)
                    ins.then_inc(s["bias_mm"], 1)

                def body(b, more):
                    with pe.Fori(0, 3) as p:
                        up(b, 2 * p + 1, 1)
                        down(b, 2 * p, 0)
                        up(b, 2 * p + 2, 0)
                        down(b, 2 * p + 1, 1)
                    if more:
                        ffn_prep(3, b + 1)
                    with pe.Fori(3, 5) as p:
                        up(b, 2 * p + 1, 1)
                        down(b, 2 * p, 0)
                        up(b, 2 * p + 2, 0)
                        down(b, 2 * p + 1, 1)
                    if more:
                        bias(b + 1)
                    up(b, E3 - 1, 1)
                    down(b, E3 - 2, 0)
                    if more:
                        up(b + 1, 0, 0)
                    down(b, E3 - 1, 1)

                stage_over(pe, "f3")
                pe.wait_ge(w["raw_used"], PIECES)
                ffn_prep(3, 0)
                bias(0)
                pe.wait_ge(s["xh"], 1)
                pe.wait_ge(s["xl"], 1)
                up(0, 0, 0, guard=False)
                with pe.Fori(0, BATCHES - 1) as b:
                    body(b, True)
                body(BATCHES - 1, False)

            def mlp():
                s = M

                def up(b, t):
                    if t == 0:
                        pe.wait_ge(s["xT"], b + 1)
                    if t >= 2:
                        pe.wait_ge(s["upb"], TILES * b + t - 1)
                    mm(pb[t % 2][:, :], xnT[:, t * P:(t + 1) * P], wq[:, 0, :], start=True, stop=True)\
                        .then_inc(s["up"], 1)

                def turn(b, t):
                    pe.wait_ge(s["n"], TILES * b + t + 1)
                    if t >= 2:
                        pe.wait_ge(s["nT"], TILES * b + t - 1)
                    for c in range(4):
                        ins = nc.tensor.transpose(pb[2 + t % 2][:, c * P:(c + 1) * P],
                                                  big[:, 0, t, c * P:(c + 1) * P], ident)
                    ins.then_inc(s["nT_mm"], 1)

                def down(b, t):
                    pe.wait_ge(s["nT"], TILES * b + t + 1)
                    for c in range(4):
                        ins = mm(pb[4][:, t * P:(t + 1) * P], hl_f[t % 2][:, c, :], wq[:, 1, c * P:(c + 1) * P],
                                 start=c == 0, stop=c == 3)
                    ins.then_inc(s["down"], 1)

                def body(b, more):
                    for t in range(TILES):
                        up(b, t)
                    if more:
                        transposes(6, xn, s["xn2"], s["xT_mm"], b + 1)
                    turn(b, 0)
                    turn(b, 1)
                    down(b, 0)
                    turn(b, 2)
                    down(b, 1)
                    turn(b, 3)
                    down(b, 2)
                    down(b, 3)

                pe.wait_ge(pre["quant"], 2)
                stage_over(pe, "f2")
                transposes(6, xn, s["xn2"], s["xT_mm"], 0)
                with pe.Fori(0, BATCHES - 1) as b:
                    body(b, True)
                body(BATCHES - 1, False)

            def abs_totals():
                pe.wait_ge(pre["abs"], 1)
                pe.wait_ge(pre["const"], 6)
                mm(pb[5][:, 0:2], ones[:, :], qsum[:, :], start=True, stop=True).then_inc(pre["abs_mm"], 1)

            for n, stage in enumerate((lambda: heads(0), moe0, single, moe1, lambda: heads(2), mlp,
                                       lambda: heads(3), moe3)):
                if n < STAGES:
                    if n == 1:
                        stage_over(pe, "f0")
                        abs_totals()
                    stage()

        @block.vector
        def _(dve):
            ts_ = nc.vector.tensor_scalar
            tt = nc.vector.tensor_tensor
            stt = nc.vector.scalar_tensor_tensor

            dve.wait_ge(ld["small"], 64)
            dve.wait_ge(ld["const"], 16)
            ch = Chain(dve, pre["dve"], 0, 0)
            for n, l in enumerate((0, 1, 2, 3)):
                dve.wait_ge(pre["v_mm"], n + 1)
                src = pb[2 + n % 2]
                bv = slice(R_BV[l], R_BV[l] + P)
                if l == 1:
                    tt(v1[:, :, :], src[0:KEYS, :].rearrange("p (b d) -> p b d", d=P),
                       bcast(row[0:KEYS, bv], 1, BATCHES), ALU.add).then_inc(pre["v"], 1)
                    continue
                if l:
                    dve.wait_ge(pre["vbd"], l - 1)
                tt(vrep[:, :, :], src[:, :].rearrange("p (b d) -> p b d", d=P), bcast(row[:, bv], 1, BATCHES),
                   ALU.add).then_inc(pre["v"], 1)
                dve.wait_ge(pre["v"], n + 1)
                for b in range(BATCHES):
                    tt(vbd[l][:, b, :, 0:32].rearrange("p c (g d) -> p c g d", d=DEPTH),
                       vrep[:, b, :].rearrange("p (c g d) -> p c g d", g=4, d=DEPTH),
                       bcast(bcast(quadm, 2, DEPTH), 1, QUADS), ALU.mult)
                nc.vector.tensor_copy(vbd[l][:, :, :, 32:36].rearrange("p b c g -> p (b c) g"),
                                      bcast(quadm, 1, BATCHES * QUADS)).then_inc(pre["vbd"], 1)

            def mean_rstd(ch, n):
                me, se, mo, so = (stats[:, :, i] for i in (1, 2, 4, 5))
                tt(tmp4[:, :], me, mo, ALU.subtract)
                tt(var[:, :], se, so, ALU.add)
                ch.then(tt(mean[:, :], me, mo, ALU.add))
                ts_(mean[:, :], mean[:, :], 0.5, None, ALU.mult)
                ch.then(stt(tmp4[:, :], tmp4[:, :], n / 4.0, tmp4[:, :], ALU.mult, ALU.mult))
                ch.then(tt(var[:, :], var[:, :], tmp4[:, :], ALU.add))
                ch.then(ts_(var[:, :], var[:, :], 1.0 / n, EPS, ALU.mult, ALU.add))
                ch.then(ts_(rstd[:, :].bitcast(I32), var[:, :].bitcast(I32), -0.5, MAGIC, ALU.mult, ALU.add))
                for _ in range(3):
                    ch.then(stt(tmp4[:, :], rstd[:, :], -0.5, rstd[:, :], ALU.mult, ALU.mult))
                    ch.then(tt(tmp4[:, :], tmp4[:, :], var[:, :], ALU.mult))
                    ch.then(stt(rstd[:, :], tmp4[:, :], 1.5, rstd[:, :], ALU.add, ALU.mult))

            def normalise(sem_step, sem_done, src, dst, b):
                ch = Chain(dve, sem_step, 15, b)
                for t in range(TILES):
                    ins = nc.vector.bn_stats(stats[:, t, :], src(t))
                ch.then(ins)
                mean_rstd(ch, P)
                ch.done()
                for t in range(TILES):
                    ins = ts_(dst(t), src(t), mean[:, t:t + 1], rstd[:, t:t + 1], ALU.subtract, ALU.mult)
                    if sem_done is None:
                        continue
                if sem_done is not None:
                    ins.then_inc(sem_done, 1)
                return ins

            def prep(stage, s, b, r0=0):
                stage_wait(dve, stage, b)
                normalise(s["ln"], s["xn"], lambda t: X[:, TILES * b + t, :], lambda t: xn[:, t, :], b + r0)

            def heads(l):
                s, r0 = A[l], ROUND0[l]

                def softmax(b, t):
                    dve.wait_ge(s["scores"], TILES * (b + r0) + t + 1)
                    src = pb[t % 2][:, :].rearrange("p (h k) -> p h k", k=KEYS)
                    nc.vector.reduce_max(mx[:, t % 2, :], src, AX).then_inc(s["dve"], 1)
                    dve.wait_ge(s["dve"], TILES * (b + r0) + t + 1)
                    if t >= 2:
                        dve.wait_ge(s["exped"], TILES * (b + r0) + t - 1)
                    tt(sub[t % 2], src, bcast(mx[:, t % 2, :], 2, KEYS), ALU.subtract).then_inc(s["subbed"], 1)

                def softmax2(b, t):
                    softmax(b, t)

                def norm(b, t):
                    dve.wait_ge(s["av"], TILES * (b + r0) + t + 1)
                    src = pb[4 + t % 2][:, 0:QUADS * VCOLS].rearrange("p (c n) -> p c n", n=VCOLS)
                    if t >= 2:
                        dve.wait_ge(s["normed"], TILES * (b + r0) + t)
                    nc.vector.reciprocal(rinv[:, :, :], src[:, :, 32:36]).then_inc(s["dve2"], 1)
                    dve.wait_ge(s["dve2"], TILES * (b + r0) + t + 1)
                    tt(o[:, t, :].rearrange("p (c g d) -> p c g d", g=4, d=DEPTH),
                       src[:, :, 0:32].rearrange("p c (g d) -> p c g d", d=DEPTH),
                       bcast(rinv[:, :, :], 3, DEPTH), ALU.mult).then_inc(s["normed"], 1)

                def body(b, more):
                    softmax(b, 1)
                    softmax(b, 2)
                    norm(b, 0)
                    if more:
                        prep(f"a{l}", s, b + 1, r0)
                    softmax(b, 3)
                    norm(b, 1)
                    norm(b, 2)
                    if more:
                        softmax2(b + 1, 0)
                    norm(b, 3)
                    dve.wait_ge(s["proj"], (b + r0) + 1)
                    tt(X[:, bass.ds(TILES * b, TILES), :], pb[7][:, :].rearrange("p (t d) -> p t d", d=P),
                       X[:, bass.ds(TILES * b, TILES), :], ALU.add).then_inc(s["x"], 1)

                prep(f"a{l}", s, 0, r0)
                softmax(0, 0)
                with dve.Fori(0, BATCHES - 1) as b:
                    body(b, True)
                body(BATCHES - 1, False)

            def single():
                s = A[1]
                isq = float(np.float32(1.0) / np.sqrt(np.float32(P)))

                def body(b, more):
                    ch = Chain(dve, s["dve"], 7, b)
                    ch.then(ts_(allow[:, :, :], m1[:, bass.ds(TILES * b, TILES), :], 0.0, None, ALU.not_equal))
                    ch.then(ts_(penal[:, :, :], allow[:, :, :], 1e10, -1e10, ALU.mult, ALU.add))
                    dve.wait_ge(s["scores"], b + 1)
                    ch.then(stt(s1b[:, :, :], pb[0][:, 0:P].rearrange("p (t k) -> p t k", k=KEYS), isq,
                                allow[:, :, :], ALU.mult, ALU.mult))
                    ch.then(tt(allow[:, :, :], s1b[:, :, :], penal[:, :, :], ALU.add))
                    ch.then(nc.vector.reduce_max(gmax[:, :], allow[:, :, :], AX))
                    tt(s1b[:, :, :], allow[:, :, :], bcast(gmax[:, :], 2, KEYS), ALU.subtract)\
                        .then_inc(s["subbed"], 1)
                    if more:
                        prep("a1", s, b + 1)
                    dve.wait_ge(s["exped"], b + 1)
                    ch.then(nc.vector.reduce_sum(gsum[:, :], s1a[:, :, :], AX))
                    ch.then(nc.vector.reciprocal(gden[:, :], gsum[:, :]))
                    ch.done()
                    dve.wait_ge(s["av"], b + 1)
                    for t in range(TILES):
                        ins = stt(X[:, TILES * b + t, :], pb[2][:, t * P:(t + 1) * P], gden[:, t:t + 1],
                                  X[:, TILES * b + t, :], ALU.mult, ALU.add)
                    ins.then_inc(s["x"], 1)

                prep("a1", s, 0)
                dve.wait_ge(ld["m1"], 16)
                with dve.Fori(0, BATCHES - 1) as b:
                    body(b, True)
                body(BATCHES - 1, False)

            def ffn_prep(l, b):
                s = F[l]
                prep(f"f{l}", s, b)
                dve.wait_ge(s["xT"], b + 1)
                dve.wait_ge(s["xh"], b + 1)
                tt(xl[:, b, :], xnT[:, :], xh[:, b, :], ALU.subtract).then_inc(s["xl"], 1)

            def choose(ch, score, n, k):
                dve.drain()
                for t in range(TILES):
                    nc.vector.max(top[:, t, :], score[:, t, 0:n])
                dve.drain()
                for t in range(TILES):
                    ins = nc.vector.max_index(topi[:, t, :], top[:, t, :], score[:, t, 0:n])
                ch.then(ins)
                it = bcast(iota[:, 0:n], 1, TILES)
                for i in range(k):
                    dst = pick if i == 0 else gtmp
                    ch.then(tt(dst[:, :, 0:n], it, bcast(topi[:, :, i], 2, n), ALU.is_equal))
                    if i:
                        ch.then(tt(pick[:, :, 0:n], pick[:, :, 0:n], gtmp[:, :, 0:n], ALU.add))

            def moe0():
                s = F[0]
                logits = pb[7][:, 0:TILES * E0].rearrange("p (t e) -> p t e", e=E0)
                g, e, pk, tm = (a[:, :, 0:E0] for a in (gate, gexp, pick, gtmp))

                def route_a(b):
                    ch = Chain(dve, s["dve"], 9, b)
                    dve.wait_ge(s["route_mm"], b + 1)
                    ch.then(nc.vector.reduce_max(gmax[:, :], logits, AX))
                    tt(g, logits, bcast(gmax[:, :], 2, E0), ALU.subtract).then_inc(s["counted"], 1)
                    dve.wait_ge(s["gexp"], b + 1)
                    nc.vector.reduce_sum(gsum[:, :], e, AX)
                    choose(ch, gexp, E0, 2)
                    ch.then(nc.vector.tensor_copy(mask16[:, :, :], pk))
                    for t in range(TILES):
                        ins = tt(before[:, t + 1, :], before[:, t, :], mask16[:, t, :], ALU.add)
                        if t < TILES - 1:
                            ch.then(ins)
                    ins.then_inc(s["cw"], 1)
                    ch.done()

                def route_b(b):
                    ch = Chain(dve, s["dve2"], 8, b)
                    dve.wait_ge(s["count_mm"], b + 1)
                    ch.then(ts_(tm, logits, float(CAPACITY), None, ALU.is_le))
                    ch.then(nc.vector.tensor_copy(before[:, 0, :], before[:, TILES, :]))
                    ch.then(tt(pk, pk, tm, ALU.mult))
                    ch.then(tt(g, e, pk, ALU.mult))
                    ch.then(nc.vector.reduce_sum(gmax[:, :], g, AX))
                    ch.then(stt(gden[:, :], gsum[:, :], 1e-6, gmax[:, :], ALU.mult, ALU.add))
                    ch.then(ts_(gsum[:, :], gden[:, :], WSCALE, None, ALU.mult))
                    ch.then(nc.vector.reciprocal(gden[:, :], gsum[:, :]))
                    ch.done()
                    tt(cw0[:, bass.ds(TILES * b, TILES), :], g, bcast(gden[:, :], 2, E0), ALU.mult)\
                        .then_inc(s["cw"], 1)

                def split(b):
                    dve.wait_ge(s["hh"], b + 1)
                    tt(hl[:, 0, 0:2, :], big[:, 0, 0:2, :], hh[:, 0, 0:2, :], ALU.subtract).then_inc(s["split"], 1)

                def add(b, t):
                    dve.wait_ge(s["down"], TILES * b + t + 1)
                    if t == 0:
                        dve.wait_ge(s["cw"], 2 * b + 2)
                    for n in range(E0):
                        at = 2 + 2 * (t % 2) + n // 4
                        ins = stt(X[:, TILES * b + t, :], pb[at][:, (n % 4) * P:(n % 4 + 1) * P],
                                  cw0[:, TILES * b + t, n:n + 1], X[:, TILES * b + t, :], ALU.mult, ALU.add)
                        if n < E0 - 1:
                            ins.then_inc(s["acc"], 1)
                            dve.wait_ge(s["acc"], (E0 - 1) * (TILES * b + t) + n + 1)
                    ins.then_inc(s["x"], 1)

                def body(b, more):
                    split(b)
                    if more:
                        ffn_prep(0, b + 1)
                        route_a(b + 1)
                    add(b, 0)
                    add(b, 1)
                    if more:
                        route_b(b + 1)
                    add(b, 2)
                    add(b, 3)

                dve.wait_ge(pre["const"], 6)
                ffn_prep(0, 0)
                route_a(0)
                route_b(0)
                with dve.Fori(0, BATCHES - 1) as b:
                    body(b, True)
                body(BATCHES - 1, False)

            def moe_add(s, cw, n, b, e, j, close=False):
                g = n * b + e
                dve.wait_ge(s["down"], g + 1)
                if close:
                    dve.wait_ge(s["x"], g)
                for t in range(TILES):
                    ins = stt(X[:, TILES * b + t, :], pb[4 + j][:, t * P:(t + 1) * P],
                              cw[:, TILES * b + t, bass.ds(e, 1)], X[:, TILES * b + t, :], ALU.mult, ALU.add)
                ins.then_inc(s["x"], 1)

            def moe1():
                s = F[1]
                e, pk = gexp[:, :, 0:E1], pick[:, :, 0:E1]

                def route(b):
                    ch = Chain(dve, s["dve"], 9, b)
                    dve.wait_ge(s["gexp"], b + 1)
                    ch.then(ts_(gtmp[:, :, 0:E1], e, 1.0, None, ALU.add))
                    nc.vector.reciprocal(gate[:, :, 0:E1], gtmp[:, :, 0:E1])
                    choose(ch, gate, E1, 2)
                    ch.then(tt(gtmp[:, :, 0:E1], gate[:, :, 0:E1], pk, ALU.mult))
                    ch.then(nc.vector.reduce_sum(gsum[:, :], gtmp[:, :, 0:E1], AX))
                    ch.then(ts_(gmax[:, :], gsum[:, :], 3.0 * WSCALE, None, ALU.mult))
                    ch.then(nc.vector.reciprocal(gden[:, :], gmax[:, :]))
                    ch.done()
                    tt(cw1[:, bass.ds(TILES * b, TILES), 0:E1], gtmp[:, :, 0:E1], bcast(gden[:, :], 2, E1),
                       ALU.mult).then_inc(s["cw"], 1)

                def split(b, e, j):
                    g = S1 * b + e
                    dve.wait_ge(s["act"], 2 * g + 2)
                    for c in range(2):
                        dve.wait_ge(s["up"], 4 * g + 3 + c)
                        ins = stt(big[:, j, c, :], pb[2 + c][:, :], 1.0 / WSCALE, big[:, j, c, :],
                                  ALU.mult, ALU.mult)
                    ins.then_inc(s["prod"], 1)
                    dve.wait_ge(s["prod"], g + 1)
                    nc.vector.tensor_copy(hh[:, j, 0:2, :], big[:, j, 0:2, :]).then_inc(s["hh"], 1)
                    dve.wait_ge(s["hh"], g + 1)
                    tt(hl[:, j, 0:2, :], big[:, j, 0:2, :], hh[:, j, 0:2, :], ALU.subtract).then_inc(s["split"], 1)

                def add(b, e, j, close=False):
                    moe_add(s, cw1, S1, b, e, j, close)

                def body(b, more):
                    dve.wait_ge(s["cw"], b + 1)
                    split(b, 0, 0)
                    for lo, hi in ((0, 2), (2, 4)):
                        with dve.Fori(lo, hi) as p:
                            split(b, 2 * p + 1, 1)
                            add(b, 2 * p, 0)
                            split(b, 2 * p + 2, 0)
                            add(b, 2 * p + 1, 1)
                        if lo == 0 and more:
                            ffn_prep(1, b + 1)
                            route(b + 1)
                    add(b, S1 - 1, 0, True)

                ffn_prep(1, 0)
                route(0)
                with dve.Fori(0, BATCHES - 1) as b:
                    body(b, True)
                body(BATCHES - 1, False)

            def moe3():
                s = F[3]

                def route(b):
                    ch = Chain(dve, s["dve"], 11, b)
                    dve.wait_ge(s["route_mm"], b + 1)
                    nc.vector.tensor_copy(gtmp2[:, :, :], pb[7][:, 0:TILES * E3]
                                          .rearrange("p (t e) -> p t e", e=E3))
                    choose(ch, gtmp2, E3, 3)
                    tt(gate[:, :, :], gtmp2[:, :, :], bcast(top[:, :, 0], 2, E3), ALU.subtract)\
                        .then_inc(s["counted"], 1)
                    dve.wait_ge(s["gexp"], b + 1)
                    ch.then(tt(gtmp[:, :, :], gexp[:, :, :], pick[:, :, :], ALU.mult))
                    ch.then(nc.vector.reduce_sum(gsum[:, :], gtmp[:, :, :], AX))
                    ch.then(ts_(gmax[:, :], gsum[:, :], WSCALE, None, ALU.mult))
                    ch.then(nc.vector.reciprocal(gden[:, :], gmax[:, :]))
                    ch.then(tt(gate[:, :, :], gtmp[:, :, :], bcast(gden[:, :], 2, E3), ALU.mult))
                    ch.done()
                    nc.vector.tensor_copy(cw3[:, bass.ds(TILES * b, TILES), :], gate[:, :, :]).then_inc(s["cw"], 1)

                def begin(b):
                    dve.wait_ge(s["cw"], b + 1)
                    dve.wait_ge(s["bias"], b + 1)
                    split(b, 0, 0)

                def bias(b):
                    dve.wait_ge(s["bias_mm"], b + 1)
                    tt(X[:, bass.ds(TILES * b, TILES), :], pb[6][:, :].rearrange("p (t d) -> p t d", d=P),
                       X[:, bass.ds(TILES * b, TILES), :], ALU.add).then_inc(s["bias"], 1)

                def split(b, e, j):
                    g = E3 * b + e
                    dve.wait_ge(s["act"], 4 * g + 4)
                    nc.vector.tensor_copy(hh[:, j, :, :], big[:, j, :, :]).then_inc(s["hh"], 1)
                    dve.wait_ge(s["hh"], g + 1)
                    tt(hl[:, j, :, :], big[:, j, :, :], hh[:, j, :, :], ALU.subtract).then_inc(s["split"], 1)

                def add(b, e, j, close=False):
                    moe_add(s, cw3, E3, b, e, j, close)

                def body(b, more):
                    with dve.Fori(0, 3) as p:
                        split(b, 2 * p + 1, 1)
                        add(b, 2 * p, 0)
                        split(b, 2 * p + 2, 0)
                        add(b, 2 * p + 1, 1)
                    if more:
                        ffn_prep(3, b + 1)
                        route(b + 1)
                    with dve.Fori(3, 5) as p:
                        split(b, 2 * p + 1, 1)
                        add(b, 2 * p, 0)
                        split(b, 2 * p + 2, 0)
                        add(b, 2 * p + 1, 1)
                    if more:
                        bias(b + 1)
                    split(b, E3 - 1, 1)
                    add(b, E3 - 2, 0)
                    if more:
                        begin(b + 1)
                    add(b, E3 - 1, 1, True)

                ffn_prep(3, 0)
                route(0)
                bias(0)
                begin(0)
                with dve.Fori(0, BATCHES - 1) as b:
                    body(b, True)
                body(BATCHES - 1, False)

            def mlp():
                s = M

                def prep2(b):
                    stage_wait(dve, "f2", b)
                    normalise(s["ln"], s["xn"], lambda t: X[:, TILES * b + t, :], lambda t: xn[:, t, :], b)
                    dve.wait_ge(s["xn"], b + 1)
                    normalise(s["ln2"], s["xn2"], lambda t: xn[:, t, :], lambda t: xn[:, t, :], b)

                def body(b, more):
                    for t in range(TILES):
                        dve.wait_ge(s["up"], TILES * b + t + 1)
                        tt(big[:, 0, t, :], pb[t % 2][:, :], row[:, R_B1:R_B1 + 512], ALU.add)\
                            .then_inc(s["upb"], 1)
                    if more:
                        prep2(b + 1)
                    ch = Chain(dve, s["dve"], 15, b)
                    for t in range(TILES):
                        dve.wait_ge(s["gelu"], TILES * b + t + 1)
                        ins = nc.vector.bn_stats(stats[:, t, :], big[:, 1, t, :])
                    ch.then(ins)
                    mean_rstd(ch, 512)
                    ch.done()
                    for t in range(TILES):
                        ts_(big[:, 0, t, :], big[:, 1, t, :], mean[:, t:t + 1], rstd[:, t:t + 1],
                            ALU.subtract, ALU.mult).then_inc(s["n"], 1)
                    dve.wait_ge(s["down"], TILES * b + TILES)
                    xs = X[:, bass.ds(TILES * b, TILES), :]
                    tt(o[:, :, :], pb[4][:, :].rearrange("p (t d) -> p t d", d=P),
                       bcast(row[:, R_B2:R_B2 + P], 1, TILES), ALU.add).then_inc(s["b2"], 1)
                    dve.wait_ge(s["b2"], b + 1)
                    tt(xs, o[:, :, :], xs, ALU.add).then_inc(s["x"], 1)

                prep2(0)
                with dve.Fori(0, BATCHES - 1) as b:
                    body(b, True)
                body(BATCHES - 1, False)

            def small_preparations():
                ch = Chain(dve, pre["dve"], 0, 0)
                dve.wait_ge(ld["mlp"], 16)
                for i in range(2):
                    ch.then(stt(big[:, 0, i, :], mw[:, i, :], -1.0, mw[:, i, :], ALU.mult, ALU.max))
                ch.then(nc.vector.reduce_sum(qsum[:, :], big[:, 0, 0:2, :], AX))
                nc.vector.tensor_copy(qs[:, 0, :], qsum[:, :]).then_inc(pre["abs"], 1)
                dve.wait_ge(pre["abs_mm"], 1)
                ch.then(ts_(qs[:, 0, :], pb[5][:, 0:2], 1.0 / (512 * P), 1e-5, ALU.mult, ALU.max))
                ch.then(nc.vector.reciprocal(qs[:, 1, :], qs[:, 0, :]))
                ch.then(nc.vector.reciprocal(qs[:, 2, :], qs[:, 1, :]))
                for i in range(2):
                    sc, inv = qs[:, 1, i:i + 1], qs[:, 2, i:i + 1]
                    t0, t1 = big[:, 0, 0, :], big[:, 0, 1, :]
                    ch.then(ts_(t0, mw[:, i, :], sc, 0.5, ALU.mult, ALU.is_gt))
                    ch.then(ts_(t1, mw[:, i, :], sc, -0.5, ALU.mult, ALU.is_lt))
                    ch.then(tt(t0, t0, t1, ALU.subtract))
                    ch.then(stt(t1, t0, inv, mw[:, i, :], ALU.mult, ALU.subtract))
                    tt(wq[:, i, :], mw[:, i, :], t1, ALU.add).then_inc(pre["quant"], 1)
                    dve.wait_ge(pre["quant"], i + 1)
                dve.wait_ge(ld["bd"], 16)
                ts_(bd[:, :], bd[:, :], WSCALE, None, ALU.mult).then_inc(pre["quant"], 1)
                dve.wait_ge(ld["m2"], 16)
                for b in range(BATCHES):
                    ins = ts_(m2b[:, b, :, :], bcast(m2[:, b, :], 1, HEADS), -1e30, None, ALU.mult)
                ch.then(ins)

            for n, stage in enumerate((lambda: heads(0), moe0, single, moe1, lambda: heads(2), mlp,
                                       lambda: heads(3), moe3)):
                if n < STAGES:
                    if n == 1:
                        small_preparations()
                    stage()


def layout(i):
    c = np.ascontiguousarray

    def wide(a, chunks):
        return a.reshape(chunks, P, -1).transpose(1, 0, 2).reshape(P, -1)

    ctx = i["ctx_1024"].transpose(2, 0, 1)[:, :, None, :]
    ctx = np.broadcast_to(ctx, (P, BATCHES, QUADS, KEYS))
    kv_w = i["L2_xattn_kv_w"]
    att = [i["L0_xattn_Wq"], i["L0_xattn_Wk"], i["L0_xattn_Wv"], i["L0_xattn_Wo"],
           i["L1_xattn_Wq"].T, i["L1_xattn_Wk"].T, i["L1_xattn_Wv"].T,
           i["L2_xattn_q_w"], kv_w[:, :P], kv_w[:, P:], i["L2_xattn_proj_w"],
           i["L3_xattn_w_q"].T, i["L3_xattn_w_k"].T, i["L3_xattn_w_v"].T, i["L3_xattn_w_o"].T]
    kv_b = i["L2_xattn_kv_b"]
    cols = [i["L0_xattn_bq"][:, None], i["L0_xattn_bk"][:, None], i["L1_xattn_bq"][:, None],
            i["L1_xattn_bk"][:, None], i["L2_xattn_q_b"][:, None], kv_b[:P, None],
            i["L3_xattn_b_q"][:, None], i["L3_xattn_b_k"][:, None],
            i["L2_ffn_ln1_g"][:, None], i["L2_ffn_ln1_b"][:, None],
            i["L2_ffn_ln2_g"].reshape(4, P).T, i["L2_ffn_ln2_b"].reshape(4, P).T,
            i["L3_ffn_bup"].reshape(4 * E3, P).T]
    rows = [i["L0_xattn_bv"], i["L1_xattn_bv"], kv_b[P:], i["L3_xattn_b_v"], i["L0_xattn_bo"],
            i["L2_xattn_proj_b"], i["L3_xattn_b_o"], i["L2_ffn_b2"], i["L2_ffn_b1"]]
    router = [i["L0_ffn_w_router"].T, i["L1_ffn_Wg"], i["L3_ffn_Wg"]]

    def experts(shared, routed):
        return np.concatenate([routed, shared[None]], 0)

    w1 = experts(i["L1_ffn_Ws1"], i["L1_ffn_We1"]).transpose(1, 0, 2).reshape(P, -1)
    w3 = experts(i["L1_ffn_Ws3"], i["L1_ffn_We3"]).transpose(1, 0, 2).reshape(P, -1)
    w2 = experts(i["L1_ffn_Ws2"], i["L1_ffn_We2"]).reshape(S1, 2, P, P).transpose(2, 0, 1, 3).reshape(P, -1)
    down0 = i["L0_ffn_w_down"].transpose(2, 0, 1).reshape(2, P, E0, P).transpose(1, 0, 2, 3).reshape(P, -1)
    up3 = i["L3_ffn_Wup"].transpose(1, 0, 2).reshape(P, -1)
    down3 = i["L3_ffn_Wdown"].reshape(E3, 4, P, P).transpose(2, 0, 1, 3).reshape(P, -1)
    moe = [i["L0_ffn_w_gate"].T, down0, w1, w3, w2, up3, down3]
    mlp = [i["L2_ffn_w1"].T, wide(i["L2_ffn_w2"].T, 4)]

    consts = np.zeros((P, K_COLS), np.float32)
    p = np.arange(P)
    consts[p, K_ID + p] = 1.0
    consts[:, K_TRI:K_TRI + P] = p[:, None] <= p[None, :]
    consts[:, K_HEAD:K_HEAD + HEADS] = p[:, None] // DEPTH == np.arange(HEADS)[None, :]
    consts[:, K_QUAD:K_QUAD + QUADS] = p[:, None] // KEYS == np.arange(QUADS)[None, :]
    consts[:, K_IOTA:K_IOTA + 12] = np.arange(12)[None, :]
    return {
        "x": c(i["x"].reshape(BATCHES * SEQ, P)),
        "ctx": c(ctx),
        "attw": c(np.concatenate([a.reshape(P, 1, P) for a in att], 1)),
        "cols": c(np.concatenate(cols, 1)),
        "rows": c(np.concatenate(rows)[None, :]),
        "router": c(np.concatenate(router, 1)),
        "moe_w": c(np.concatenate(moe, 1)),
        "mlp_w": c(np.concatenate([a.reshape(P, 1, 512) for a in mlp], 1)),
        "bdown": c(i["L3_ffn_bdown"]),
        "mask1": c(i["mask_BxSxS2_ik1"].reshape(BATCHES * SEQ, KEYS)),
        "mask2": c(i["mask_BxS2_bk0"].reshape(1, BATCHES, KEYS)),
        "consts": consts,
    }


def kernel(**inputs):
    import concourse.bacc as bacc
    from concourse.bass_utils import run_bass_kernel_spmd as run

    nc = bacc.Bacc("TRN2", target_bir_lowering=False, num_devices=1)
    arrays = layout({k: np.asarray(v) for k, v in inputs.items()})
    args = [nc.dram_tensor(n, a.shape, mybir.dt.from_np(a.dtype), kind="ExternalInput").ap()
            for n, a in arrays.items()]
    out = nc.dram_tensor("out", (BATCHES * SEQ, P), F32, kind="ExternalOutput").ap()
    build(nc, *args, out)
    r = run(nc, [arrays], core_ids=[0])
    return r.results[0]["out"].reshape(BATCHES, SEQ, P)
```

```python
import concourse.bass as bass
import numpy as np
from concourse import mybir
from contextlib import ExitStack

F32 = mybir.dt.float32
F16 = mybir.dt.float16
BF16 = mybir.dt.bfloat16
I32 = mybir.dt.int32
U32 = mybir.dt.uint32
U8 = mybir.dt.uint8
ALU = mybir.AluOpType
ACT = mybir.ActivationFunctionType
AX = mybir.AxisListType.X

P = 128
BATCHES, SEQ, KEYS = 4, 512, 32
TILES = SEQ // P
NTILES = BATCHES * TILES
HEADS, DEPTH = 16, 8
QUADS = 4
VCOLS = 36
E0, E1, E3 = 8, 8, 12
S1 = E1 + 1
AT_LAST = 2
BANK_LAST = 7
CAPACITY = -(-BATCHES * SEQ * 5 // (E0 * 4))
WSCALE = 64.0
EPS = 1e-5
MAGIC = float(0x5F3759DF)

W_GATE = 0
W_DOWN0 = W_GATE + 256
W_1 = W_DOWN0 + 2 * E0 * P
W_3 = W_1 + S1 * 256
W_2 = W_3 + S1 * 256
W_UP = W_2 + S1 * 256
W_DOWN3 = W_UP + E3 * 512
W_COLS = W_DOWN3 + E3 * 512
PIECE = 384
PIECES = W_COLS // PIECE
PIECES_L0 = -(-W_1 // PIECE)
PIECES_L1 = -(-W_UP // PIECE)

Q, K, V, O = 0, 1, 2, 3
ATT_AT = {0: 0, 1: 4, 2: 7, 3: 11}
C_BQ = {0: 0, 1: 2, 2: 4, 3: 6}
C_BK = {0: 1, 1: 3, 2: 5, 3: 7}
C_G1, C_B1, C_G2, C_B2, C_BUP = 8, 9, 10, 14, 18
C_COLS = C_BUP + 4 * E3
R_BV = {0: 0, 1: 128, 2: 256, 3: 384}
R_COLS = 512
B_O = {0: 0, 2: 128, 3: 256}
B_2, B_1 = 384, 512
B_COLS = 1024
K_ID, K_TRI, K_HEAD, K_QUAD, K_IOTA = 0, 128, 256, 272, 276
K_COLS = K_IOTA + 12
STAGES = 8
LN_COUNT = 16


class Chain:

    def __init__(self, eng, sem, per, rnd):
        self.eng, self.sem, self.per, self.rnd, self.at = eng, sem, per, rnd, 0

    def then(self, ins, between=None):
        self.at += 1
        ins.then_inc(self.sem, 1)
        if between:
            between()
        self.eng.wait_ge(self.sem, self.rnd * self.per + self.at)

    def done(self):
        assert self.at == self.per, (self.at, self.per)


def bcast(ap, axis, count):
    shape = list(ap.shape)
    shape.insert(axis, count)
    return ap.unsqueeze(axis).to_broadcast(shape)


def build(nc, x, ctx, attw, cols, rows, biases, router, moe_w, mlp_w, bdown, mask1, mask2, consts, out):
    stack = ExitStack()
    with stack:
        def sb(name, shape, dt=F32):
            return stack.enter_context(nc.sbuf_tensor(name, shape, dt))

        def sem(name):
            return stack.enter_context(nc.semaphore(name))

        def sems(prefix, *names):
            return {n: sem(f"{prefix}_{n}") for n in names}

        X = sb("X", [P, NTILES, P])
        ctxT = sb("ctxT", [P, BATCHES, QUADS, KEYS])
        aw = sb("aw", [P, 15, P])
        col = sb("col", [P, C_COLS])
        row = sb("row", [P, R_COLS])
        bias16 = sb("bias16", [1, 2, B_COLS], F16)
        wr = sb("wr", [P, E0 + E1 + E3])
        raw = [sb(f"raw{i}", [P, PIECE]) for i in range(2)]
        scaled = [sb(f"scaled{i}", [P, PIECE]) for i in range(2)]
        scale64 = sb("scale64", [P, 1])
        WH = sb("WH", [P, W_COLS], F16)
        WL = sb("WL", [P, W_COLS], F16)
        mw = sb("mw", [P, 2, 512])
        bd = sb("bd", [E3, P])
        m1 = sb("m1", [P, NTILES, KEYS], I32)
        m2 = sb("m2", [1, BATCHES, KEYS], U8)
        kc = sb("kc", [P, K_COLS])
        ident = kc[:, K_ID:K_ID + P]
        headm = kc[:, K_HEAD:K_HEAD + HEADS]
        quadm = kc[:, K_QUAD:K_QUAD + QUADS]
        iota = kc[:, K_IOTA:K_IOTA + 12]
        tri16 = sb("tri16", [P, P], F16)
        ones16 = sb("ones16", [P, P], F16)
        ones = sb("ones", [P, P])
        onesb = sb("onesb", [1, P], BF16)
        m2b = sb("m2b", [1, BATCHES, HEADS, KEYS], BF16)
        kT = sb("kT", [P, 4, BATCHES, KEYS])
        kbd02 = sb("kbd02", [P, BATCHES, HEADS, KEYS])
        kbd = {0: kbd02, 2: kbd02, 3: sb("kbd3", [P, BATCHES, HEADS, KEYS])}
        vbd = {l: sb(f"vbd{l}", [P, BATCHES, QUADS, VCOLS]) for l in (0, 2, 3)}
        v1 = sb("v1", [KEYS, BATCHES, P])
        xn = sb("xn", [P, TILES, P])
        xnT = sb("xnT", [P, SEQ])
        xh = sb("xh", [P, BATCHES, SEQ], F16)
        xl = sb("xl", [P, BATCHES, SEQ], F16)
        qT = sb("qT", [P, SEQ])
        big = sb("big", [P, 2, 4, SEQ])
        sub = [big[:, 0, j, :].rearrange("p (h k) -> p h k", k=KEYS) for j in range(2)]
        prob = [big[:, 0, 2 + j, :] for j in range(2)]
        probT = [big[:, 1, j, :].rearrange("p (c t) -> p c t", t=P) for j in range(2)]
        hh = sb("hh", [P, 2, 4, SEQ], F16)
        hl = sb("hl", [P, 2, 4, SEQ], F16)
        mx = sb("mx", [P, 2, HEADS])
        rinv = sb("rinv", [P, QUADS, 4])
        o = sb("o", [P, TILES, P])
        vrep = o
        oT = sb("oT", [P, SEQ])
        cwT = oT[0:E3, :]
        p1T = oT[0:KEYS, :]
        norm_x, norm_h = ({"stats": sb(f"stats_{i}", [P, TILES, 6]), "mean": sb(f"mean_{i}", [P, TILES]),
                           "var": sb(f"var_{i}", [P, TILES]), "rstd": sb(f"rstd_{i}", [P, TILES]),
                           "tmp": sb(f"tmp_{i}", [P, TILES])} for i in "xh")
        gate = sb("gate", [P, TILES, 12])
        logit3 = sb("logit3", [P, TILES, 12])
        gexp = sb("gexp", [P, TILES, 12])
        gtmp = sb("gtmp", [P, TILES, 12])
        pick = sb("pick", [P, TILES, 12])
        top = sb("top", [P, TILES, 8])
        topi = sb("topi", [P, TILES, 8], U32)
        gsum = sb("gsum", [P, TILES])
        gden = sb("gden", [P, TILES])
        gmax = sb("gmax", [P, TILES])
        mask16 = sb("mask16", [P, TILES, E0], F16)
        before = sb("before", [P, TILES + 1, E0], F16)
        cw = sb("cw", [P, TILES, 12])
        acc = o
        bias32 = big[0:1, 1, 2:4, :].rearrange("p a b -> p (a b)")
        inv1 = mx[:, 0, 0:TILES]
        allow, penal, s1a, s1b = (big[:, 1, 2, i * P:(i + 1) * P].rearrange("p (t k) -> p t k", k=KEYS)
                                  for i in range(4))
        qsum = sb("qsum", [P, 2])
        qs = sb("qs", [P, 4, 2])
        wq = mw

        pb = [stack.enter_context(nc.psum_tensor(f"pb{i}", [P, 512], F32)) for i in range(8)]

        hl_f = [hl[:, j, 0:2, :].bitcast(F32).rearrange("p a b -> p (a b)").rearrange("p (c t) -> p c t", t=P)
                for j in range(2)]

        ld = sems("ld", "x", "att", "small", "const", "mlp", "m1", "m2", "bd", "stored")
        ld_w = [sem(f"ld_w{i}") for i in range(2)]
        w = sems("w", "raw_used")
        pre = sems("pre", "bias", "kT_mm", "kT", "v_mm", "v", "const", "kbd", "vbd", "dve", "abs", "abs_mm", "quant")
        shared = ("ln", "xn", "xT_mm", "xT", "q_mm", "q", "scores", "subbed", "exped", "pT_mm", "pT", "av",
                  "dve", "x")
        many = ("dve2", "normed", "oT_mm", "oT", "proj")
        heads_sems = sems("heads", *shared, *many)
        A = {0: heads_sems, 1: sems("single", *shared), 2: heads_sems, 3: heads_sems}
        ROUND0 = {0: 0, 1: 0, 2: BATCHES, 3: 2 * BATCHES}
        common = ("ln", "xn", "xT_mm", "xT", "xh", "xl", "route_mm", "diff", "gexp", "dve", "cw", "up", "act", "hh",
                  "split", "down", "acc", "x")
        own = {0: ("masks", "count_mm"), 1: ("prod",), 3: ("cwT_mm", "cwT", "bias_mm", "bias")}
        F = {l: sems(f"f{l}", *common, *own[l]) for l in (0, 1, 3)}
        M = sems("m", "ln", "xn", "ln2", "xn2", "xT_mm", "xT", "up", "gelu", "dve", "n", "nT_mm", "nT", "down", "x")

        block = stack.enter_context(nc.Block())

        XADD = {"a0": (A[0]["x"], 1, 0), "f0": (F[0]["x"], 1, 0), "a1": (A[1]["x"], 1, 0), "f1": (F[1]["x"], 1, 0),
                "a2": (A[2]["x"], 1, ROUND0[2]), "f2": (M["x"], 1, 0), "a3": (A[3]["x"], 1, ROUND0[3]),
                "f3": (F[3]["x"], 1, 0)}
        SET = {"a0": (A[0], 0), "f0": (F[0], 0), "a1": (A[1], 0), "f1": (F[1], 0), "a2": (A[2], ROUND0[2]),
               "f2": (M, 0), "a3": (A[3], ROUND0[3]), "f3": (F[3], 0)}
        NEXT = {"a0": "f0", "f0": "a1", "a1": "f1", "f1": "a2", "a2": "f2", "f2": "a3", "a3": "f3", "f3": None}

        def following(stage, b, more):
            return (stage, b + 1) if more else (NEXT[stage], 0)

        ORDER = ["a0", "f0", "a1", "f1", "a2", "f2", "a3", "f3"]

        def stage_wait(eng, stage, b):
            n = ORDER.index(stage)
            if n == 0:
                eng.wait_ge(ld["x"], 16)
            else:
                s, k, done = XADD[ORDER[n - 1]]
                eng.wait_ge(s, (b + 1) * k + done)

        def last_stage_wait(eng, b):
            s, k, done = XADD[ORDER[STAGES - 1]]
            eng.wait_ge(s, (b + 1) * k + done)

        def place(e):
            return (0, AT_LAST) if e == S1 - 1 else (e % 2, 0)

        @block.sync
        def _(sp):
            sp.dma_start(ctxT[:, :, :, :], ctx).then_inc(ld["small"], 16)
            sp.dma_start(col[:, :], cols).then_inc(ld["small"], 16)
            sp.dma_start(kc[:, :], consts).then_inc(ld["const"], 16)
            sp.dma_start(X[:, :, :], x.rearrange("(t p) d -> p t d", p=P)).then_inc(ld["x"], 16)
            sp.dma_start(aw[:, :, :], attw).then_inc(ld["att"], 16)
            sp.dma_start(row[:, :], rows.to_broadcast([P, R_COLS])).then_inc(ld["small"], 16)
            sp.dma_start(wr[:, :], router).then_inc(ld["small"], 16)
            sp.dma_start(bias32, biases).then_inc(ld["small"], 16)
            for n in range(PIECES):
                if n >= 2:
                    sp.wait_ge(w["raw_used"], n - 1)
                if n == PIECES_L0:
                    sp.dma_start(mw[:, :, :], mlp_w).then_inc(ld["mlp"], 16)
                    sp.dma_start(m1[:, :, :], mask1.rearrange("(t p) k -> p t k", p=P)).then_inc(ld["m1"], 16)
                    sp.dma_start(m2[:, :, :], mask2).then_inc(ld["m2"], 16)
                    sp.dma_start(bd[:, :], bdown).then_inc(ld["bd"], 16)
                sp.dma_start(raw[n % 2][:, :], moe_w[:, n * PIECE:(n + 1) * PIECE]).then_inc(ld_w[n % 2], 16)
            for b in range(BATCHES):
                last_stage_wait(sp, b)
                sp.dma_start(out[b * SEQ:(b + 1) * SEQ, :].rearrange("(t p) d -> p t d", p=P),
                             X[:, b * TILES:(b + 1) * TILES, :]).then_inc(ld["stored"], 16)
            sp.wait_ge(ld["stored"], 16 * BATCHES)

        @block.gpsimd
        def _(pool):
            nc.gpsimd.memset(ones[:, :], 1.0).then_inc(pre["const"], 1)
            nc.gpsimd.memset(ones16[:, :], 1.0).then_inc(pre["const"], 1)
            nc.gpsimd.memset(onesb[:, :], 1.0).then_inc(pre["const"], 1)
            pool.wait_ge(ld["const"], 16)
            nc.gpsimd.tensor_copy(tri16[:, :], kc[:, K_TRI:K_TRI + P]).then_inc(pre["const"], 1)
            nc.gpsimd.memset(before[:, 0, :], 0.0).then_inc(pre["const"], 1)
            nc.gpsimd.memset(scale64[:, :], WSCALE).then_inc(pre["const"], 1)
            pool.wait_ge(pre["const"], 6)
            def keys_apart(l):
                pool.wait_ge(pre["kT"], 4)
                for b in range(BATCHES):
                    ins = nc.gpsimd.tensor_tensor(kbd[l][:, b, :, :], bcast(kT[:, l, b, :], 1, HEADS),
                                                  bcast(headm, 2, KEYS), ALU.mult)
                ins.then_inc(pre["kbd"], 1)

            keys_apart(0)
            keys_apart(3)

            def cut(n, at):
                dst = bass.ds((2 * at + n) * PIECE, PIECE)
                factor = scale64[:, :].to_broadcast([P, PIECE])
                pool.wait_ge(ld_w[n], 16 * (at + 1))
                nc.gpsimd.tensor_tensor(scaled[n][:, :], raw[n][:, :], factor, ALU.mult)
                nc.gpsimd.tensor_tensor(WH[:, dst], raw[n][:, :], factor, ALU.mult)
                pool.drain()
                nc.gpsimd.tensor_tensor(WL[:, dst], scaled[n][:, :], WH[:, dst], ALU.subtract)\
                    .then_inc(w["raw_used"], 1)

            with pool.Fori(0, PIECES // 2) as i:
                cut(0, i)
                cut(1, i)
            pool.wait_ge(A[0]["x"], BATCHES)
            keys_apart(2)
            s = F[1]
            with pool.Fori(0, BATCHES) as b:
                for e in range(S1):
                    j, at = place(e)
                    pool.wait_ge(s["hh"], 2 * (S1 * b + e) + 2)
                    nc.gpsimd.tensor_tensor(hl[:, j, at:at + 2, :], big[:, j, at:at + 2, :], hh[:, j, at:at + 2, :],
                                            ALU.subtract).then_inc(s["split"], 1)

        @block.scalar
        def _(act):
            A_ = nc.scalar.activation

            act.wait_ge(ld["small"], 80)
            for n, l in enumerate((0, 1, 2, 3)):
                act.wait_ge(pre["kT_mm"], n + 1)
                A_(kT[:, l, :, :], pb[n % 2][:, 0:P].rearrange("p (b k) -> p b k", k=KEYS), ACT.Identity,
                   bias=col[:, C_BK[l]:C_BK[l] + 1]).then_inc(pre["kT"], 1)

            def turned(stage, b):
                if stage in (None, "f2"):
                    return
                s, r0 = SET[stage]
                act.wait_ge(s["xT_mm"], (b + r0) + 1)
                A_(xnT[:, :], pb[6][:, :], ACT.Copy).then_inc(s["xT"], 1)
                if stage[0] == "f":
                    A_(xh[:, b, :], pb[6][:, :], ACT.Copy).then_inc(s["xh"], 1)

            def query(stage, b):
                if stage is not None and stage[0] == "a":
                    s, r0 = SET[stage]
                    l = int(stage[1])
                    act.wait_ge(s["q_mm"], (b + r0) + 1)
                    A_(qT[:, :], pb[6][:, :], ACT.Identity, bias=col[:, C_BQ[l]:C_BQ[l] + 1]).then_inc(s["q"], 1)

            def heads(l):
                s, r0 = A[l], ROUND0[l]
                scale = 1.0 if l == 0 else float(np.float32(DEPTH ** -0.5))

                def ex(b, t):
                    act.wait_ge(s["subbed"], TILES * (b + r0) + t + 1)
                    A_(prob[t % 2], sub[t % 2].rearrange("p h k -> p (h k)"), ACT.Exp, scale=scale)\
                        .then_inc(s["exped"], 1)

                def copy(b, t):
                    act.wait_ge(s["pT_mm"], TILES * (b + r0) + t + 1)
                    if t >= 2:
                        act.wait_ge(s["av"], TILES * (b + r0) + t - 1)
                    A_(probT[t % 2].rearrange("p c t -> p (c t)"), pb[2 + t % 2][:, :], ACT.Copy)\
                        .then_inc(s["pT"], 1)

                def body(b, left):
                    after = following(f"a{l}", b, left > 0)
                    copy(b, 0)
                    ex(b, 2)
                    copy(b, 1)
                    turned(*after)
                    ex(b, 3)
                    copy(b, 2)
                    query(*after)
                    copy(b, 3)
                    if left:
                        ex(b + 1, 0)
                    act.wait_ge(s["oT_mm"], (b + r0) + 1)
                    A_(oT[:, :], pb[7][:, :], ACT.Copy).then_inc(s["oT"], 1)
                    if left:
                        ex(b + 1, 1)
                    elif l != 2:
                        route_exp(l, 0)

                if l == 0:
                    turned("a0", 0)
                    query("a0", 0)
                ex(0, 0)
                ex(0, 1)
                with act.Fori(0, BATCHES - 2) as b:
                    body(b, 2)
                body(BATCHES - 2, 1)
                body(BATCHES - 1, 0)

            def single():
                s = A[1]

                def body(b, left):
                    after = following("a1", b, left > 0)
                    act.wait_ge(s["subbed"], b + 1)
                    A_(s1a[:, :, :], s1b[:, :, :], ACT.Exp).then_inc(s["exped"], 1)
                    turned(*after)
                    act.wait_ge(s["pT_mm"], b + 1)
                    A_(p1T[:, :], pb[1][0:KEYS, :], ACT.Copy).then_inc(s["pT"], 1)
                    query(*after)
                    if not left:
                        route_exp(1, 0)

                with act.Fori(0, BATCHES - 2) as b:
                    body(b, 2)
                body(BATCHES - 2, 1)
                body(BATCHES - 1, 0)

            def route_exp(l, b):
                s = F[l]
                if l == 1:
                    act.wait_ge(s["route_mm"], b + 1)
                    A_(gexp[:, :, 0:E1], pb[6][:, 0:TILES * E1].rearrange("p (t e) -> p t e", e=E1), ACT.Exp,
                       scale=-1.0).then_inc(s["gexp"], 1)
                else:
                    n = E0 if l == 0 else E3
                    act.wait_ge(s["diff"], b + 1)
                    A_(gexp[:, :, 0:n], gate[:, :, 0:n], ACT.Exp).then_inc(s["gexp"], 1)

            def moe0():
                s = F[0]

                def hidden(b, first=False):
                    for c in range(2):
                        act.wait_ge(s["up"], 2 * b + c + 1)
                        A_(big[:, 0, c, :], pb[c][:, :], ACT.Silu, scale=1.0 / WSCALE).then_inc(s["act"], 1)
                    act.wait_ge(s["act"], 2 * b + 2)
                    if not first:
                        act.wait_ge(s["down"], TILES * b)
                    A_(hh[:, 0, 0:2, :], big[:, 0, 0:2, :], ACT.Copy).then_inc(s["hh"], 1)

                def body(b, more):
                    turned(*following("f0", b, more))
                    query(*following("f0", b, more))
                    if more:
                        route_exp(0, b + 1)
                        hidden(b + 1)

                hidden(0, first=True)
                with act.Fori(0, BATCHES - 1) as b:
                    body(b, True)
                body(BATCHES - 1, False)

            def moe1():
                s = F[1]

                def hidden(b, e, j, at=0):
                    g = S1 * b + e
                    for c in range(2):
                        act.wait_ge(s["up"], 4 * g + 2 * c + 1)
                        A_(big[:, j, at + c, :], pb[c][:, :], ACT.Silu, scale=1.0 / WSCALE).then_inc(s["act"], 1)
                    for c in range(2):
                        act.wait_ge(s["prod"], 2 * g + c + 1)
                        A_(hh[:, j, at + c, :], big[:, j, at + c, :], ACT.Copy).then_inc(s["hh"], 1)

                def pair(b, p, at=0):
                    hidden(b, 2 * p + 1, 1)
                    hidden(b, 2 * p + 2, 0, at)

                def body(b, more):
                    with act.Fori(0, 2) as p:
                        pair(b, p)
                    turned(*following("f1", b, more))
                    pair(b, 2)
                    query(*following("f1", b, more))
                    if more:
                        route_exp(1, b + 1)
                    pair(b, 3, AT_LAST)
                    if more:
                        hidden(b + 1, 0, 0)

                hidden(0, 0, 0)
                with act.Fori(0, BATCHES - 1) as b:
                    body(b, True)
                body(BATCHES - 1, False)

            def moe3():
                s = F[3]

                def hidden(b, e, j):
                    g = E3 * b + e
                    for c in range(4):
                        act.wait_ge(s["up"], 4 * g + c + 1)
                        A_(big[:, j, c, :], pb[c][:, :], ACT.Gelu, scale=1.0 / WSCALE,
                           bias=col[:, bass.ds(C_BUP + 4 * e + c, 1)]).then_inc(s["act"], 1)
                        if c >= 2:
                            act.wait_ge(s["act"], 4 * g + 2 * c - 2)
                            A_(hh[:, j, 2 * c - 4:2 * c - 2, :], big[:, j, 2 * c - 4:2 * c - 2, :], ACT.Copy)\
                                .then_inc(s["hh"], 1)

                def copy_cwT(b):
                    act.wait_ge(s["cwT_mm"], b + 1)
                    A_(cwT[:, :], pb[7][0:E3, :], ACT.Copy).then_inc(s["cwT"], 1)

                def pair(b, p):
                    hidden(b, 2 * p + 1, 1)
                    hidden(b, 2 * p + 2, 0)

                def body(b, more):
                    with act.Fori(0, 2) as p:
                        pair(b, p)
                    if more:
                        turned("f3", b + 1)
                    with act.Fori(2, 4) as p:
                        pair(b, p)
                    if more:
                        route_exp(3, b + 1)
                    pair(b, 4)
                    hidden(b, E3 - 1, 1)
                    if more:
                        copy_cwT(b + 1)
                        hidden(b + 1, 0, 0)

                hidden(0, 0, 0)
                copy_cwT(0)
                with act.Fori(0, BATCHES - 1) as b:
                    body(b, True)
                body(BATCHES - 1, False)

            def mlp():
                s = M

                def prep(b):
                    act.wait_ge(s["xT_mm"], b + 1)
                    A_(xnT[:, :], pb[6][:, :], ACT.Identity, scale=col[:, C_G1:C_G1 + 1],
                       bias=col[:, C_B1:C_B1 + 1]).then_inc(s["xT"], 1)

                def gelu(b, t, first=False):
                    act.wait_ge(s["up"], TILES * b + t + 1)
                    if not first:
                        act.wait_ge(s["n"], TILES * (b - 1) + t + 1)
                    A_(big[:, 1, t, :], pb[t][:, :], ACT.Gelu).then_inc(s["gelu"], 1)

                def affine(b, t):
                    act.wait_ge(s["nT_mm"], TILES * b + t + 1)
                    if t >= 2:
                        act.wait_ge(s["down"], TILES * b + t - 1)
                    for c in range(4):
                        ins = A_(hl_f[t % 2][:, c, :], pb[4 + t % 2][:, c * P:(c + 1) * P], ACT.Identity,
                                 scale=col[:, C_G2 + c:C_G2 + c + 1], bias=col[:, C_B2 + c:C_B2 + c + 1])
                    ins.then_inc(s["nT"], 1)

                def body(b, left):
                    if left == 0:
                        query("a3", 0)
                    if left:
                        for t in range(TILES):
                            gelu(b + 1, t)
                    for t in range(TILES):
                        affine(b, t)
                    if left > 1:
                        prep(b + 2)
                    elif left:
                        turned("a3", 0)

                prep(0)
                for t in range(TILES):
                    gelu(0, t, first=True)
                prep(1)
                with act.Fori(0, BATCHES - 2) as b:
                    body(b, 2)
                body(BATCHES - 2, 1)
                body(BATCHES - 1, 0)

            for n, stage in enumerate((lambda: heads(0), moe0, single, moe1, lambda: heads(2), mlp,
                                       lambda: heads(3), moe3)):
                if n < STAGES:
                    stage()

        @block.tensor
        def _(pe):
            mm = nc.tensor.matmul

            def pairs(dst, stat, mov, start, stop):
                (sh, sl), (mh, ml) = stat, mov
                mm(dst, sh, mh, start=start, stop=False)
                mm(dst, sl, mh, start=False, stop=False)
                return mm(dst, sh, ml, start=False, stop=stop)

            pe.wait_ge(ld["small"], 80)
            pe.wait_ge(ld["att"], 16)
            for n, l in enumerate((0, 1, 2, 3)):
                if n >= 2:
                    pe.wait_ge(pre["kT"], n - 1)
                mm(pb[n % 2][:, 0:P], aw[:, ATT_AT[l] + K, :], ctxT[:, :, 0, :], start=True, stop=True)\
                    .then_inc(pre["kT_mm"], 1)
            for n, l in enumerate((0, 1, 2, 3)):
                if n >= 2:
                    pe.wait_ge(pre["v"], n - 1)
                for b in range(BATCHES):
                    if l == 1:
                        ins = mm(pb[2 + n % 2][0:KEYS, b * P:(b + 1) * P], ctxT[:, b, 0, :],
                                 aw[:, ATT_AT[l] + V, :], start=True, stop=True)
                    else:
                        ins = mm(pb[2 + n % 2][:, b * P:(b + 1) * P],
                                 ctxT[:, b, :, :].rearrange("p r k -> p (r k)"),
                                 aw[:, ATT_AT[l] + V, :], start=True, stop=True)
                ins.then_inc(pre["v_mm"], 1)

            def transposes(bank, src, s_ready, s_done, b):
                pe.wait_ge(s_ready, b + 1)
                for t in range(TILES):
                    ins = nc.tensor.transpose(pb[bank][:, t * P:(t + 1) * P], src[:, t, :], ident)
                ins.then_inc(s_done, 1)

            def turn_normal(stage, b):
                if stage in (None, "f2"):
                    return
                s, r0 = SET[stage]
                transposes(6, xn, s["xn"], s["xT_mm"], b + r0)

            def first_product(stage, b):
                if stage in (None, "f2"):
                    return
                s, r0 = SET[stage]
                l = int(stage[1])
                pe.wait_ge(s["xT"], (b + r0) + 1)
                if stage[0] == "a":
                    mm(pb[6][:, :], aw[:, ATT_AT[l] + Q, :], xnT[:, :], start=True, stop=True).then_inc(s["q_mm"], 1)
                    return
                n, at = ((E0, 0), (E1, E0), None, (E3, E0 + E1))[l]
                pe.wait_ge(s["xh"], b + 1)
                for t in range(TILES):
                    ins = mm(pb[6][:, t * n:(t + 1) * n], xnT[:, t * P:(t + 1) * P], wr[:, at:at + n],
                             start=True, stop=True)
                ins.then_inc(s["route_mm"], 1)

            def heads(l):
                s, r0 = A[l], ROUND0[l]

                def scores(b, t, first=None):
                    if t == 0:
                        pe.wait_ge(s["q"], (b + r0) + 1)
                        if first:
                            pe.wait_ge(pre["kbd"], {0: 1, 3: 2, 2: 3}[l])
                    if t >= 2:
                        pe.wait_ge(s["subbed"], TILES * (b + r0) + t - 1)
                    ins = mm(pb[t % 2][:, :], qT[:, t * P:(t + 1) * P],
                             kbd[l][:, b, :, :].rearrange("p h k -> p (h k)"), start=True, stop=l != 2)
                    if l == 2:
                        ins = mm(pb[t % 2][:, :], onesb[:, :], m2b[:, b, :, :].rearrange("p h k -> p (h k)"),
                                 start=False, stop=True)
                    ins.then_inc(s["scores"], 1)

                def turn(b, t):
                    pe.wait_ge(s["exped"], TILES * (b + r0) + t + 1)
                    for c in range(QUADS):
                        ins = nc.tensor.transpose(pb[2 + t % 2][:, c * P:(c + 1) * P],
                                                  prob[t % 2][:, c * P:(c + 1) * P], ident)
                    ins.then_inc(s["pT_mm"], 1)

                def values(b, t):
                    pe.wait_ge(s["pT"], TILES * (b + r0) + t + 1)
                    if t >= 2:
                        pe.wait_ge(s["normed"], TILES * (b + r0) + t - 1)
                    for c in range(QUADS):
                        ins = mm(pb[4 + t % 2][:, c * VCOLS:(c + 1) * VCOLS], probT[t % 2][:, c, :],
                                 vbd[l][:, b, c, :], start=True, stop=True)
                    ins.then_inc(s["av"], 1)

                def project(b):
                    for i in range(2):
                        mm(pb[7][:, :], ones16[0:1, :], bcast(bias16[0:1, i, B_O[l]:B_O[l] + P], 1, TILES),
                           start=i == 0, stop=False)
                    for t in range(TILES):
                        ins = mm(pb[7][:, t * P:(t + 1) * P], oT[:, t * P:(t + 1) * P], aw[:, ATT_AT[l] + O, :],
                                 start=False, stop=t == TILES - 1)
                    ins.then_inc(s["proj"], 1)

                def turn_values(b):
                    pe.wait_ge(s["normed"], TILES * (b + r0) + TILES)
                    for t in range(TILES):
                        ins = nc.tensor.transpose(pb[7][:, t * P:(t + 1) * P], o[:, t, :], ident)
                    ins.then_inc(s["oT_mm"], 1)

                def scores_next(b, t):
                    pe.wait_ge(s["subbed"], TILES * (b + r0) + t - 1)
                    scores(b, t)

                def body(b, left):
                    after = following(f"a{l}", b, left > 0)
                    turn(b, 0)
                    scores(b, 2)
                    turn(b, 1)
                    values(b, 0)
                    turn_normal(*after)
                    scores(b, 3)
                    turn(b, 2)
                    values(b, 1)
                    first_product(*after)
                    turn(b, 3)
                    values(b, 2)
                    if left:
                        scores_next(b + 1, 0)
                    values(b, 3)
                    if left:
                        scores_next(b + 1, 1)
                    turn_values(b)
                    pe.wait_ge(s["oT"], (b + r0) + 1)
                    project(b)

                if l == 0:
                    pe.wait_ge(pre["vbd"], 1)
                    pe.wait_ge(pre["bias"], 2)
                    pe.wait_ge(pre["const"], 6)
                if l == 0:
                    turn_normal("a0", 0)
                    first_product("a0", 0)
                scores(0, 0, True)
                scores(0, 1)
                with pe.Fori(0, BATCHES - 2) as b:
                    body(b, 2)
                body(BATCHES - 2, 1)
                body(BATCHES - 1, 0)

            def single():
                s = A[1]

                def body(b, more):
                    pe.wait_ge(s["q"], b + 1)
                    for t in range(TILES):
                        ins = mm(pb[0][:, t * KEYS:(t + 1) * KEYS], qT[:, t * P:(t + 1) * P],
                                 kT[:, 1, b, :], start=True, stop=True)
                    ins.then_inc(s["scores"], 1)
                    turn_normal(*following("a1", b, more))
                    pe.wait_ge(s["exped"], b + 1)
                    for t in range(TILES):
                        ins = nc.tensor.transpose(pb[1][0:KEYS, t * P:(t + 1) * P], s1a[:, t, :], ident)
                    ins.then_inc(s["pT_mm"], 1)
                    first_product(*following("a1", b, more))
                    pe.wait_ge(s["pT"], b + 1)
                    for t in range(TILES):
                        ins = mm(pb[4][:, t * P:(t + 1) * P], p1T[:, t * P:(t + 1) * P], v1[:, b, :],
                                 start=True, stop=True)
                    ins.then_inc(s["av"], 1)

                with pe.Fori(0, BATCHES - 1) as b:
                    body(b, True)
                body(BATCHES - 1, False)

            def moe0():
                s = F[0]
                gate_w = [(WH[:, W_GATE + c * P:W_GATE + (c + 1) * P], WL[:, W_GATE + c * P:W_GATE + (c + 1) * P])
                          for c in range(2)]

                def count(b):
                    pe.wait_ge(s["masks"], b + 1)
                    for t in range(TILES):
                        dst = pb[7][:, t * E0:(t + 1) * E0]
                        mm(dst, tri16[:, :], mask16[:, t, :], start=True, stop=False)
                        ins = mm(dst, ones16[:, :], before[:, t, :], start=False, stop=True)
                    ins.then_inc(s["count_mm"], 1)

                def up(b):
                    pe.wait_ge(s["xl"], b + 1)
                    for c in range(2):
                        pairs(pb[c][:, :], gate_w[c], (xh[:, b, :], xl[:, b, :]), True, True).then_inc(s["up"], 1)

                def down(b, t):
                    if t == 0:
                        pe.wait_ge(s["split"], b + 1)
                    if t >= 2:
                        pe.wait_ge(s["acc"], E0 * (TILES * b + t - 1))
                    for n in range(2):
                        for c in range(2):
                            at = W_DOWN0 + c * E0 * P + n * 512
                            tok = slice(t * P, (t + 1) * P)
                            ins = pairs(pb[2 + 2 * (t % 2) + n][:, :], (hh[:, 0, c, tok], hl[:, 0, c, tok]),
                                        (WH[:, at:at + 512], WL[:, at:at + 512]), c == 0, c == 1)
                    ins.then_inc(s["down"], 1)

                def body(b, more):
                    down(b, 0)
                    down(b, 1)
                    turn_normal(*following("f0", b, more))
                    down(b, 2)
                    first_product(*following("f0", b, more))
                    if more:
                        up(b + 1)
                    down(b, 3)
                    if more:
                        count(b + 1)

                pe.wait_ge(w["raw_used"], PIECES_L0)
                up(0)
                pe.wait_ge(A[0]["x"], BATCHES)
                count(0)
                abs_totals()
                with pe.Fori(0, BATCHES - 1) as b:
                    body(b, True)
                body(BATCHES - 1, False)

            def wpair(at, n=P):
                return WH[:, bass.ds(at, n)], WL[:, bass.ds(at, n)]

            def moe1():
                s = F[1]

                def up(b, e, guard=True):
                    g = S1 * b + e
                    for c in range(2):
                        for i, base in enumerate((W_1, W_3)):
                            if guard and i:
                                pe.wait_ge(s["prod"], 2 * g + c - 1)
                            elif guard:
                                pe.wait_ge(s["act"], 2 * g + c - 1)
                            pairs(pb[2 * i + c][:, :], wpair(base + e * 256 + c * P),
                                  (xh[:, b, :], xl[:, b, :]), True, True).then_inc(s["up"], 1)

                def down(b, e, j, at=0, bank=None):
                    bank = 4 + j if bank is None else bank
                    pe.wait_ge(s["split"], S1 * b + e + 1)
                    for t in range(TILES):
                        tok = slice(t * P, (t + 1) * P)
                        for c in range(2):
                            ins = pairs(pb[bank][:, tok], (hh[:, j, at + c, tok], hl[:, j, at + c, tok]),
                                        wpair(W_2 + e * 256 + c * P), c == 0, c == 1)
                    ins.then_inc(s["down"], 1)

                def pair(b, p):
                    up(b, 2 * p + 1)
                    down(b, 2 * p, 0)
                    up(b, 2 * p + 2)
                    down(b, 2 * p + 1, 1)

                def body(b, more):
                    with pe.Fori(0, 2) as p:
                        pair(b, p)
                    turn_normal(*following("f1", b, more))
                    pair(b, 2)
                    first_product(*following("f1", b, more))
                    pair(b, 3)
                    if more:
                        pe.wait_ge(s["xl"], b + 2)
                        up(b + 1, 0)
                    down(b, S1 - 1, 0, AT_LAST, BANK_LAST)

                pe.wait_ge(w["raw_used"], PIECES_L1)
                pe.wait_ge(s["xl"], 1)
                up(0, 0, guard=False)
                with pe.Fori(0, BATCHES - 1) as b:
                    body(b, True)
                body(BATCHES - 1, False)

            def moe3():
                s = F[3]

                def up(b, e, guard=True):
                    g = E3 * b + e
                    for c in range(4):
                        if guard:
                            pe.wait_ge(s["act"], 4 * g - 3 + c)
                        pairs(pb[c][:, :], wpair(W_UP + e * 512 + c * P),
                              (xh[:, b, :], xl[:, b, :]), True, True).then_inc(s["up"], 1)

                def down(b, e, j):
                    pe.wait_ge(s["split"], E3 * b + e + 1)
                    for t in range(TILES):
                        tok = slice(t * P, (t + 1) * P)
                        for c in range(4):
                            ins = pairs(pb[4 + j][:, tok], (hh[:, j, c, tok], hl[:, j, c, tok]),
                                        wpair(W_DOWN3 + e * 512 + c * P), c == 0, c == 3)
                    ins.then_inc(s["down"], 1)

                def turn_weights(b):
                    pe.wait_ge(s["cw"], b + 1)
                    for t in range(TILES):
                        ins = nc.tensor.transpose(pb[7][0:E3, t * P:(t + 1) * P], gate[:, t, :], ident)
                    ins.then_inc(s["cwT_mm"], 1)

                def bias(b):
                    pe.wait_ge(s["cwT"], b + 1)
                    for t in range(TILES):
                        ins = mm(pb[6][:, t * P:(t + 1) * P], cwT[:, t * P:(t + 1) * P], bd[:, :],
                                 start=True, stop=True)
                    ins.then_inc(s["bias_mm"], 1)

                def pair(b, p):
                    up(b, 2 * p + 1)
                    down(b, 2 * p, 0)
                    up(b, 2 * p + 2)
                    down(b, 2 * p + 1, 1)

                def body(b, more):
                    with pe.Fori(0, 2) as p:
                        pair(b, p)
                    if more:
                        turn_normal("f3", b + 1)
                    pair(b, 2)
                    if more:
                        first_product("f3", b + 1)
                    with pe.Fori(3, 5) as p:
                        pair(b, p)
                    up(b, E3 - 1)
                    if more:
                        turn_weights(b + 1)
                    down(b, E3 - 2, 0)
                    if more:
                        bias(b + 1)
                        up(b + 1, 0)
                    down(b, E3 - 1, 1)

                pe.wait_ge(w["raw_used"], PIECES)
                pe.wait_ge(pre["quant"], 3)
                pe.wait_ge(s["xl"], 1)
                up(0, 0, guard=False)
                pe.wait_ge(A[3]["x"], BATCHES + ROUND0[3])
                turn_weights(0)
                bias(0)
                with pe.Fori(0, BATCHES - 1) as b:
                    body(b, True)
                body(BATCHES - 1, False)

            def mlp():
                s = M

                def up(b, t):
                    if t == 0:
                        pe.wait_ge(s["xT"], b + 1)
                    for i in range(2):
                        mm(pb[t][:, :], ones16[0:1, :], bias16[0:1, i, B_1:B_1 + 512], start=i == 0, stop=False)
                    mm(pb[t][:, :], xnT[:, t * P:(t + 1) * P], wq[:, 0, :], start=False, stop=True)\
                        .then_inc(s["up"], 1)

                def turn(b, t):
                    pe.wait_ge(s["n"], TILES * b + t + 1)
                    if t >= 2:
                        pe.wait_ge(s["nT"], TILES * b + t - 1)
                    for c in range(4):
                        ins = nc.tensor.transpose(pb[4 + t % 2][:, c * P:(c + 1) * P],
                                                  big[:, 0, t, c * P:(c + 1) * P], ident)
                    ins.then_inc(s["nT_mm"], 1)

                def down(b, t):
                    dst = pb[7][:, t * P:(t + 1) * P]
                    for i in range(2):
                        mm(dst, ones16[0:1, :], bias16[0:1, i, B_2:B_2 + P], start=i == 0, stop=False)
                    pe.wait_ge(s["nT"], TILES * b + t + 1)
                    for c in range(4):
                        ins = mm(dst, hl_f[t % 2][:, c, :], wq[:, 1, c * P:(c + 1) * P],
                                 start=False, stop=c == 3)
                    ins.then_inc(s["down"], 1)

                def body(b, left):
                    if left == 0:
                        first_product("a3", 0)
                    if left:
                        for t in range(TILES):
                            up(b + 1, t)
                    for t in range(TILES):
                        turn(b, t)
                        if t:
                            down(b, t - 1)
                    down(b, TILES - 1)
                    if left > 1:
                        transposes(6, xn, s["xn2"], s["xT_mm"], b + 2)
                    elif left:
                        turn_normal("a3", 0)

                pe.wait_ge(pre["quant"], 2)
                transposes(6, xn, s["xn2"], s["xT_mm"], 0)
                for t in range(TILES):
                    up(0, t)
                transposes(6, xn, s["xn2"], s["xT_mm"], 1)
                with pe.Fori(0, BATCHES - 2) as b:
                    body(b, 2)
                body(BATCHES - 2, 1)
                body(BATCHES - 1, 0)

            def abs_totals():
                pe.wait_ge(pre["abs"], 1)
                pe.wait_ge(pre["const"], 6)
                mm(pb[7][:, 64:66], ones[:, :], qsum[:, :], start=True, stop=True).then_inc(pre["abs_mm"], 1)

            for n, stage in enumerate((lambda: heads(0), moe0, single, moe1, lambda: heads(2), mlp,
                                       lambda: heads(3), moe3)):
                if n < STAGES:
                    stage()

        @block.vector
        def _(dve):
            ts_ = nc.vector.tensor_scalar
            tt = nc.vector.tensor_tensor
            stt = nc.vector.scalar_tensor_tensor

            dve.wait_ge(ld["small"], 80)
            dve.wait_ge(ld["const"], 16)
            ch = Chain(dve, pre["dve"], 0, 0)
            for n, l in enumerate((0, 1, 2, 3)):
                dve.wait_ge(pre["v_mm"], n + 1)
                src = pb[2 + n % 2]
                bv = slice(R_BV[l], R_BV[l] + P)
                if l == 1:
                    tt(v1[:, :, :], src[0:KEYS, :].rearrange("p (b d) -> p b d", d=P),
                       bcast(row[0:KEYS, bv], 1, BATCHES), ALU.add).then_inc(pre["v"], 1)
                    continue
                if l:
                    dve.wait_ge(pre["vbd"], l - 1)
                tt(vrep[:, :, :], src[:, :].rearrange("p (b d) -> p b d", d=P), bcast(row[:, bv], 1, BATCHES),
                   ALU.add).then_inc(pre["v"], 1)
                dve.wait_ge(pre["v"], n + 1)
                for b in range(BATCHES):
                    tt(vbd[l][:, b, :, 0:32].rearrange("p c (g d) -> p c g d", d=DEPTH),
                       vrep[:, b, :].rearrange("p (c g d) -> p c g d", g=4, d=DEPTH),
                       bcast(bcast(quadm, 2, DEPTH), 1, QUADS), ALU.mult)
                nc.vector.tensor_copy(vbd[l][:, :, :, 32:36].rearrange("p b c g -> p (b c) g"),
                                      bcast(quadm, 1, BATCHES * QUADS)).then_inc(pre["vbd"], 1)

            nc.vector.tensor_copy(bias16[:, 0, :], bias32).then_inc(pre["bias"], 1)
            dve.wait_ge(pre["bias"], 1)
            tt(bias16[:, 1, :], bias32, bias16[:, 0, :], ALU.subtract).then_inc(pre["bias"], 1)

            def ln_step(k, base, ln, src, dst, done, n=P, small=norm_x):
                stats, mean, var, rstd, tmp4 = (small[i] for i in ("stats", "mean", "var", "rstd", "tmp"))
                me, se, mo, so = (stats[:, :, i] for i in (1, 2, 4, 5))
                if k > 1:
                    dve.wait_ge(ln, base + k)
                root = float(np.sqrt(n)) if k in (12, 14) else 1.0
                if k < 2:
                    nc.vector.bn_stats(stats[:, 2 * k, :], src(2 * k))
                    ins = nc.vector.bn_stats(stats[:, 2 * k + 1, :], src(2 * k + 1))
                elif k == 2:
                    tt(tmp4[:, :], me, mo, ALU.subtract)
                    tt(var[:, :], se, so, ALU.add)
                    ins = tt(mean[:, :], me, mo, ALU.add)
                elif k == 3:
                    ts_(mean[:, :], mean[:, :], 0.5, None, ALU.mult)
                    ins = stt(tmp4[:, :], tmp4[:, :], n / 4.0, tmp4[:, :], ALU.mult, ALU.mult)
                elif k == 4:
                    ins = stt(var[:, :], tmp4[:, :], n * EPS, var[:, :], ALU.add, ALU.add)
                elif k == 5:
                    ins = ts_(rstd[:, :].bitcast(I32), var[:, :].bitcast(I32), -0.5, MAGIC, ALU.mult, ALU.add)
                elif k in (6, 9, 12):
                    ins = stt(tmp4[:, :], rstd[:, :], -0.5 * root, rstd[:, :], ALU.mult, ALU.mult)
                elif k in (7, 10, 13):
                    ins = tt(tmp4[:, :], tmp4[:, :], var[:, :], ALU.mult)
                elif k in (8, 11, 14):
                    ins = stt(rstd[:, :], tmp4[:, :], 1.5 * root, rstd[:, :], ALU.add, ALU.mult)
                else:
                    for t in (2 * k - 30, 2 * k - 29):
                        ins = ts_(dst(t), src(t), mean[:, t:t + 1], rstd[:, t:t + 1], ALU.subtract, ALU.mult)
                ins.then_inc(ln if k < 16 else done, 1)

            def prep(stage, b, *steps):
                if stage is None:
                    return
                s, r0 = SET[stage]
                for k in steps:
                    if k == 0:
                        stage_wait(dve, stage, b)
                    ln_step(k, LN_COUNT * (b + r0), s["ln"], lambda t: X[:, TILES * b + t, :],
                            lambda t: xn[:, t, :], s["xn"])

            def ahead(stage):
                low_part(int(stage[1]), 0)
                steps, route = {"f0": (13, route0), "f1": (12, route1), "f3": (14, route3)}[stage]
                for k in range(steps):
                    route(0, k)

            def heads(l):
                s, r0 = A[l], ROUND0[l]

                def softmax(b, t, between=lambda: None):
                    dve.wait_ge(s["scores"], TILES * (b + r0) + t + 1)
                    src = pb[t % 2][:, :].rearrange("p (h k) -> p h k", k=KEYS)
                    nc.vector.reduce_max(mx[:, t % 2, :], src, AX).then_inc(s["dve"], 1)
                    between()
                    dve.wait_ge(s["dve"], TILES * (b + r0) + t + 1)
                    if t >= 2:
                        dve.wait_ge(s["exped"], TILES * (b + r0) + t - 1)
                    tt(sub[t % 2], src, bcast(mx[:, t % 2, :], 2, KEYS), ALU.subtract).then_inc(s["subbed"], 1)

                def norm(b, t, between=lambda: None):
                    dve.wait_ge(s["av"], TILES * (b + r0) + t + 1)
                    src = pb[4 + t % 2][:, 0:QUADS * VCOLS].rearrange("p (c n) -> p c n", n=VCOLS)
                    if t:
                        dve.wait_ge(s["normed"], TILES * (b + r0) + t)
                    nc.vector.reciprocal(rinv[:, :, :], src[:, :, 32:36]).then_inc(s["dve2"], 1)
                    between()
                    dve.wait_ge(s["dve2"], TILES * (b + r0) + t + 1)
                    tt(o[:, t, :].rearrange("p (c g d) -> p c g d", g=4, d=DEPTH),
                       src[:, :, 0:32].rearrange("p c (g d) -> p c g d", d=DEPTH),
                       bcast(rinv[:, :, :], 3, DEPTH), ALU.mult).then_inc(s["normed"], 1)

                def free(b):
                    dve.wait_ge(s["xT_mm"], (b + r0) + 1)

                def body(b, left):
                    def ln(*steps):
                        if left > 1:
                            prep(f"a{l}", b + 2, *steps)
                        elif left:
                            prep(NEXT[f"a{l}"], 0, *steps)
                        elif l == 2:
                            for step in steps:
                                prep2(0, 17 + step)

                    softmax(b, 2, lambda: ln(0))
                    ln(1, 2)
                    norm(b, 0, lambda: ln(3))
                    ln(4)
                    softmax(b, 3, lambda: ln(5))
                    ln(6)
                    norm(b, 1, lambda: ln(7))
                    ln(8)
                    norm(b, 2, lambda: ln(9))
                    ln(10)
                    if left:
                        softmax(b + 1, 0, lambda: ln(11))
                        ln(12)
                        norm(b, 3, lambda: ln(13))
                        softmax(b + 1, 1, lambda: ln(14))
                        free(b + 1)
                        ln(15, 16)
                    else:
                        norm(b, 3, lambda: ln(11))
                        ln(12, 13, 14, 15, 16)
                        if l != 2:
                            ahead(NEXT[f"a{l}"])
                    dve.wait_ge(s["proj"], (b + r0) + 1)
                    tt(X[:, bass.ds(TILES * b, TILES), :], pb[7][:, :].rearrange("p (t d) -> p t d", d=P),
                       X[:, bass.ds(TILES * b, TILES), :], ALU.add).then_inc(s["x"], 1)

                if l == 0:
                    prep("a0", 0, *range(17))
                prep(f"a{l}", 1, *range(8))
                softmax(0, 0, lambda: prep(f"a{l}", 1, *range(8, 12)))
                softmax(0, 1, lambda: prep(f"a{l}", 1, 12, 13))
                prep(f"a{l}", 1, 14)
                free(0)
                prep(f"a{l}", 1, 15, 16)
                with dve.Fori(0, BATCHES - 2) as b:
                    body(b, 2)
                body(BATCHES - 2, 1)
                body(BATCHES - 1, 0)

            def single():
                s = A[1]
                isq = float(np.float32(1.0) / np.sqrt(np.float32(P)))

                def body(b, left):
                    def ln(*steps):
                        if left > 1:
                            prep("a1", b + 2, *steps)
                        elif left:
                            prep("f1", 0, *steps)

                    ch = Chain(dve, s["dve"], 7, b)
                    ch.then(ts_(allow[:, :, :], m1[:, bass.ds(TILES * b, TILES), :], 0.0, None, ALU.not_equal))
                    ch.then(ts_(penal[:, :, :], allow[:, :, :], 1e10, -1e10, ALU.mult, ALU.add))
                    dve.wait_ge(s["scores"], b + 1)
                    ch.then(stt(s1b[:, :, :], pb[0][:, 0:P].rearrange("p (t k) -> p t k", k=KEYS), isq,
                                allow[:, :, :], ALU.mult, ALU.mult))
                    ch.then(tt(allow[:, :, :], s1b[:, :, :], penal[:, :, :], ALU.add))
                    ch.then(nc.vector.reduce_max(gmax[:, :], allow[:, :, :], AX))
                    tt(s1b[:, :, :], allow[:, :, :], bcast(gmax[:, :], 2, KEYS), ALU.subtract)\
                        .then_inc(s["subbed"], 1)
                    ln(*range(7))
                    dve.wait_ge(s["exped"], b + 1)
                    ch.then(nc.vector.reduce_sum(gsum[:, :], s1a[:, :, :], AX), lambda: ln(7))
                    ch.then(nc.vector.reciprocal(inv1[:, :], gsum[:, :]), lambda: ln(8))
                    ch.done()
                    ln(*range(9, 15))
                    if left:
                        dve.wait_ge(s["xT_mm"], b + 2)
                    ln(15, 16)
                    if not left:
                        ahead("f1")
                    dve.wait_ge(s["av"], b + 1)
                    for t in range(TILES):
                        ins = stt(X[:, TILES * b + t, :], pb[4][:, t * P:(t + 1) * P], inv1[:, t:t + 1],
                                  X[:, TILES * b + t, :], ALU.mult, ALU.add)
                    ins.then_inc(s["x"], 1)

                prep("a1", 1, *range(15))
                dve.wait_ge(s["xT_mm"], 1)
                prep("a1", 1, 15, 16)
                dve.wait_ge(ld["m1"], 16)
                with dve.Fori(0, BATCHES - 2) as b:
                    body(b, 2)
                body(BATCHES - 2, 1)
                body(BATCHES - 1, 0)

            def low_part(l, b):
                s = F[l]
                dve.wait_ge(s["xT"], b + 1)
                dve.wait_ge(s["xh"], b + 1)
                tt(xl[:, b, :], xnT[:, :], xh[:, b, :], ALU.subtract).then_inc(s["xl"], 1)

            def choose(k, score, n):
                it = bcast(iota[:, 0:n], 1, TILES)
                if k < 2:
                    dve.drain()
                    for t in range(TILES):
                        ins = nc.vector.max(top[:, t, :], score[:, t, 0:n]) if k == 0 else \
                            nc.vector.max_index(topi[:, t, :], top[:, t, :], score[:, t, 0:n])
                elif k == 2:
                    ins = tt(pick[:, :, 0:n], it, bcast(topi[:, :, 0], 2, n), ALU.is_equal)
                elif k in (3, 5):
                    ins = tt(gtmp[:, :, 0:n], it, bcast(topi[:, :, (k - 1) // 2], 2, n), ALU.is_equal)
                else:
                    ins = tt(pick[:, :, 0:n], pick[:, :, 0:n], gtmp[:, :, 0:n], ALU.add)
                return ins

            def add_expert(s, b, e, n, bank, weights, aside, slot):
                dve.wait_ge(s["down"], n * b + e + 1)
                if e:
                    dve.wait_ge(s["acc"], n * b + e)
                for t in range(TILES):
                    ins = stt(acc[:, t, :], pb[bank][:, t * P:(t + 1) * P], weights(t), acc[:, t, :],
                              ALU.mult, ALU.add)
                    if t == TILES - 1:
                        ins.then_inc(s["acc"], 1)
                    aside(slot + t)

            def add_batch(s, b, count):
                dve.wait_ge(s["acc"], count * (b + 1))
                xs = X[:, bass.ds(TILES * b, TILES), :]
                tt(xs, acc[:, :, :], xs, ALU.add).then_inc(s["x"], 1)

            logits0 = pb[6][:, 0:TILES * E0].rearrange("p (t e) -> p t e", e=E0)
            counts0 = pb[7][:, 0:TILES * E0].rearrange("p (t e) -> p t e", e=E0)
            g0, e0_, pk0, tm0 = (a[:, :, 0:E0] for a in (gate, gexp, pick, gtmp))
            STEPS0 = 18

            def route0(b, k):
                if k == 0:
                    dve.wait_ge(F[0]["route_mm"], b + 1)
                    nc.vector.reduce_max(gmax[:, :], logits0, AX).then_inc(F[0]["dve"], 1)
                elif k == 1:
                    dve.wait_ge(F[0]["dve"], STEPS0 * b + 1)
                    tt(g0, logits0, bcast(gmax[:, :], 2, E0), ALU.subtract).then_inc(F[0]["diff"], 1)
                elif k == 2:
                    dve.wait_ge(F[0]["gexp"], b + 1)
                    nc.vector.reduce_sum(gsum[:, :], e0_, AX).then_inc(F[0]["dve"], 1)
                elif k < 8:
                    if k > 4:
                        dve.wait_ge(F[0]["dve"], STEPS0 * b + k - 1)
                    choose(k - 3, gexp, E0).then_inc(F[0]["dve"], 1)
                elif k == 8:
                    dve.wait_ge(F[0]["dve"], STEPS0 * b + k - 1)
                    nc.vector.tensor_copy(mask16[:, :, :], pk0).then_inc(F[0]["dve"], 1)
                elif k < 13:
                    t = k - 9
                    dve.wait_ge(F[0]["dve"], STEPS0 * b + k - 1)
                    tt(before[:, t + 1, :], before[:, t, :], mask16[:, t, :], ALU.add)\
                        .then_inc(F[0]["masks" if k == 12 else "dve"], 1)
                elif k == 13:
                    dve.wait_ge(F[0]["count_mm"], b + 1)
                    ts_(tm0, counts0, float(CAPACITY), None, ALU.is_le)
                    nc.vector.tensor_copy(before[:, 0, :], before[:, TILES, :]).then_inc(F[0]["dve"], 1)
                else:
                    dve.wait_ge(F[0]["dve"], STEPS0 * b + k - 2)
                    if k == 14:
                        ins = tt(pk0, pk0, tm0, ALU.mult)
                    elif k == 15:
                        ins = tt(g0, e0_, pk0, ALU.mult)
                    elif k == 16:
                        ins = nc.vector.reduce_sum(gmax[:, :], g0, AX)
                    elif k == 17:
                        ins = stt(gden[:, :], gsum[:, :], 1e-6, gmax[:, :], ALU.mult, ALU.add)
                    elif k == 18:
                        ins = ts_(gsum[:, :], gden[:, :], WSCALE, None, ALU.mult)
                    elif k == 19:
                        ins = nc.vector.reciprocal(gden[:, :], gsum[:, :])
                    else:
                        ins = tt(cw[:, :, 0:E0], g0, bcast(gden[:, :], 2, E0), ALU.mult)
                    ins.then_inc(F[0]["cw" if k == 20 else "dve"], 1)

            e1_, g1, tm1 = gexp[:, :, 0:E1], gate[:, :, 0:E1], gtmp[:, :, 0:E1]
            STEPS1 = 11

            def route1(b, k):
                if k == 0:
                    dve.wait_ge(F[1]["gexp"], b + 1)
                    ins = ts_(tm1, e1_, 1.0, None, ALU.add)
                else:
                    if k not in (2, 3):
                        dve.wait_ge(F[1]["dve"], STEPS1 * b + k)
                    if k == 1:
                        ins = nc.vector.reciprocal(g1, tm1)
                    elif k < 7:
                        ins = choose(k - 2, gate, E1)
                    elif k == 7:
                        ins = tt(tm1, g1, pick[:, :, 0:E1], ALU.mult)
                    elif k == 8:
                        ins = nc.vector.reduce_sum(gsum[:, :], tm1, AX)
                    elif k == 9:
                        ins = ts_(gmax[:, :], gsum[:, :], 3.0 * WSCALE, None, ALU.mult)
                    elif k == 10:
                        ins = nc.vector.reciprocal(gden[:, :], gmax[:, :])
                    else:
                        ins = tt(g1, tm1, bcast(gden[:, :], 2, E1), ALU.mult)
                ins.then_inc(F[1]["dve" if k < 11 else "cw"], 1)

            STEPS3 = 12

            def route3(b, k):
                if k == 0:
                    dve.wait_ge(F[3]["route_mm"], b + 1)
                    nc.vector.tensor_copy(logit3[:, :, :], pb[6][:, 0:TILES * E3]
                                          .rearrange("p (t e) -> p t e", e=E3)).then_inc(F[3]["dve"], 1)
                elif k < 8:
                    if k > 2:
                        dve.wait_ge(F[3]["dve"], STEPS3 * b + k)
                    choose(k - 1, logit3, E3).then_inc(F[3]["dve"], 1)
                elif k == 8:
                    tt(gate[:, :, :], logit3[:, :, :], bcast(top[:, :, 0], 2, E3), ALU.subtract)\
                        .then_inc(F[3]["diff"], 1)
                else:
                    if k == 9:
                        dve.wait_ge(F[3]["gexp"], b + 1)
                    dve.wait_ge(F[3]["dve"], STEPS3 * b + k - 1)
                    if k == 9:
                        ins = tt(gtmp[:, :, :], gexp[:, :, :], pick[:, :, :], ALU.mult)
                    elif k == 10:
                        ins = nc.vector.reduce_sum(gsum[:, :], gtmp[:, :, :], AX)
                    elif k == 11:
                        ins = ts_(gmax[:, :], gsum[:, :], WSCALE, None, ALU.mult)
                    elif k == 12:
                        ins = nc.vector.reciprocal(gden[:, :], gmax[:, :])
                    else:
                        ins = tt(gate[:, :, :], gtmp[:, :, :], bcast(gden[:, :], 2, E3), ALU.mult)
                    ins.then_inc(F[3]["dve" if k < 13 else "cw"], 1)

            def abs_sums(ch):
                dve.wait_ge(ld["mlp"], 16)
                for i in range(2):
                    ch.then(stt(big[:, 1, 2 + i, :], mw[:, i, :], -1.0, mw[:, i, :], ALU.mult, ALU.max))
                ch.then(nc.vector.reduce_sum(qsum[:, :], big[:, 1, 2:4, :], AX))
                nc.vector.tensor_copy(qs[:, 0, :], qsum[:, :]).then_inc(pre["abs"], 1)

            def small_preparations(ch):
                dve.wait_ge(pre["abs_mm"], 1)
                ch.then(ts_(qs[:, 0, :], pb[7][:, 64:66], 1.0 / (512 * P), 1e-5, ALU.mult, ALU.max))
                ch.then(nc.vector.reciprocal(qs[:, 1, :], qs[:, 0, :]))
                ch.then(nc.vector.reciprocal(qs[:, 2, :], qs[:, 1, :]))
                for i in range(2):
                    sc, inv = qs[:, 1, i:i + 1], qs[:, 2, i:i + 1]
                    t0, t1 = big[:, 1, 2, :], big[:, 1, 3, :]
                    ch.then(ts_(t0, mw[:, i, :], sc, 0.5, ALU.mult, ALU.is_gt))
                    ch.then(ts_(t1, mw[:, i, :], sc, -0.5, ALU.mult, ALU.is_lt))
                    ch.then(tt(t0, t0, t1, ALU.subtract))
                    ch.then(stt(t1, t0, inv, mw[:, i, :], ALU.mult, ALU.subtract))
                    tt(wq[:, i, :], mw[:, i, :], t1, ALU.add).then_inc(pre["quant"], 1)
                    dve.wait_ge(pre["quant"], i + 1)
                dve.wait_ge(ld["bd"], 16)
                ts_(bd[:, :], bd[:, :], WSCALE, None, ALU.mult).then_inc(pre["quant"], 1)
                dve.wait_ge(ld["m2"], 16)
                for b in range(BATCHES):
                    ins = ts_(m2b[:, b, :, :], bcast(m2[:, b, :], 1, HEADS), -1e30, None, ALU.mult)
                ch.then(ins)

            def moe0():
                s = F[0]

                def split(b):
                    dve.wait_ge(s["hh"], b + 1)
                    tt(hl[:, 0, 0:2, :], big[:, 0, 0:2, :], hh[:, 0, 0:2, :], ALU.subtract).then_inc(s["split"], 1)

                def aside(b, more, slot):
                    if slot < 8:
                        prep(*following("f0", b, more), slot + 9)
                    elif more and slot == 14:
                        low_part(0, b + 1)
                    elif more and slot in (16, 17):
                        route0(b + 1, slot - 16)
                    elif more and 19 <= slot < 30:
                        route0(b + 1, slot - 17)
                    elif more and slot == 31:
                        split(b + 1)

                def add(b, more, t):
                    dve.wait_ge(s["down"], TILES * b + t + 1)
                    for n in range(E0):
                        at = 2 + 2 * (t % 2) + n // 4
                        src, weight = pb[at][:, (n % 4) * P:(n % 4 + 1) * P], cw[:, t, n:n + 1]
                        if n == 0:
                            ins = ts_(acc[:, t, :], src, weight, None, ALU.mult)
                        else:
                            dve.wait_ge(s["acc"], E0 * (TILES * b + t) + n)
                            ins = stt(acc[:, t, :], src, weight, acc[:, t, :], ALU.mult, ALU.add)
                        ins.then_inc(s["acc"], 1)
                        aside(b, more, E0 * t + n)

                def body(b, more):
                    prep(*following("f0", b, more), *range(9))
                    dve.wait_ge(s["cw"], b + 1)
                    for t in range(TILES):
                        add(b, more, t)
                    add_batch(s, b, TILES * E0)
                    if more:
                        for k in range(13, 21):
                            route0(b + 1, k)

                ch = Chain(dve, pre["dve"], 0, 0)
                abs_sums(ch)
                split(0)
                dve.wait_ge(pre["abs_mm"], 1)
                for k in range(13, 21):
                    route0(0, k)
                small_preparations(ch)
                with dve.Fori(0, BATCHES - 1) as b:
                    body(b, True)
                body(BATCHES - 1, False)

            def moe1():
                s = F[1]

                def begin(b, first=False):
                    dve.wait_ge(s["cw"], b + 1)
                    nc.vector.tensor_copy(cw[:, :, 0:E1], gate[:, :, 0:E1])
                    if not first:
                        dve.wait_ge(s["x"], b)
                    nc.vector.memset(acc[:, :, :], 0.0).then_inc(s["diff"], 1)
                    dve.wait_ge(s["diff"], b + 1)

                def multiply(b, e):
                    j, at = place(e)
                    for c in range(2):
                        dve.wait_ge(s["act"], 2 * (S1 * b + e) + c + 1)
                        dve.wait_ge(s["up"], 4 * (S1 * b + e) + 2 * c + 2)
                        stt(big[:, j, at + c, :], pb[2 + c][:, :], 1.0 / WSCALE, big[:, j, at + c, :],
                            ALU.mult, ALU.mult).then_inc(s["prod"], 1)


                def body(b, more):
                    def aside(slot):
                        if slot < 17:
                            prep(*following("f1", b, more), slot)
                        elif more and slot == 20:
                            low_part(1, b + 1)
                        elif more and 30 <= slot < 42:
                            route1(b + 1, slot - 30)

                    def weights(e):
                        if e < E1:
                            return lambda t: cw[:, t, e:e + 1]
                        return lambda t: 1.0 / (3.0 * WSCALE)

                    for e in range(S1):
                        last = e == S1 - 1
                        if not last:
                            multiply(b, e + 1)
                        elif more:
                            multiply(b + 1, 0)
                        add_expert(s, b, e, S1, BANK_LAST if last else 4 + e % 2, weights(e), aside, 5 * e)
                        aside(5 * e + 4)
                    add_batch(s, b, S1)
                    if more:
                        begin(b + 1)

                begin(0, first=True)
                multiply(0, 0)
                with dve.Fori(0, BATCHES - 1) as b:
                    body(b, True)
                body(BATCHES - 1, False)

            def moe3():
                s = F[3]

                def begin(b, first=False):
                    nc.vector.tensor_copy(cw[:, :, 0:E3], gate[:, :, :])
                    if not first:
                        dve.wait_ge(s["x"], b)
                    dve.wait_ge(s["bias_mm"], b + 1)
                    nc.vector.tensor_copy(acc[:, :, :], pb[6][:, :].rearrange("p (t d) -> p t d", d=P))\
                        .then_inc(s["bias"], 1)
                    dve.wait_ge(s["bias"], b + 1)

                def split(b, e, j, half):
                    at = slice(2 * half, 2 * half + 2)
                    dve.wait_ge(s["hh"], 2 * (E3 * b + e) + half + 1)
                    ins = tt(hl[:, j, at, :], big[:, j, at, :], hh[:, j, at, :], ALU.subtract)
                    if half:
                        ins.then_inc(s["split"], 1)

                def body(b, more):
                    def aside(slot):
                        if not more:
                            return
                        if slot < 17:
                            prep("f3", b + 1, slot)
                        elif slot == 30:
                            low_part(3, b + 1)
                        elif 36 <= slot < 45:
                            route3(b + 1, slot - 36)
                        elif 48 <= slot < 53:
                            route3(b + 1, slot - 39)

                    for e in range(E3):
                        after = (b, e + 1) if e < E3 - 1 else (b + 1, 0)
                        for half in range(2):
                            if e < E3 - 1 or more:
                                split(*after, (e + 1) % 2, half)
                            aside(6 * e + half)
                        add_expert(s, b, e, E3, 4 + e % 2, lambda t: cw[:, t, e:e + 1], aside, 6 * e + 2)
                    add_batch(s, b, E3)
                    if more:
                        begin(b + 1)

                for half in range(2):
                    split(0, 0, 0, half)
                dve.wait_ge(s["cw"], 1)
                begin(0, first=True)
                with dve.Fori(0, BATCHES - 1) as b:
                    body(b, True)
                body(BATCHES - 1, False)

            def prep2(b, step):
                if step < 17:
                    prep("f2", b, step)
                else:
                    if step == 17:
                        dve.wait_ge(M["xn"], b + 1)
                    ln_step(step - 17, LN_COUNT * b, M["ln2"], lambda t: xn[:, t, :], lambda t: xn[:, t, :], M["xn2"])

            def mlp():
                s = M

                def hidden_step(b, k):
                    if k < 2:
                        dve.wait_ge(s["gelu"], TILES * b + 2 * k + 2)
                    ln_step(k, 15 * b, s["dve"], lambda t: big[:, 1, t, :], None, None, 512, norm_h)

                def hidden_norm(b, t):
                    if t == 0:
                        dve.wait_ge(s["dve"], 15 * (b + 1))
                    ts_(big[:, 0, t, :], big[:, 1, t, :], norm_h["mean"][:, t:t + 1], norm_h["rstd"][:, t:t + 1],
                        ALU.subtract, ALU.mult).then_inc(s["n"], 1)

                def add(b):
                    dve.wait_ge(s["down"], TILES * b + TILES)
                    xs = X[:, bass.ds(TILES * b, TILES), :]
                    tt(xs, pb[7][:, :].rearrange("p (t d) -> p t d", d=P), xs, ALU.add).then_inc(s["x"], 1)

                def statistics(b, ahead, steps):
                    for step in range(4, 15):
                        ahead(step)
                    for k in range(15):
                        hidden_step(b, k)
                        for step in (2 * k + 15, 2 * k + 16):
                            if step < steps:
                                ahead(step)

                def body(b, left):
                    def ahead(step):
                        if left > 1:
                            prep2(b + 2, step)
                        else:
                            prep("a3", 0, step)

                    for t in range(TILES):
                        hidden_norm(b, t)
                        if left:
                            ahead(t)
                    if left:
                        statistics(b + 1, ahead, 34 if left > 1 else 17)
                    add(b)

                for step in range(4):
                    prep2(1, step)
                statistics(0, lambda step: prep2(1, step), 34)
                with dve.Fori(0, BATCHES - 2) as b:
                    body(b, 2)
                body(BATCHES - 2, 1)
                body(BATCHES - 1, 0)

            for n, stage in enumerate((lambda: heads(0), moe0, single, moe1, lambda: heads(2), mlp,
                                       lambda: heads(3), moe3)):
                if n < STAGES:
                    stage()


def layout(i):
    c = np.ascontiguousarray

    def wide(a, chunks):
        return a.reshape(chunks, P, -1).transpose(1, 0, 2).reshape(P, -1)

    ctx = i["ctx_1024"].transpose(2, 0, 1)[:, :, None, :]
    ctx = np.broadcast_to(ctx, (P, BATCHES, QUADS, KEYS))
    kv_w = i["L2_xattn_kv_w"]
    att = [i["L0_xattn_Wq"], i["L0_xattn_Wk"], i["L0_xattn_Wv"], i["L0_xattn_Wo"],
           i["L1_xattn_Wq"].T, i["L1_xattn_Wk"].T, i["L1_xattn_Wv"].T,
           i["L2_xattn_q_w"], kv_w[:, :P], kv_w[:, P:], i["L2_xattn_proj_w"],
           i["L3_xattn_w_q"].T, i["L3_xattn_w_k"].T, i["L3_xattn_w_v"].T, i["L3_xattn_w_o"].T]
    kv_b = i["L2_xattn_kv_b"]
    cols = [i["L0_xattn_bq"][:, None], i["L0_xattn_bk"][:, None], i["L1_xattn_bq"][:, None],
            i["L1_xattn_bk"][:, None], i["L2_xattn_q_b"][:, None], kv_b[:P, None],
            i["L3_xattn_b_q"][:, None], i["L3_xattn_b_k"][:, None],
            i["L2_ffn_ln1_g"][:, None], i["L2_ffn_ln1_b"][:, None],
            i["L2_ffn_ln2_g"].reshape(4, P).T, i["L2_ffn_ln2_b"].reshape(4, P).T,
            i["L3_ffn_bup"].reshape(4 * E3, P).T]
    rows = [i["L0_xattn_bv"], i["L1_xattn_bv"], kv_b[P:], i["L3_xattn_b_v"]]
    biases = [i["L0_xattn_bo"], i["L2_xattn_proj_b"], i["L3_xattn_b_o"], i["L2_ffn_b2"], i["L2_ffn_b1"]]
    router = [i["L0_ffn_w_router"].T, i["L1_ffn_Wg"], i["L3_ffn_Wg"]]

    def experts(shared, routed):
        return np.concatenate([routed, shared[None]], 0)

    w1 = experts(i["L1_ffn_Ws1"], i["L1_ffn_We1"]).transpose(1, 0, 2).reshape(P, -1)
    w3 = experts(i["L1_ffn_Ws3"], i["L1_ffn_We3"]).transpose(1, 0, 2).reshape(P, -1)
    w2 = experts(i["L1_ffn_Ws2"], i["L1_ffn_We2"]).reshape(S1, 2, P, P).transpose(2, 0, 1, 3).reshape(P, -1)
    down0 = i["L0_ffn_w_down"].transpose(2, 0, 1).reshape(2, P, E0, P).transpose(1, 0, 2, 3).reshape(P, -1)
    up3 = i["L3_ffn_Wup"].transpose(1, 0, 2).reshape(P, -1)
    down3 = i["L3_ffn_Wdown"].reshape(E3, 4, P, P).transpose(2, 0, 1, 3).reshape(P, -1)
    moe = [i["L0_ffn_w_gate"].T, down0, w1, w3, w2, up3, down3]
    mlp = [i["L2_ffn_w1"].T, wide(i["L2_ffn_w2"].T, 4)]

    consts = np.zeros((P, K_COLS), np.float32)
    p = np.arange(P)
    consts[p, K_ID + p] = 1.0
    consts[:, K_TRI:K_TRI + P] = p[:, None] <= p[None, :]
    consts[:, K_HEAD:K_HEAD + HEADS] = p[:, None] // DEPTH == np.arange(HEADS)[None, :]
    consts[:, K_QUAD:K_QUAD + QUADS] = p[:, None] // KEYS == np.arange(QUADS)[None, :]
    consts[:, K_IOTA:K_IOTA + 12] = np.arange(12)[None, :]
    return {
        "x": c(i["x"].reshape(BATCHES * SEQ, P)),
        "ctx": c(ctx),
        "attw": c(np.concatenate([a.reshape(P, 1, P) for a in att], 1)),
        "cols": c(np.concatenate(cols, 1)),
        "rows": c(np.concatenate(rows)[None, :]),
        "biases": c(np.concatenate(biases)[None, :]),
        "router": c(np.concatenate(router, 1)),
        "moe_w": c(np.concatenate(moe, 1)),
        "mlp_w": c(np.concatenate([a.reshape(P, 1, 512) for a in mlp], 1)),
        "bdown": c(i["L3_ffn_bdown"]),
        "mask1": c(i["mask_BxSxS2_ik1"].reshape(BATCHES * SEQ, KEYS)),
        "mask2": c(i["mask_BxS2_bk0"].reshape(1, BATCHES, KEYS)),
        "consts": consts,
    }


def kernel(**inputs):
    import concourse.bacc as bacc
    from concourse.bass_utils import run_bass_kernel_spmd as run

    nc = bacc.Bacc("TRN2", target_bir_lowering=False, num_devices=1)
    arrays = layout({k: np.asarray(v) for k, v in inputs.items()})
    args = [nc.dram_tensor(n, a.shape, mybir.dt.from_np(a.dtype), kind="ExternalInput").ap()
            for n, a in arrays.items()]
    out = nc.dram_tensor("out", (BATCHES * SEQ, P), F32, kind="ExternalOutput").ap()
    build(nc, *args, out)
    r = run(nc, [arrays], core_ids=[0])
    return r.results[0]["out"].reshape(BATCHES, SEQ, P)
```

```python
import concourse.bass as bass
import numpy as np
from concourse import mybir
from contextlib import ExitStack

F32 = mybir.dt.float32
F16 = mybir.dt.float16
BF16 = mybir.dt.bfloat16
I32 = mybir.dt.int32
U32 = mybir.dt.uint32
U8 = mybir.dt.uint8
ALU = mybir.AluOpType
ACT = mybir.ActivationFunctionType
AX = mybir.AxisListType.X

P = 128
BATCHES, SEQ, KEYS = 4, 512, 32
TILES = SEQ // P
NTILES = BATCHES * TILES
HEADS, DEPTH = 16, 8
QUADS = 4
VCOLS = 36
E0, E1, E3 = 8, 8, 12
S1 = E1 + 1
AT_LAST = 2
BANK_LAST = 7
BY_DVE = 9
CAPACITY = -(-BATCHES * SEQ * 5 // (E0 * 4))
WSCALE = 64.0
EPS = 1e-5
MAGIC = float(0x5F3759DF)

W_GATE = 0
W_DOWN0 = W_GATE + 256
W_1 = W_DOWN0 + 2 * E0 * P
W_3 = W_1 + S1 * 256
W_2 = W_3 + S1 * 256
W_UP = W_2 + S1 * 256
W_DOWN3 = W_UP + E3 * 512
W_COLS = W_DOWN3 + E3 * 512
PIECE = 384
PIECES = W_COLS // PIECE
PIECES_L0 = -(-W_1 // PIECE)
PIECES_L1 = -(-W_UP // PIECE)

Q, K, V, O = 0, 1, 2, 3
ATT_AT = {0: 0, 1: 4, 2: 7, 3: 11}
C_BQ = {0: 0, 1: 2, 2: 4, 3: 6}
C_BK = {0: 1, 1: 3, 2: 5, 3: 7}
C_G1, C_B1, C_G2, C_B2, C_BUP = 8, 9, 10, 14, 18
C_COLS = C_BUP + 4 * E3
R_BV = {0: 0, 1: 128, 2: 256, 3: 384}
R_COLS = 512
B_O = {0: 0, 2: 128, 3: 256}
B_2, B_1 = 384, 512
B_COLS = 1024
K_ID, K_TRI, K_HEAD, K_QUAD, K_IOTA = 0, 128, 256, 272, 276
K_COLS = K_IOTA + 12
STAGES = 8
LN_COUNT = 16


class Chain:

    def __init__(self, eng, sem, per, rnd):
        self.eng, self.sem, self.per, self.rnd, self.at = eng, sem, per, rnd, 0

    def then(self, ins, between=None):
        self.at += 1
        ins.then_inc(self.sem, 1)
        if between:
            between()
        self.eng.wait_ge(self.sem, self.rnd * self.per + self.at)

    def done(self):
        assert self.at == self.per, (self.at, self.per)


def bcast(ap, axis, count):
    shape = list(ap.shape)
    shape.insert(axis, count)
    return ap.unsqueeze(axis).to_broadcast(shape)


def build(nc, x, ctx, attw, cols, rows, biases, router, moe_w, mlp_w, bdown, mask1, mask2, consts, out):
    stack = ExitStack()
    with stack:
        def sb(name, shape, dt=F32):
            return stack.enter_context(nc.sbuf_tensor(name, shape, dt))

        def sem(name):
            return stack.enter_context(nc.semaphore(name))

        def sems(prefix, *names):
            return {n: sem(f"{prefix}_{n}") for n in names}

        X = sb("X", [P, NTILES, P])
        ctxT = sb("ctxT", [P, BATCHES, QUADS, KEYS])
        aw = sb("aw", [P, 15, P])
        col = sb("col", [P, C_COLS])
        row = sb("row", [P, R_COLS])
        bias16 = sb("bias16", [1, 2, B_COLS], F16)
        wr = sb("wr", [P, E0 + E1 + E3])
        raw = [sb(f"raw{i}", [P, PIECE]) for i in range(2)]
        scaled = [sb(f"scaled{i}", [P, PIECE]) for i in range(2)]
        scale64 = sb("scale64", [P, 1])
        WH = sb("WH", [P, W_COLS], F16)
        WL = sb("WL", [P, W_COLS], F16)
        mw = sb("mw", [P, 2, 512])
        bd = sb("bd", [E3, P])
        m1 = sb("m1", [P, NTILES, KEYS], I32)
        m2 = sb("m2", [1, BATCHES, KEYS], U8)
        kc = sb("kc", [P, K_COLS])
        ident = kc[:, K_ID:K_ID + P]
        headm = kc[:, K_HEAD:K_HEAD + HEADS]
        quadm = kc[:, K_QUAD:K_QUAD + QUADS]
        iota = kc[:, K_IOTA:K_IOTA + 12]
        tri16 = sb("tri16", [P, P], F16)
        ones16 = sb("ones16", [P, P], F16)
        ones = sb("ones", [P, P])
        onesb = sb("onesb", [1, P], BF16)
        m2b = sb("m2b", [1, BATCHES, HEADS, KEYS], BF16)
        kT = sb("kT", [P, 4, BATCHES, KEYS])
        kbd02 = sb("kbd02", [P, BATCHES, HEADS, KEYS])
        kbd = {0: kbd02, 2: kbd02, 3: sb("kbd3", [P, BATCHES, HEADS, KEYS])}
        vbd = {l: sb(f"vbd{l}", [P, BATCHES, QUADS, VCOLS]) for l in (0, 2, 3)}
        v1 = sb("v1", [KEYS, BATCHES, P])
        xn = sb("xn", [P, TILES, P])
        xnT = sb("xnT", [P, SEQ])
        xh = sb("xh", [P, BATCHES, SEQ], F16)
        xl = sb("xl", [P, BATCHES, SEQ], F16)
        qT = sb("qT", [P, SEQ])
        big = sb("big", [P, 2, 4, SEQ])
        sub = [big[:, 0, j, :].rearrange("p (h k) -> p h k", k=KEYS) for j in range(2)]
        prob = [big[:, 0, 2 + j, :] for j in range(2)]
        probT = [big[:, 1, j, :].rearrange("p (c t) -> p c t", t=P) for j in range(2)]
        hh = sb("hh", [P, 2, 4, SEQ], F16)
        hl = sb("hl", [P, 2, 4, SEQ], F16)
        mx = sb("mx", [P, 2, HEADS])
        rinv = sb("rinv", [P, QUADS, 4])
        o = sb("o", [P, TILES, P])
        vrep = o
        oT = sb("oT", [P, SEQ])
        cwT = oT[0:E3, :]
        p1T = oT[0:KEYS, :]
        norm_x, norm_h = ({"stats": sb(f"stats_{i}", [P, TILES, 6]), "mean": sb(f"mean_{i}", [P, TILES]),
                           "var": sb(f"var_{i}", [P, TILES]), "rstd": sb(f"rstd_{i}", [P, TILES]),
                           "tmp": sb(f"tmp_{i}", [P, TILES])} for i in "xh")
        gate = sb("gate", [P, TILES, 12])
        logit3 = sb("logit3", [P, TILES, 12])
        gexp = sb("gexp", [P, TILES, 12])
        gtmp = sb("gtmp", [P, TILES, 12])
        pick = sb("pick", [P, TILES, 12])
        top = sb("top", [P, TILES, 8])
        topi = sb("topi", [P, TILES, 8], U32)
        gsum = sb("gsum", [P, TILES])
        gden = sb("gden", [P, TILES])
        gmax = sb("gmax", [P, TILES])
        mask16 = sb("mask16", [P, TILES, E0], F16)
        before = sb("before", [P, TILES + 1, E0], F16)
        cw = sb("cw", [P, TILES, 12])
        acc = o
        bias32 = big[0:1, 1, 2:4, :].rearrange("p a b -> p (a b)")
        inv1 = mx[:, 0, 0:TILES]
        allow, penal, s1a, s1b = (big[:, 1, 2, i * P:(i + 1) * P].rearrange("p (t k) -> p t k", k=KEYS)
                                  for i in range(4))
        qsum = sb("qsum", [P, 2])
        qs = sb("qs", [P, 4, 2])
        wq = mw

        pb = [stack.enter_context(nc.psum_tensor(f"pb{i}", [P, 512], F32)) for i in range(8)]

        hl_f = [hl[:, j, 0:2, :].bitcast(F32).rearrange("p a b -> p (a b)").rearrange("p (c t) -> p c t", t=P)
                for j in range(2)]

        ld = sems("ld", "first", "x0", "rows", "x", "att", "small", "const", "mlp", "m1", "m2", "bd", "stored")
        ld_w = [sem(f"ld_w{i}") for i in range(2)]
        w = sems("w", "raw_used")
        pre = sems("pre", "spread", "bias", "kT_mm", "kT", "v_mm", "v", "const", "kbd", "vbd",
                   "dve", "abs", "abs_mm", "quant")
        shared = ("ln", "xn", "xT_mm", "xT", "q_mm", "q", "scores", "subbed", "exped", "pT_mm", "pT", "av",
                  "dve", "x")
        many = ("dve2", "normed", "oT_mm", "oT", "proj")
        heads_sems = sems("heads", *shared, *many)
        A = {0: heads_sems, 1: sems("single", *shared), 2: heads_sems, 3: heads_sems}
        ROUND0 = {0: 0, 1: 0, 2: BATCHES, 3: 2 * BATCHES}
        common = ("ln", "xn", "xT_mm", "xT", "xh", "xl", "route_mm", "diff", "gexp", "dve", "cw", "up", "act", "hh",
                  "split", "down", "acc", "x")
        own = {0: ("masks", "count_mm"), 1: ("prod",), 3: ("high", "cwT_mm", "cwT", "bias_mm", "bias")}
        F = {l: sems(f"f{l}", *common, *own[l]) for l in (0, 1, 3)}
        M = sems("m", "ln", "xn", "ln2", "xn2", "xT_mm", "xT", "up", "gelu", "dve", "n", "nT_mm", "nT", "down", "x")

        block = stack.enter_context(nc.Block())

        XADD = {"a0": (A[0]["x"], 1, 0), "f0": (F[0]["x"], 1, 0), "a1": (A[1]["x"], 1, 0), "f1": (F[1]["x"], 1, 0),
                "a2": (A[2]["x"], 1, ROUND0[2]), "f2": (M["x"], 1, 0), "a3": (A[3]["x"], 1, ROUND0[3]),
                "f3": (F[3]["x"], 1, 0)}
        SET = {"a0": (A[0], 0), "f0": (F[0], 0), "a1": (A[1], 0), "f1": (F[1], 0), "a2": (A[2], ROUND0[2]),
               "f2": (M, 0), "a3": (A[3], ROUND0[3]), "f3": (F[3], 0)}
        NEXT = {"a0": "f0", "f0": "a1", "a1": "f1", "f1": "a2", "a2": "f2", "f2": "a3", "a3": "f3", "f3": None}

        def following(stage, b, more):
            return (stage, b + 1) if more else (NEXT[stage], 0)

        ORDER = ["a0", "f0", "a1", "f1", "a2", "f2", "a3", "f3"]

        def stage_wait(eng, stage, b):
            n = ORDER.index(stage)
            if n == 0:
                eng.wait_ge(ld["x"], 16)
            else:
                s, k, done = XADD[ORDER[n - 1]]
                eng.wait_ge(s, (b + 1) * k + done)

        def last_stage_wait(eng, b):
            s, k, done = XADD[ORDER[STAGES - 1]]
            eng.wait_ge(s, (b + 1) * k + done)

        def place(e):
            return (0, AT_LAST) if e == S1 - 1 else (e % 2, 0)

        @block.sync
        def _(sp):
            xt = x.rearrange("(t p) d -> p t d", p=P)
            sp.dma_start(ctxT[:, :, :, :], ctx).then_inc(ld["first"], 16)
            sp.dma_start(aw[:, 0:4, :], attw[:, 0:4, :]).then_inc(ld["first"], 16)
            sp.dma_start(X[:, 0:TILES, :], xt[:, 0:TILES, :]).then_inc(ld["x0"], 16)
            sp.dma_start(col[:, :], cols).then_inc(ld["first"], 16)
            sp.dma_start(kc[:, :], consts).then_inc(ld["const"], 16)
            sp.dma_start(row[:, :], rows.to_broadcast([P, R_COLS])).then_inc(ld["rows"], 16)
            sp.dma_start(aw[:, 4:15, :], attw[:, 4:15, :]).then_inc(ld["att"], 16)
            sp.dma_start(bias32, biases).then_inc(ld["rows"], 16)
            sp.dma_start(X[:, TILES:NTILES, :], xt[:, TILES:NTILES, :]).then_inc(ld["x"], 16)
            sp.dma_start(wr[:, :], router).then_inc(ld["small"], 16)
            for n in range(PIECES):
                if n >= 2:
                    sp.wait_ge(w["raw_used"], n - 1)
                if n == PIECES_L0:
                    sp.dma_start(mw[:, :, :], mlp_w).then_inc(ld["mlp"], 16)
                    sp.dma_start(m1[:, :, :], mask1.rearrange("(t p) k -> p t k", p=P)).then_inc(ld["m1"], 16)
                    sp.dma_start(m2[:, :, :], mask2).then_inc(ld["m2"], 16)
                    sp.dma_start(bd[:, :], bdown).then_inc(ld["bd"], 16)
                sp.dma_start(raw[n % 2][:, :], moe_w[:, n * PIECE:(n + 1) * PIECE]).then_inc(ld_w[n % 2], 16)
            for b in range(BATCHES):
                last_stage_wait(sp, b)
                sp.dma_start(out[b * SEQ:(b + 1) * SEQ, :].rearrange("(t p) d -> p t d", p=P),
                             X[:, b * TILES:(b + 1) * TILES, :]).then_inc(ld["stored"], 16)
            sp.wait_ge(ld["stored"], 16 * BATCHES)

        @block.gpsimd
        def _(pool):
            nc.gpsimd.memset(ones[:, :], 1.0).then_inc(pre["const"], 1)
            nc.gpsimd.memset(ones16[:, :], 1.0).then_inc(pre["const"], 1)
            nc.gpsimd.memset(onesb[:, :], 1.0).then_inc(pre["const"], 1)
            pool.wait_ge(ld["const"], 16)
            nc.gpsimd.tensor_copy(tri16[:, :], kc[:, K_TRI:K_TRI + P]).then_inc(pre["const"], 1)
            nc.gpsimd.memset(before[:, 0, :], 0.0).then_inc(pre["const"], 1)
            nc.gpsimd.memset(scale64[:, :], WSCALE).then_inc(pre["const"], 1)
            pool.wait_ge(pre["const"], 6)
            def keys_apart(l):
                pool.wait_ge(pre["kT"], l + 1)
                for b in range(BATCHES):
                    ins = nc.gpsimd.tensor_tensor(kbd[l][:, b, :, :], bcast(kT[:, l, b, :], 1, HEADS),
                                                  bcast(headm, 2, KEYS), ALU.mult)
                ins.then_inc(pre["kbd"], 1)

            keys_apart(0)
            keys_apart(3)

            def cut(n, at):
                dst = bass.ds((2 * at + n) * PIECE, PIECE)
                factor = scale64[:, :].to_broadcast([P, PIECE])
                pool.wait_ge(ld_w[n], 16 * (at + 1))
                nc.gpsimd.tensor_tensor(scaled[n][:, :], raw[n][:, :], factor, ALU.mult)
                nc.gpsimd.tensor_tensor(WH[:, dst], raw[n][:, :], factor, ALU.mult)
                pool.drain()
                nc.gpsimd.tensor_tensor(WL[:, dst], scaled[n][:, :], WH[:, dst], ALU.subtract)\
                    .then_inc(w["raw_used"], 1)

            with pool.Fori(0, PIECES // 2) as i:
                cut(0, i)
                cut(1, i)
            pool.wait_ge(A[0]["x"], BATCHES)
            keys_apart(2)
            s = F[1]
            with pool.Fori(0, BATCHES) as b:
                for e in range(S1):
                    j, at = place(e)
                    for c in range(2):
                        pool.wait_ge(s["hh"], 2 * (S1 * b + e) + c + 1)
                        nc.gpsimd.tensor_tensor(hl[:, j, at + c, :], big[:, j, at + c, :], hh[:, j, at + c, :],
                                                ALU.subtract).then_inc(s["split"], 1)

        @block.scalar
        def _(act):
            A_ = nc.scalar.activation

            act.wait_ge(ld["first"], 48)
            def key_copy(l):
                act.wait_ge(pre["kT_mm"], l + 1)
                A_(kT[:, l, :, :], pb[l % 2][:, 0:P].rearrange("p (b k) -> p b k", k=KEYS), ACT.Identity,
                   bias=col[:, C_BK[l]:C_BK[l] + 1]).then_inc(pre["kT"], 1)

            def turned(stage, b):
                if stage in (None, "f2"):
                    return
                s, r0 = SET[stage]
                act.wait_ge(s["xT_mm"], (b + r0) + 1)
                A_(xnT[:, :], pb[6][:, :], ACT.Copy).then_inc(s["xT"], 1)
                if stage[0] == "f":
                    A_(xh[:, b, :], pb[6][:, :], ACT.Copy).then_inc(s["xh"], 1)

            def query(stage, b):
                if stage is not None and stage[0] == "a":
                    s, r0 = SET[stage]
                    l = int(stage[1])
                    act.wait_ge(s["q_mm"], (b + r0) + 1)
                    A_(qT[:, :], pb[6][:, :], ACT.Identity, bias=col[:, C_BQ[l]:C_BQ[l] + 1]).then_inc(s["q"], 1)

            def heads(l):
                s, r0 = A[l], ROUND0[l]
                scale = 1.0 if l == 0 else float(np.float32(DEPTH ** -0.5))

                def ex(b, t):
                    act.wait_ge(s["subbed"], TILES * (b + r0) + t + 1)
                    A_(prob[t % 2], sub[t % 2].rearrange("p h k -> p (h k)"), ACT.Exp, scale=scale)\
                        .then_inc(s["exped"], 1)

                def copy(b, t):
                    act.wait_ge(s["pT_mm"], TILES * (b + r0) + t + 1)
                    if t >= 2:
                        act.wait_ge(s["av"], TILES * (b + r0) + t - 1)
                    A_(probT[t % 2].rearrange("p c t -> p (c t)"), pb[2 + t % 2][:, :], ACT.Copy)\
                        .then_inc(s["pT"], 1)

                def body(b, left):
                    after = following(f"a{l}", b, left > 0)
                    copy(b, 0)
                    copy(b, 1)
                    ex(b, 2)
                    turned(*after)
                    ex(b, 3)
                    query(*after)
                    copy(b, 2)
                    copy(b, 3)
                    if left:
                        ex(b + 1, 0)
                    act.wait_ge(s["oT_mm"], (b + r0) + 1)
                    A_(oT[:, :], pb[6 if left else 7][:, :], ACT.Copy).then_inc(s["oT"], 1)
                    if left:
                        ex(b + 1, 1)
                    elif l != 2:
                        route_exp(l, 0)

                if l == 0:
                    key_copy(0)
                    turned("a0", 0)
                    key_copy(1)
                    query("a0", 0)
                    key_copy(2)
                    key_copy(3)
                ex(0, 0)
                ex(0, 1)
                with act.Fori(0, BATCHES - 2) as b:
                    body(b, 2)
                body(BATCHES - 2, 1)
                body(BATCHES - 1, 0)

            def single():
                s = A[1]

                def body(b, left):
                    after = following("a1", b, left > 0)
                    act.wait_ge(s["subbed"], b + 1)
                    A_(s1a[:, :, :], s1b[:, :, :], ACT.Exp).then_inc(s["exped"], 1)
                    turned(*after)
                    act.wait_ge(s["pT_mm"], b + 1)
                    A_(p1T[:, :], pb[1][0:KEYS, :], ACT.Copy).then_inc(s["pT"], 1)
                    query(*after)
                    if not left:
                        route_exp(1, 0)

                with act.Fori(0, BATCHES - 2) as b:
                    body(b, 2)
                body(BATCHES - 2, 1)
                body(BATCHES - 1, 0)

            def route_exp(l, b):
                s = F[l]
                if l == 1:
                    act.wait_ge(s["route_mm"], b + 1)
                    A_(gexp[:, :, 0:E1], pb[6][:, 0:TILES * E1].rearrange("p (t e) -> p t e", e=E1), ACT.Exp,
                       scale=-1.0).then_inc(s["gexp"], 1)
                else:
                    n = E0 if l == 0 else E3
                    act.wait_ge(s["diff"], b + 1)
                    A_(gexp[:, :, 0:n], gate[:, :, 0:n], ACT.Exp).then_inc(s["gexp"], 1)

            def moe0():
                s = F[0]

                def hidden(b, first=False):
                    for c in range(2):
                        act.wait_ge(s["up"], 2 * b + c + 1)
                        A_(big[:, 0, c, :], pb[c][:, :], ACT.Silu, scale=1.0 / WSCALE).then_inc(s["act"], 1)
                    act.wait_ge(s["act"], 2 * b + 2)
                    if not first:
                        act.wait_ge(s["down"], TILES * b)
                    A_(hh[:, 0, 0:2, :], big[:, 0, 0:2, :], ACT.Copy).then_inc(s["hh"], 1)

                def body(b, more):
                    turned(*following("f0", b, more))
                    query(*following("f0", b, more))
                    if more:
                        route_exp(0, b + 1)
                        hidden(b + 1)

                hidden(0, first=True)
                with act.Fori(0, BATCHES - 1) as b:
                    body(b, True)
                body(BATCHES - 1, False)

            def moe1():
                s = F[1]

                def hidden(b, e, j, at=0):
                    g = S1 * b + e
                    for c in range(2):
                        act.wait_ge(s["up"], 4 * g + 2 * c + 1)
                        A_(big[:, j, at + c, :], pb[c][:, :], ACT.Silu, scale=1.0 / WSCALE).then_inc(s["act"], 1)
                    for c in range(2):
                        act.wait_ge(s["prod"], 2 * g + c + 1)
                        A_(hh[:, j, at + c, :], big[:, j, at + c, :], ACT.Copy).then_inc(s["hh"], 1)

                def pair(b, p, at=0):
                    hidden(b, 2 * p + 1, 1)
                    hidden(b, 2 * p + 2, 0, at)

                def body(b, more):
                    with act.Fori(0, 2) as p:
                        pair(b, p)
                    turned(*following("f1", b, more))
                    pair(b, 2)
                    query(*following("f1", b, more))
                    if more:
                        route_exp(1, b + 1)
                    pair(b, 3, AT_LAST)
                    if more:
                        hidden(b + 1, 0, 0)

                hidden(0, 0, 0)
                with act.Fori(0, BATCHES - 1) as b:
                    body(b, True)
                body(BATCHES - 1, False)

            def moe3():
                s = F[3]

                def hidden(b, e, j, high=True):
                    g = E3 * b + e
                    for c in range(4):
                        act.wait_ge(s["up"], 4 * g + c + 1)
                        A_(big[:, j, c, :], pb[c][:, :], ACT.Gelu, scale=1.0 / WSCALE,
                           bias=col[:, bass.ds(C_BUP + 4 * e + c, 1)]).then_inc(s["act"], 1)
                        if high and c >= 2:
                            act.wait_ge(s["act"], 4 * g + 2 * c - 2)
                            A_(hh[:, j, 2 * c - 4:2 * c - 2, :], big[:, j, 2 * c - 4:2 * c - 2, :], ACT.Copy)\
                                .then_inc(s["hh"], 1)

                def copy_cwT(b):
                    act.wait_ge(s["cwT_mm"], b + 1)
                    A_(cwT[:, :], pb[7][0:E3, :], ACT.Copy).then_inc(s["cwT"], 1)

                def pair(b, p):
                    hidden(b, 2 * p + 1, 1)
                    hidden(b, 2 * p + 2, 0)

                def body(b, more):
                    with act.Fori(0, 2) as p:
                        pair(b, p)
                    if more:
                        turned("f3", b + 1)
                    with act.Fori(2, 4) as p:
                        pair(b, p)
                    if more:
                        route_exp(3, b + 1)
                    hidden(b, BY_DVE, 1, high=False)
                    hidden(b, BY_DVE + 1, 0)
                    hidden(b, E3 - 1, 1)
                    if more:
                        copy_cwT(b + 1)
                        hidden(b + 1, 0, 0)

                copy_cwT(0)
                hidden(0, 0, 0)
                with act.Fori(0, BATCHES - 1) as b:
                    body(b, True)
                body(BATCHES - 1, False)

            def mlp():
                s = M

                def prep(b):
                    act.wait_ge(s["xT_mm"], b + 1)
                    A_(xnT[:, :], pb[6][:, :], ACT.Identity, scale=col[:, C_G1:C_G1 + 1],
                       bias=col[:, C_B1:C_B1 + 1]).then_inc(s["xT"], 1)

                def gelu(b, t, first=False):
                    act.wait_ge(s["up"], TILES * b + t + 1)
                    if not first:
                        act.wait_ge(s["n"], TILES * (b - 1) + t + 1)
                    A_(big[:, 1, t, :], pb[t][:, :], ACT.Gelu).then_inc(s["gelu"], 1)

                def affine(b, t):
                    act.wait_ge(s["nT_mm"], TILES * b + t + 1)
                    if t >= 2:
                        act.wait_ge(s["down"], TILES * b + t - 1)
                    for c in range(4):
                        ins = A_(hl_f[t % 2][:, c, :], pb[4 + t % 2][:, c * P:(c + 1) * P], ACT.Identity,
                                 scale=col[:, C_G2 + c:C_G2 + c + 1], bias=col[:, C_B2 + c:C_B2 + c + 1])
                    ins.then_inc(s["nT"], 1)

                def body(b, left):
                    if left == 0:
                        query("a3", 0)
                    if left:
                        for t in range(TILES):
                            gelu(b + 1, t)
                    for t in range(TILES):
                        affine(b, t)
                    if left > 1:
                        prep(b + 2)
                    elif left:
                        turned("a3", 0)

                prep(0)
                for t in range(TILES):
                    gelu(0, t, first=True)
                prep(1)
                with act.Fori(0, BATCHES - 2) as b:
                    body(b, 2)
                body(BATCHES - 2, 1)
                body(BATCHES - 1, 0)

            for n, stage in enumerate((lambda: heads(0), moe0, single, moe1, lambda: heads(2), mlp,
                                       lambda: heads(3), moe3)):
                if n < STAGES:
                    stage()

        @block.tensor
        def _(pe):
            mm = nc.tensor.matmul

            def pairs(dst, stat, mov, start, stop):
                (sh, sl), (mh, ml) = stat, mov
                mm(dst, sh, mh, start=start, stop=False)
                mm(dst, sl, mh, start=False, stop=False)
                return mm(dst, sh, ml, start=False, stop=stop)

            pe.wait_ge(ld["first"], 48)

            def keys(l):
                if l == 1:
                    pe.wait_ge(ld["att"], 16)
                if l >= 2:
                    pe.wait_ge(pre["kT"], l - 1)
                mm(pb[l % 2][:, 0:P], aw[:, ATT_AT[l] + K, :], ctxT[:, :, 0, :], start=True, stop=True)\
                    .then_inc(pre["kT_mm"], 1)

            def vals(l):
                if l >= 2:
                    pe.wait_ge(pre["v"], l - 1)
                for b in range(BATCHES):
                    if l == 1:
                        ins = mm(pb[2 + l % 2][0:KEYS, b * P:(b + 1) * P], ctxT[:, b, 0, :],
                                 aw[:, ATT_AT[l] + V, :], start=True, stop=True)
                    else:
                        ins = mm(pb[2 + l % 2][:, b * P:(b + 1) * P],
                                 ctxT[:, b, :, :].rearrange("p r k -> p (r k)"),
                                 aw[:, ATT_AT[l] + V, :], start=True, stop=True)
                ins.then_inc(pre["v_mm"], 1)

            def transposes(bank, src, s_ready, s_done, b):
                pe.wait_ge(s_ready, b + 1)
                for t in range(TILES):
                    ins = nc.tensor.transpose(pb[bank][:, t * P:(t + 1) * P], src[:, t, :], ident)
                ins.then_inc(s_done, 1)

            def turn_normal(stage, b):
                if stage in (None, "f2"):
                    return
                s, r0 = SET[stage]
                transposes(6, xn, s["xn"], s["xT_mm"], b + r0)

            def first_product(stage, b):
                if stage in (None, "f2"):
                    return
                s, r0 = SET[stage]
                l = int(stage[1])
                pe.wait_ge(s["xT"], (b + r0) + 1)
                if stage[0] == "a":
                    mm(pb[6][:, :], aw[:, ATT_AT[l] + Q, :], xnT[:, :], start=True, stop=True).then_inc(s["q_mm"], 1)
                    return
                n, at = ((E0, 0), (E1, E0), None, (E3, E0 + E1))[l]
                if l == 0:
                    pe.wait_ge(ld["small"], 16)
                pe.wait_ge(s["xh"], b + 1)
                for t in range(TILES):
                    ins = mm(pb[6][:, t * n:(t + 1) * n], xnT[:, t * P:(t + 1) * P], wr[:, at:at + n],
                             start=True, stop=True)
                ins.then_inc(s["route_mm"], 1)

            def heads(l):
                s, r0 = A[l], ROUND0[l]

                def scores(b, t, first=None):
                    if t == 0:
                        pe.wait_ge(s["q"], (b + r0) + 1)
                        if first:
                            pe.wait_ge(pre["kbd"], {0: 1, 3: 2, 2: 3}[l])
                    if t >= 2:
                        pe.wait_ge(s["subbed"], TILES * (b + r0) + t - 1)
                    ins = mm(pb[t % 2][:, :], qT[:, t * P:(t + 1) * P],
                             kbd[l][:, b, :, :].rearrange("p h k -> p (h k)"), start=True, stop=l != 2)
                    if l == 2:
                        ins = mm(pb[t % 2][:, :], onesb[:, :], m2b[:, b, :, :].rearrange("p h k -> p (h k)"),
                                 start=False, stop=True)
                    ins.then_inc(s["scores"], 1)

                def turn(b, t):
                    pe.wait_ge(s["exped"], TILES * (b + r0) + t + 1)
                    for c in range(QUADS):
                        ins = nc.tensor.transpose(pb[2 + t % 2][:, c * P:(c + 1) * P],
                                                  prob[t % 2][:, c * P:(c + 1) * P], ident)
                    ins.then_inc(s["pT_mm"], 1)

                def values(b, t):
                    pe.wait_ge(s["pT"], TILES * (b + r0) + t + 1)
                    if t >= 2:
                        pe.wait_ge(s["normed"], TILES * (b + r0) + t - 1)
                    for c in range(QUADS):
                        ins = mm(pb[4 + t % 2][:, c * VCOLS:(c + 1) * VCOLS], probT[t % 2][:, c, :],
                                 vbd[l][:, b, c, :], start=True, stop=True)
                    ins.then_inc(s["av"], 1)

                def output_bias():
                    for i in range(2):
                        mm(pb[7][:, :], ones16[0:1, :], bcast(bias16[0:1, i, B_O[l]:B_O[l] + P], 1, TILES),
                           start=i == 0, stop=False)

                def project(b):
                    pe.wait_ge(s["oT"], (b + r0) + 1)
                    for t in range(TILES):
                        ins = mm(pb[7][:, t * P:(t + 1) * P], oT[:, t * P:(t + 1) * P], aw[:, ATT_AT[l] + O, :],
                                 start=False, stop=t == TILES - 1)
                    ins.then_inc(s["proj"], 1)

                def turn_values(b, bank):
                    pe.wait_ge(s["normed"], TILES * (b + r0) + TILES)
                    for t in range(TILES):
                        ins = nc.tensor.transpose(pb[bank][:, t * P:(t + 1) * P], o[:, t, :], ident)
                    ins.then_inc(s["oT_mm"], 1)

                def scores_next(b, t):
                    pe.wait_ge(s["subbed"], TILES * (b + r0) + t - 1)
                    scores(b, t)

                def body(b, left):
                    after = following(f"a{l}", b, left > 0)
                    scores(b, 2)
                    turn(b, 1)
                    scores(b, 3)
                    turn_normal(*after)
                    values(b, 0)
                    values(b, 1)
                    first_product(*after)
                    turn(b, 2)
                    turn(b, 3)
                    if left:
                        scores_next(b + 1, 0)
                    values(b, 2)
                    values(b, 3)
                    if left:
                        scores_next(b + 1, 1)
                    if left:
                        turn_values(b, 6)
                        output_bias()
                        turn(b + 1, 0)
                    else:
                        turn_values(b, 7)
                        pe.wait_ge(s["oT"], (b + r0) + 1)
                        output_bias()
                    project(b)

                if l == 0:
                    keys(0)
                    vals(0)
                    pe.wait_ge(ld["const"], 16)
                    turn_normal("a0", 0)
                    keys(1)
                    first_product("a0", 0)
                    vals(1)
                    keys(2)
                    vals(2)
                    keys(3)
                    vals(3)
                    pe.wait_ge(pre["kT"], 4)
                if l == 2:
                    pe.wait_ge(pre["spread"], 2)
                scores(0, 0, True)
                scores(0, 1)
                if l == 0:
                    pe.wait_ge(pre["vbd"], 1)
                    pe.wait_ge(pre["bias"], 2)
                    pe.wait_ge(pre["const"], 6)
                turn(0, 0)
                with pe.Fori(0, BATCHES - 2) as b:
                    body(b, 2)
                body(BATCHES - 2, 1)
                body(BATCHES - 1, 0)

            def single():
                s = A[1]

                def body(b, more):
                    pe.wait_ge(s["q"], b + 1)
                    for t in range(TILES):
                        ins = mm(pb[0][:, t * KEYS:(t + 1) * KEYS], qT[:, t * P:(t + 1) * P],
                                 kT[:, 1, b, :], start=True, stop=True)
                    ins.then_inc(s["scores"], 1)
                    turn_normal(*following("a1", b, more))
                    pe.wait_ge(s["exped"], b + 1)
                    for t in range(TILES):
                        ins = nc.tensor.transpose(pb[1][0:KEYS, t * P:(t + 1) * P], s1a[:, t, :], ident)
                    ins.then_inc(s["pT_mm"], 1)
                    first_product(*following("a1", b, more))
                    pe.wait_ge(s["pT"], b + 1)
                    for t in range(TILES):
                        ins = mm(pb[4][:, t * P:(t + 1) * P], p1T[:, t * P:(t + 1) * P], v1[:, b, :],
                                 start=True, stop=True)
                    ins.then_inc(s["av"], 1)

                with pe.Fori(0, BATCHES - 1) as b:
                    body(b, True)
                body(BATCHES - 1, False)

            def moe0():
                s = F[0]
                gate_w = [(WH[:, W_GATE + c * P:W_GATE + (c + 1) * P], WL[:, W_GATE + c * P:W_GATE + (c + 1) * P])
                          for c in range(2)]

                def count(b):
                    pe.wait_ge(s["masks"], b + 1)
                    for t in range(TILES):
                        dst = pb[7][:, t * E0:(t + 1) * E0]
                        mm(dst, tri16[:, :], mask16[:, t, :], start=True, stop=False)
                        ins = mm(dst, ones16[:, :], before[:, t, :], start=False, stop=True)
                    ins.then_inc(s["count_mm"], 1)

                def up(b):
                    pe.wait_ge(s["xl"], b + 1)
                    for c in range(2):
                        pairs(pb[c][:, :], gate_w[c], (xh[:, b, :], xl[:, b, :]), True, True).then_inc(s["up"], 1)

                def down(b, t):
                    if t == 0:
                        pe.wait_ge(s["split"], b + 1)
                    if t == 1:
                        pe.wait_ge(s["cw"], b + 1)
                    if t >= 2:
                        pe.wait_ge(s["acc"], E0 * (TILES * b + t - 1))
                    for n in range(2):
                        for c in range(2):
                            at = W_DOWN0 + c * E0 * P + n * 512
                            tok = slice(t * P, (t + 1) * P)
                            ins = pairs(pb[2 + 2 * (t % 2) + n][:, :], (hh[:, 0, c, tok], hl[:, 0, c, tok]),
                                        (WH[:, at:at + 512], WL[:, at:at + 512]), c == 0, c == 1)
                    ins.then_inc(s["down"], 1)

                def body(b, more):
                    turn_normal(*following("f0", b, more))
                    down(b, 0)
                    down(b, 1)
                    first_product(*following("f0", b, more))
                    if more:
                        up(b + 1)
                    down(b, 2)
                    down(b, 3)
                    if more:
                        count(b + 1)

                pe.wait_ge(w["raw_used"], PIECES_L0)
                up(0)
                pe.wait_ge(A[0]["x"], BATCHES)
                count(0)
                with pe.Fori(0, BATCHES - 1) as b:
                    body(b, True)
                body(BATCHES - 1, False)

            def wpair(at, n=P):
                return WH[:, bass.ds(at, n)], WL[:, bass.ds(at, n)]

            def abs_totals():
                pe.wait_ge(pre["abs"], 1)
                mm(pb[7][:, 64:66], ones[:, :], qsum[:, :], start=True, stop=True).then_inc(pre["abs_mm"], 1)

            def moe1():
                s = F[1]

                def up(b, e, guard=True):
                    g = S1 * b + e
                    for c in range(2):
                        for i, base in enumerate((W_1, W_3)):
                            if guard and i:
                                pe.wait_ge(s["prod"], 2 * g + c - 1)
                            elif guard:
                                pe.wait_ge(s["act"], 2 * g + c - 1)
                            pairs(pb[2 * i + c][:, :], wpair(base + e * 256 + c * P),
                                  (xh[:, b, :], xl[:, b, :]), True, True).then_inc(s["up"], 1)

                def down(b, e, j, at=0, bank=None):
                    bank = 4 + j if bank is None else bank
                    pe.wait_ge(s["split"], 2 * (S1 * b + e) + 2)
                    for t in range(TILES):
                        tok = slice(t * P, (t + 1) * P)
                        for c in range(2):
                            ins = pairs(pb[bank][:, tok], (hh[:, j, at + c, tok], hl[:, j, at + c, tok]),
                                        wpair(W_2 + e * 256 + c * P), c == 0, c == 1)
                    ins.then_inc(s["down"], 1)

                def pair(b, p):
                    up(b, 2 * p + 1)
                    down(b, 2 * p, 0)
                    up(b, 2 * p + 2)
                    down(b, 2 * p + 1, 1)

                def body(b, more):
                    with pe.Fori(0, 2) as p:
                        pair(b, p)
                    up(b, 5)
                    turn_normal(*following("f1", b, more))
                    down(b, 4, 0)
                    up(b, 6)
                    down(b, 5, 1)
                    if not more:
                        abs_totals()
                    first_product(*following("f1", b, more))
                    pair(b, 3)
                    if more:
                        pe.wait_ge(s["xl"], b + 2)
                        up(b + 1, 0)
                    down(b, S1 - 1, 0, AT_LAST, BANK_LAST)

                pe.wait_ge(w["raw_used"], PIECES_L1)
                pe.wait_ge(s["xl"], 1)
                up(0, 0, guard=False)
                with pe.Fori(0, BATCHES - 1) as b:
                    body(b, True)
                body(BATCHES - 1, False)

            def moe3():
                s = F[3]

                def up(b, e, guard=True):
                    g = E3 * b + e
                    for c in range(4):
                        if guard:
                            pe.wait_ge(s["act"], 4 * g - 3 + c)
                        pairs(pb[c][:, :], wpair(W_UP + e * 512 + c * P),
                              (xh[:, b, :], xl[:, b, :]), True, True).then_inc(s["up"], 1)

                def down(b, e, j):
                    pe.wait_ge(s["split"], E3 * b + e + 1)
                    for t in range(TILES):
                        tok = slice(t * P, (t + 1) * P)
                        for c in range(4):
                            ins = pairs(pb[4 + j][:, tok], (hh[:, j, c, tok], hl[:, j, c, tok]),
                                        wpair(W_DOWN3 + e * 512 + c * P), c == 0, c == 3)
                    ins.then_inc(s["down"], 1)

                def turn_weights(b):
                    pe.wait_ge(s["cw"], b + 1)
                    for t in range(TILES):
                        ins = nc.tensor.transpose(pb[7][0:E3, t * P:(t + 1) * P], gate[:, t, :], ident)
                    ins.then_inc(s["cwT_mm"], 1)

                def bias(b):
                    pe.wait_ge(s["cwT"], b + 1)
                    for t in range(TILES):
                        ins = mm(pb[6][:, t * P:(t + 1) * P], cwT[:, t * P:(t + 1) * P], bd[:, :],
                                 start=True, stop=True)
                    ins.then_inc(s["bias_mm"], 1)

                def pair(b, p):
                    up(b, 2 * p + 1)
                    down(b, 2 * p, 0)
                    up(b, 2 * p + 2)
                    down(b, 2 * p + 1, 1)

                def body(b, more):
                    with pe.Fori(0, 2) as p:
                        pair(b, p)
                    if more:
                        turn_normal("f3", b + 1)
                    pair(b, 2)
                    if more:
                        first_product("f3", b + 1)
                    with pe.Fori(3, 5) as p:
                        pair(b, p)
                    up(b, E3 - 1)
                    if more:
                        turn_weights(b + 1)
                    down(b, E3 - 2, 0)
                    if more:
                        bias(b + 1)
                        up(b + 1, 0)
                    down(b, E3 - 1, 1)

                pe.wait_ge(w["raw_used"], PIECES)
                pe.wait_ge(pre["spread"], 2)
                pe.wait_ge(A[3]["x"], BATCHES + ROUND0[3])
                turn_weights(0)
                up(0, 0, guard=False)
                bias(0)
                with pe.Fori(0, BATCHES - 1) as b:
                    body(b, True)
                body(BATCHES - 1, False)

            def mlp():
                s = M

                def up(b, t):
                    if t == 0:
                        pe.wait_ge(s["xT"], b + 1)
                    for i in range(2):
                        mm(pb[t][:, :], ones16[0:1, :], bias16[0:1, i, B_1:B_1 + 512], start=i == 0, stop=False)
                    mm(pb[t][:, :], xnT[:, t * P:(t + 1) * P], wq[:, 0, :], start=False, stop=True)\
                        .then_inc(s["up"], 1)

                def turn(b, t):
                    pe.wait_ge(s["n"], TILES * b + t + 1)
                    if t >= 2:
                        pe.wait_ge(s["nT"], TILES * b + t - 1)
                    for c in range(4):
                        ins = nc.tensor.transpose(pb[4 + t % 2][:, c * P:(c + 1) * P],
                                                  big[:, 0, t, c * P:(c + 1) * P], ident)
                    ins.then_inc(s["nT_mm"], 1)

                def down(b, t):
                    dst = pb[7][:, t * P:(t + 1) * P]
                    for i in range(2):
                        mm(dst, ones16[0:1, :], bias16[0:1, i, B_2:B_2 + P], start=i == 0, stop=False)
                    pe.wait_ge(s["nT"], TILES * b + t + 1)
                    for c in range(4):
                        ins = mm(dst, hl_f[t % 2][:, c, :], wq[:, 1, c * P:(c + 1) * P],
                                 start=False, stop=c == 3)
                    ins.then_inc(s["down"], 1)

                def body(b, left):
                    if left == 0:
                        first_product("a3", 0)
                    if left:
                        for t in range(TILES):
                            up(b + 1, t)
                    for t in range(TILES):
                        turn(b, t)
                        if t:
                            down(b, t - 1)
                    down(b, TILES - 1)
                    if left > 1:
                        transposes(6, xn, s["xn2"], s["xT_mm"], b + 2)
                    elif left:
                        turn_normal("a3", 0)

                pe.wait_ge(pre["quant"], 2)
                transposes(6, xn, s["xn2"], s["xT_mm"], 0)
                for t in range(TILES):
                    up(0, t)
                transposes(6, xn, s["xn2"], s["xT_mm"], 1)
                with pe.Fori(0, BATCHES - 2) as b:
                    body(b, 2)
                body(BATCHES - 2, 1)
                body(BATCHES - 1, 0)

            for n, stage in enumerate((lambda: heads(0), moe0, single, moe1, lambda: heads(2), mlp,
                                       lambda: heads(3), moe3)):
                if n < STAGES:
                    stage()

        @block.vector
        def _(dve):
            ts_ = nc.vector.tensor_scalar
            tt = nc.vector.tensor_tensor
            stt = nc.vector.scalar_tensor_tensor

            def context_values(l):
                dve.wait_ge(pre["v_mm"], l + 1)
                src = pb[2 + l % 2]
                bv = slice(R_BV[l], R_BV[l] + P)
                if l == 1:
                    tt(v1[:, :, :], src[0:KEYS, :].rearrange("p (b d) -> p b d", d=P),
                       bcast(row[0:KEYS, bv], 1, BATCHES), ALU.add).then_inc(pre["v"], 1)
                    return
                if l:
                    dve.wait_ge(pre["vbd"], l - 1)
                tt(vrep[:, :, :], src[:, :].rearrange("p (b d) -> p b d", d=P), bcast(row[:, bv], 1, BATCHES),
                   ALU.add).then_inc(pre["v"], 1)
                dve.wait_ge(pre["v"], l + 1)
                for b in range(BATCHES):
                    tt(vbd[l][:, b, :, 0:32].rearrange("p c (g d) -> p c g d", d=DEPTH),
                       vrep[:, b, :].rearrange("p (c g d) -> p c g d", g=4, d=DEPTH),
                       bcast(bcast(quadm, 2, DEPTH), 1, QUADS), ALU.mult)
                nc.vector.tensor_copy(vbd[l][:, :, :, 32:36].rearrange("p b c g -> p (b c) g"),
                                      bcast(quadm, 1, BATCHES * QUADS)).then_inc(pre["vbd"], 1)

            def bias_pair():
                nc.vector.tensor_copy(bias16[:, 0, :], bias32).then_inc(pre["bias"], 1)
                dve.wait_ge(pre["bias"], 1)
                tt(bias16[:, 1, :], bias32, bias16[:, 0, :], ALU.subtract).then_inc(pre["bias"], 1)

            def ln_step(k, base, ln, src, dst, done, n=P, small=norm_x):
                stats, mean, var, rstd, tmp4 = (small[i] for i in ("stats", "mean", "var", "rstd", "tmp"))
                me, se, mo, so = (stats[:, :, i] for i in (1, 2, 4, 5))
                if k > 1:
                    dve.wait_ge(ln, base + k)
                root = float(np.sqrt(n)) if k in (12, 14) else 1.0
                if k < 2:
                    nc.vector.bn_stats(stats[:, 2 * k, :], src(2 * k))
                    ins = nc.vector.bn_stats(stats[:, 2 * k + 1, :], src(2 * k + 1))
                elif k == 2:
                    tt(tmp4[:, :], me, mo, ALU.subtract)
                    tt(var[:, :], se, so, ALU.add)
                    ins = tt(mean[:, :], me, mo, ALU.add)
                elif k == 3:
                    ts_(mean[:, :], mean[:, :], 0.5, None, ALU.mult)
                    ins = stt(tmp4[:, :], tmp4[:, :], n / 4.0, tmp4[:, :], ALU.mult, ALU.mult)
                elif k == 4:
                    ins = stt(var[:, :], tmp4[:, :], n * EPS, var[:, :], ALU.add, ALU.add)
                elif k == 5:
                    ins = ts_(rstd[:, :].bitcast(I32), var[:, :].bitcast(I32), -0.5, MAGIC, ALU.mult, ALU.add)
                elif k in (6, 9, 12):
                    ins = stt(tmp4[:, :], rstd[:, :], -0.5 * root, rstd[:, :], ALU.mult, ALU.mult)
                elif k in (7, 10, 13):
                    ins = tt(tmp4[:, :], tmp4[:, :], var[:, :], ALU.mult)
                elif k in (8, 11, 14):
                    ins = stt(rstd[:, :], tmp4[:, :], 1.5 * root, rstd[:, :], ALU.add, ALU.mult)
                else:
                    for t in (2 * k - 30, 2 * k - 29):
                        ins = ts_(dst(t), src(t), mean[:, t:t + 1], rstd[:, t:t + 1], ALU.subtract, ALU.mult)
                ins.then_inc(ln if k < 16 else done, 1)

            def prep(stage, b, *steps):
                if stage is None:
                    return
                s, r0 = SET[stage]
                for k in steps:
                    if k == 0:
                        stage_wait(dve, stage, b)
                    ln_step(k, LN_COUNT * (b + r0), s["ln"], lambda t: X[:, TILES * b + t, :],
                            lambda t: xn[:, t, :], s["xn"])

            def ahead(stage):
                low_part(int(stage[1]), 0)
                steps, route = {"f0": (13, route0), "f1": (12, route1), "f3": (14, route3)}[stage]
                for k in range(steps):
                    route(0, k)

            def norm_free(stage, b):
                s, r0 = SET[stage]
                dve.wait_ge(s["xT_mm"], (b + r0) + 1)

            def heads(l):
                s, r0 = A[l], ROUND0[l]

                def softmax(b, t, between=lambda: None, first=False):
                    dve.wait_ge(s["scores"], TILES * (b + r0) + t + 1)
                    src = pb[t % 2][:, :].rearrange("p (h k) -> p h k", k=KEYS)
                    nc.vector.reduce_max(mx[:, t % 2, :], src, AX).then_inc(s["dve"], 1)
                    between()
                    dve.wait_ge(s["dve"], TILES * (b + r0) + t + 1)
                    if not first:
                        dve.wait_ge(s["exped"], TILES * (b + r0) + t - 1)
                    tt(sub[t % 2], src, bcast(mx[:, t % 2, :], 2, KEYS), ALU.subtract).then_inc(s["subbed"], 1)

                def norm(b, t, between=lambda: None):
                    dve.wait_ge(s["av"], TILES * (b + r0) + t + 1)
                    src = pb[4 + t % 2][:, 0:QUADS * VCOLS].rearrange("p (c n) -> p c n", n=VCOLS)
                    if t:
                        dve.wait_ge(s["normed"], TILES * (b + r0) + t)
                    nc.vector.reciprocal(rinv[:, :, :], src[:, :, 32:36]).then_inc(s["dve2"], 1)
                    between()
                    dve.wait_ge(s["dve2"], TILES * (b + r0) + t + 1)
                    tt(o[:, t, :].rearrange("p (c g d) -> p c g d", g=4, d=DEPTH),
                       src[:, :, 0:32].rearrange("p c (g d) -> p c g d", d=DEPTH),
                       bcast(rinv[:, :, :], 3, DEPTH), ALU.mult).then_inc(s["normed"], 1)

                def body(b, left):
                    def ln(*steps):
                        if left > 1:
                            prep(f"a{l}", b + 2, *steps)
                        elif left:
                            prep(NEXT[f"a{l}"], 0, *steps)
                        elif l == 2:
                            for step in steps:
                                prep2(0, 17 + step)
                        elif l == 0:
                            prep("f0", 1, *steps)

                    softmax(b, 2, lambda: ln(0))
                    ln(1)
                    softmax(b, 3, lambda: ln(2))
                    ln(3)
                    norm(b, 0, lambda: ln(4))
                    ln(5)
                    norm(b, 1, lambda: ln(6))
                    ln(7, 8, 9, 10)
                    if left:
                        softmax(b + 1, 0, lambda: ln(11))
                        ln(12)
                        norm(b, 2, lambda: ln(13))
                        norm(b, 3, lambda: ln(14))
                        norm_free(f"a{l}", b + 1)
                        softmax(b + 1, 1, lambda: ln(15))
                        ln(16)
                    else:
                        norm(b, 2, lambda: ln(11))
                        norm(b, 3, lambda: ln(12))
                        ln(13, 14)
                        if l == 0:
                            norm_free("f0", 0)
                        ln(15, 16)
                        if l != 2:
                            ahead(NEXT[f"a{l}"])
                    dve.wait_ge(s["proj"], (b + r0) + 1)
                    tt(X[:, bass.ds(TILES * b, TILES), :], pb[7][:, :].rearrange("p (t d) -> p t d", d=P),
                       X[:, bass.ds(TILES * b, TILES), :], ALU.add).then_inc(s["x"], 1)

                if l == 0:
                    dve.wait_ge(ld["x0"], 16)
                    for k in range(17):
                        ln_step(k, 0, s["ln"], lambda t: X[:, t, :], lambda t: xn[:, t, :], s["xn"])
                    dve.wait_ge(ld["rows"], 32)
                    dve.wait_ge(ld["const"], 16)
                    context_values(0)
                    prep("a0", 1, *range(8))
                    for layer in range(1, 4):
                        context_values(layer)
                    bias_pair()
                    prep("a0", 1, *range(8, 15))
                softmax(0, 0, first=True)
                if l == 0:
                    norm_free("a0", 0)
                    prep("a0", 1, 15)
                softmax(0, 1, first=True)
                if l == 0:
                    prep("a0", 1, 16)
                with dve.Fori(0, BATCHES - 2) as b:
                    body(b, 2)
                body(BATCHES - 2, 1)
                body(BATCHES - 1, 0)

            def single():
                s = A[1]
                isq = float(np.float32(1.0) / np.sqrt(np.float32(P)))

                def body(b, left):
                    def ln(*steps):
                        if left > 1:
                            prep("a1", b + 2, *steps)
                        elif left:
                            prep("f1", 0, *steps)

                    ch = Chain(dve, s["dve"], 7, b)
                    ch.then(ts_(allow[:, :, :], m1[:, bass.ds(TILES * b, TILES), :], 0.0, None, ALU.not_equal))
                    ch.then(ts_(penal[:, :, :], allow[:, :, :], 1e10, -1e10, ALU.mult, ALU.add))
                    dve.wait_ge(s["scores"], b + 1)
                    ch.then(stt(s1b[:, :, :], pb[0][:, 0:P].rearrange("p (t k) -> p t k", k=KEYS), isq,
                                allow[:, :, :], ALU.mult, ALU.mult))
                    ch.then(tt(allow[:, :, :], s1b[:, :, :], penal[:, :, :], ALU.add))
                    ch.then(nc.vector.reduce_max(gmax[:, :], allow[:, :, :], AX))
                    tt(s1b[:, :, :], allow[:, :, :], bcast(gmax[:, :], 2, KEYS), ALU.subtract)\
                        .then_inc(s["subbed"], 1)
                    ln(*range(7))
                    dve.wait_ge(s["exped"], b + 1)
                    ch.then(nc.vector.reduce_sum(gsum[:, :], s1a[:, :, :], AX), lambda: ln(7))
                    ch.then(nc.vector.reciprocal(inv1[:, :], gsum[:, :]), lambda: ln(8))
                    ch.done()
                    ln(*range(9, 15))
                    if left:
                        norm_free("a1", b + 1)
                    ln(15, 16)
                    if not left:
                        ahead("f1")
                    dve.wait_ge(s["av"], b + 1)
                    for t in range(TILES):
                        ins = stt(X[:, TILES * b + t, :], pb[4][:, t * P:(t + 1) * P], inv1[:, t:t + 1],
                                  X[:, TILES * b + t, :], ALU.mult, ALU.add)
                    ins.then_inc(s["x"], 1)

                dve.wait_ge(ld["m1"], 16)
                with dve.Fori(0, BATCHES - 2) as b:
                    body(b, 2)
                body(BATCHES - 2, 1)
                body(BATCHES - 1, 0)

            def low_part(l, b):
                s = F[l]
                dve.wait_ge(s["xT"], b + 1)
                dve.wait_ge(s["xh"], b + 1)
                tt(xl[:, b, :], xnT[:, :], xh[:, b, :], ALU.subtract).then_inc(s["xl"], 1)

            def choose(k, score, n):
                it = bcast(iota[:, 0:n], 1, TILES)
                if k < 2:
                    dve.drain()
                    for t in range(TILES):
                        ins = nc.vector.max(top[:, t, :], score[:, t, 0:n]) if k == 0 else \
                            nc.vector.max_index(topi[:, t, :], top[:, t, :], score[:, t, 0:n])
                elif k == 2:
                    ins = tt(pick[:, :, 0:n], it, bcast(topi[:, :, 0], 2, n), ALU.is_equal)
                elif k in (3, 5):
                    ins = tt(gtmp[:, :, 0:n], it, bcast(topi[:, :, (k - 1) // 2], 2, n), ALU.is_equal)
                else:
                    ins = tt(pick[:, :, 0:n], pick[:, :, 0:n], gtmp[:, :, 0:n], ALU.add)
                return ins

            def add_expert(s, b, e, n, bank, weights, aside, slot):
                dve.wait_ge(s["down"], n * b + e + 1)
                if e:
                    dve.wait_ge(s["acc"], n * b + e)
                for t in range(TILES):
                    ins = stt(acc[:, t, :], pb[bank][:, t * P:(t + 1) * P], weights(t), acc[:, t, :],
                              ALU.mult, ALU.add)
                    if t == TILES - 1:
                        ins.then_inc(s["acc"], 1)
                    aside(slot + t)

            def add_batch(s, b, count):
                dve.wait_ge(s["acc"], count * (b + 1))
                xs = X[:, bass.ds(TILES * b, TILES), :]
                tt(xs, acc[:, :, :], xs, ALU.add).then_inc(s["x"], 1)

            logits0 = pb[6][:, 0:TILES * E0].rearrange("p (t e) -> p t e", e=E0)
            counts0 = pb[7][:, 0:TILES * E0].rearrange("p (t e) -> p t e", e=E0)
            g0, e0_, pk0, tm0 = (a[:, :, 0:E0] for a in (gate, gexp, pick, gtmp))
            STEPS0 = 18

            def route0(b, k):
                if k == 0:
                    dve.wait_ge(F[0]["route_mm"], b + 1)
                    nc.vector.reduce_max(gmax[:, :], logits0, AX).then_inc(F[0]["dve"], 1)
                elif k == 1:
                    dve.wait_ge(F[0]["dve"], STEPS0 * b + 1)
                    tt(g0, logits0, bcast(gmax[:, :], 2, E0), ALU.subtract).then_inc(F[0]["diff"], 1)
                elif k == 2:
                    dve.wait_ge(F[0]["gexp"], b + 1)
                    nc.vector.reduce_sum(gsum[:, :], e0_, AX).then_inc(F[0]["dve"], 1)
                elif k < 8:
                    if k > 4:
                        dve.wait_ge(F[0]["dve"], STEPS0 * b + k - 1)
                    choose(k - 3, gexp, E0).then_inc(F[0]["dve"], 1)
                elif k == 8:
                    dve.wait_ge(F[0]["dve"], STEPS0 * b + k - 1)
                    nc.vector.tensor_copy(mask16[:, :, :], pk0).then_inc(F[0]["dve"], 1)
                elif k < 13:
                    t = k - 9
                    dve.wait_ge(F[0]["dve"], STEPS0 * b + k - 1)
                    tt(before[:, t + 1, :], before[:, t, :], mask16[:, t, :], ALU.add)\
                        .then_inc(F[0]["masks" if k == 12 else "dve"], 1)
                elif k == 13:
                    dve.wait_ge(F[0]["count_mm"], b + 1)
                    ts_(tm0, counts0, float(CAPACITY), None, ALU.is_le)
                    nc.vector.tensor_copy(before[:, 0, :], before[:, TILES, :]).then_inc(F[0]["dve"], 1)
                else:
                    dve.wait_ge(F[0]["dve"], STEPS0 * b + k - 2)
                    if k == 14:
                        ins = tt(pk0, pk0, tm0, ALU.mult)
                    elif k == 15:
                        ins = tt(g0, e0_, pk0, ALU.mult)
                    elif k == 16:
                        ins = nc.vector.reduce_sum(gmax[:, :], g0, AX)
                    elif k == 17:
                        ins = stt(gden[:, :], gsum[:, :], 1e-6, gmax[:, :], ALU.mult, ALU.add)
                    elif k == 18:
                        ins = ts_(gsum[:, :], gden[:, :], WSCALE, None, ALU.mult)
                    elif k == 19:
                        ins = nc.vector.reciprocal(gden[:, :], gsum[:, :])
                    else:
                        ins = tt(cw[:, :, 0:E0], g0, bcast(gden[:, :], 2, E0), ALU.mult)
                    ins.then_inc(F[0]["cw" if k == 20 else "dve"], 1)

            e1_, g1, tm1 = gexp[:, :, 0:E1], gate[:, :, 0:E1], gtmp[:, :, 0:E1]
            STEPS1 = 11

            def route1(b, k):
                if k == 0:
                    dve.wait_ge(F[1]["gexp"], b + 1)
                    ins = ts_(tm1, e1_, 1.0, None, ALU.add)
                else:
                    if k not in (2, 3):
                        dve.wait_ge(F[1]["dve"], STEPS1 * b + k)
                    if k == 1:
                        ins = nc.vector.reciprocal(g1, tm1)
                    elif k < 7:
                        ins = choose(k - 2, gate, E1)
                    elif k == 7:
                        ins = tt(tm1, g1, pick[:, :, 0:E1], ALU.mult)
                    elif k == 8:
                        ins = nc.vector.reduce_sum(gsum[:, :], tm1, AX)
                    elif k == 9:
                        ins = ts_(gmax[:, :], gsum[:, :], 3.0 * WSCALE, None, ALU.mult)
                    elif k == 10:
                        ins = nc.vector.reciprocal(gden[:, :], gmax[:, :])
                    else:
                        ins = tt(g1, tm1, bcast(gden[:, :], 2, E1), ALU.mult)
                ins.then_inc(F[1]["dve" if k < 11 else "cw"], 1)

            STEPS3 = 12

            def route3(b, k):
                if k == 0:
                    dve.wait_ge(F[3]["route_mm"], b + 1)
                    nc.vector.tensor_copy(logit3[:, :, :], pb[6][:, 0:TILES * E3]
                                          .rearrange("p (t e) -> p t e", e=E3)).then_inc(F[3]["dve"], 1)
                elif k < 8:
                    if k > 2:
                        dve.wait_ge(F[3]["dve"], STEPS3 * b + k)
                    choose(k - 1, logit3, E3).then_inc(F[3]["dve"], 1)
                elif k == 8:
                    tt(gate[:, :, :], logit3[:, :, :], bcast(top[:, :, 0], 2, E3), ALU.subtract)\
                        .then_inc(F[3]["diff"], 1)
                else:
                    if k == 9:
                        dve.wait_ge(F[3]["gexp"], b + 1)
                    dve.wait_ge(F[3]["dve"], STEPS3 * b + k - 1)
                    if k == 9:
                        ins = tt(gtmp[:, :, :], gexp[:, :, :], pick[:, :, :], ALU.mult)
                    elif k == 10:
                        ins = nc.vector.reduce_sum(gsum[:, :], gtmp[:, :, :], AX)
                    elif k == 11:
                        ins = ts_(gmax[:, :], gsum[:, :], WSCALE, None, ALU.mult)
                    elif k == 12:
                        ins = nc.vector.reciprocal(gden[:, :], gmax[:, :])
                    else:
                        ins = tt(gate[:, :, :], gtmp[:, :, :], bcast(gden[:, :], 2, E3), ALU.mult)
                    ins.then_inc(F[3]["dve" if k < 13 else "cw"], 1)

            OTHER = {3: "abs", 11: "quant", 16: "quant", 17: "spread", 18: "spread"}

            def small_step(k):
                if k == 0:
                    dve.wait_ge(ld["mlp"], 16)
                elif k == 4:
                    dve.wait_ge(pre["abs_mm"], 1)
                elif k == 12:
                    dve.wait_ge(pre["quant"], 1)
                elif k < 17:
                    dve.wait_ge(pre["dve"], sum(i not in OTHER for i in range(k)))
                t0, t1 = big[:, 1, 2, :], big[:, 1, 3, :]
                i = int(12 <= k < 17)
                sc, inv = qs[:, 1, i:i + 1], qs[:, 2, i:i + 1]
                if k < 2:
                    ins = stt(big[:, 1, 2 + k, :], mw[:, k, :], -1.0, mw[:, k, :], ALU.mult, ALU.max)
                elif k == 2:
                    ins = nc.vector.reduce_sum(qsum[:, :], big[:, 1, 2:4, :], AX)
                elif k == 3:
                    ins = nc.vector.tensor_copy(qs[:, 0, :], qsum[:, :])
                elif k == 4:
                    ins = ts_(qs[:, 0, :], pb[7][:, 64:66], 1.0 / (512 * P), 1e-5, ALU.mult, ALU.max)
                elif k < 7:
                    ins = nc.vector.reciprocal(qs[:, k - 4, :], qs[:, k - 5, :])
                elif k in (7, 12):
                    ins = ts_(t0, mw[:, i, :], sc, 0.5, ALU.mult, ALU.is_gt)
                elif k in (8, 13):
                    ins = ts_(t1, mw[:, i, :], sc, -0.5, ALU.mult, ALU.is_lt)
                elif k in (9, 14):
                    ins = tt(t0, t0, t1, ALU.subtract)
                elif k in (10, 15):
                    ins = stt(t1, t0, inv, mw[:, i, :], ALU.mult, ALU.subtract)
                elif k in (11, 16):
                    ins = tt(wq[:, i, :], mw[:, i, :], t1, ALU.add)
                elif k == 17:
                    dve.wait_ge(ld["bd"], 16)
                    ins = ts_(bd[:, :], bd[:, :], WSCALE, None, ALU.mult)
                else:
                    dve.wait_ge(ld["m2"], 16)
                    for b in range(BATCHES):
                        ins = ts_(m2b[:, b, :, :], bcast(m2[:, b, :], 1, HEADS), -1e30, None, ALU.mult)
                ins.then_inc(pre[OTHER.get(k, "dve")], 1)

            def moe0():
                s = F[0]

                def split(b):
                    dve.wait_ge(s["hh"], b + 1)
                    tt(hl[:, 0, 0:2, :], big[:, 0, 0:2, :], hh[:, 0, 0:2, :], ALU.subtract).then_inc(s["split"], 1)

                def aside(b, left, slot):
                    if slot < 6:
                        ln(b, left, slot + 9)
                    elif slot == 6 and left:
                        low_part(0, b + 1)
                    elif slot == 7:
                        norm_free("f0" if left else "a1", b + 1 if left else 0)
                        ln(b, left, 15)
                    elif slot == 8:
                        ln(b, left, 16)
                    if left and slot in (8, 9):
                        route0(b + 1, slot - 8)
                    elif left and 11 <= slot < 22:
                        route0(b + 1, slot - 9)
                    elif left and 25 <= slot < 32:
                        route0(b + 1, slot - 12)
                    if left and slot == 27:
                        split(b + 1)

                def ln(b, left, *steps):
                    if left > 1:
                        prep("f0", b + 2, *steps)
                    else:
                        prep("a1", 1 - left, *steps)

                def add(b, left, t):
                    dve.wait_ge(s["down"], TILES * b + t + 1)
                    for n in range(E0):
                        at = 2 + 2 * (t % 2) + n // 4
                        src, weight = pb[at][:, (n % 4) * P:(n % 4 + 1) * P], cw[:, t, n:n + 1]
                        if n == 0:
                            ins = ts_(acc[:, t, :], src, weight, None, ALU.mult)
                        else:
                            dve.wait_ge(s["acc"], E0 * (TILES * b + t) + n)
                            ins = stt(acc[:, t, :], src, weight, acc[:, t, :], ALU.mult, ALU.add)
                        ins.then_inc(s["acc"], 1)
                        aside(b, left, E0 * t + n)

                def body(b, left):
                    ln(b, left, *range(9))
                    dve.wait_ge(s["cw"], b + 1)
                    for t in range(TILES):
                        add(b, left, t)
                    add_batch(s, b, TILES * E0)
                    if left:
                        route0(b + 1, 20)

                split(0)
                for k in range(13, 21):
                    route0(0, k)
                with dve.Fori(0, BATCHES - 2) as b:
                    body(b, 2)
                body(BATCHES - 2, 1)
                body(BATCHES - 1, 0)

            def moe1():
                s = F[1]

                def begin(b, first=False):
                    dve.wait_ge(s["cw"], b + 1)
                    nc.vector.tensor_copy(cw[:, :, 0:E1], gate[:, :, 0:E1])
                    if not first:
                        dve.wait_ge(s["x"], b)
                    nc.vector.memset(acc[:, :, :], 0.0).then_inc(s["diff"], 1)
                    dve.wait_ge(s["diff"], b + 1)

                def multiply(b, e):
                    j, at = place(e)
                    for c in range(2):
                        dve.wait_ge(s["act"], 2 * (S1 * b + e) + c + 1)
                        dve.wait_ge(s["up"], 4 * (S1 * b + e) + 2 * c + 2)
                        stt(big[:, j, at + c, :], pb[2 + c][:, :], 1.0 / WSCALE, big[:, j, at + c, :],
                            ALU.mult, ALU.mult).then_inc(s["prod"], 1)


                def body(b, more):
                    def aside(slot):
                        if slot < 17:
                            prep(*following("f1", b, more), slot)
                        elif more and slot == 20:
                            low_part(1, b + 1)
                        elif more and 30 <= slot < 42:
                            route1(b + 1, slot - 30)
                        elif not more and slot < 21:
                            small_step(slot - 17)
                        elif not more and slot in (21, 22):
                            small_step(slot - 4)
                        elif not more and 26 <= slot < 39:
                            small_step(slot - 22)
                        if not more and 28 <= slot < 45:
                            if slot == 43:
                                norm_free("a2", 0)
                            prep("a2", 1, slot - 28)

                    def weights(e):
                        if e < E1:
                            return lambda t: cw[:, t, e:e + 1]
                        return lambda t: 1.0 / (3.0 * WSCALE)

                    for e in range(S1):
                        last = e == S1 - 1
                        if not last:
                            multiply(b, e + 1)
                        elif more:
                            multiply(b + 1, 0)
                        add_expert(s, b, e, S1, BANK_LAST if last else 4 + e % 2, weights(e), aside, 5 * e)
                        aside(5 * e + 4)
                    add_batch(s, b, S1)
                    if more:
                        begin(b + 1)

                begin(0, first=True)
                multiply(0, 0)
                with dve.Fori(0, BATCHES - 1) as b:
                    body(b, True)
                body(BATCHES - 1, False)

            def moe3():
                s = F[3]

                def begin(b, first=False):
                    nc.vector.tensor_copy(cw[:, :, 0:E3], gate[:, :, :])
                    if not first:
                        dve.wait_ge(s["x"], b)
                    dve.wait_ge(s["bias_mm"], b + 1)
                    nc.vector.tensor_copy(acc[:, :, :], pb[6][:, :].rearrange("p (t d) -> p t d", d=P))\
                        .then_inc(s["bias"], 1)
                    dve.wait_ge(s["bias"], b + 1)

                def split(b, e, j, half):
                    at = slice(2 * half, 2 * half + 2)
                    if e == BY_DVE:
                        dve.wait_ge(s["act"], 4 * (E3 * b + e) + 2 * half + 2)
                        nc.vector.tensor_copy(hh[:, j, at, :], big[:, j, at, :]).then_inc(s["high"], 1)
                        dve.wait_ge(s["high"], 2 * b + half + 1)
                    else:
                        dve.wait_ge(s["hh"], 2 * ((E3 - 1) * b + e - (e > BY_DVE)) + half + 1)
                    ins = tt(hl[:, j, at, :], big[:, j, at, :], hh[:, j, at, :], ALU.subtract)
                    if half:
                        ins.then_inc(s["split"], 1)

                def body(b, more):
                    def aside(slot):
                        if not more:
                            return
                        if slot < 17:
                            prep("f3", b + 1, slot)
                        elif slot == 30:
                            low_part(3, b + 1)
                        elif 36 <= slot < 45:
                            route3(b + 1, slot - 36)
                        elif 48 <= slot < 53:
                            route3(b + 1, slot - 39)

                    for e in range(E3):
                        after = (b, e + 1) if e < E3 - 1 else (b + 1, 0)
                        for half in range(2):
                            if e < E3 - 1 or more:
                                split(*after, (e + 1) % 2, half)
                            aside(6 * e + half)
                        add_expert(s, b, e, E3, 4 + e % 2, lambda t: cw[:, t, e:e + 1], aside, 6 * e + 2)
                    add_batch(s, b, E3)
                    if more:
                        begin(b + 1)

                for half in range(2):
                    split(0, 0, 0, half)
                dve.wait_ge(s["cw"], 1)
                begin(0, first=True)
                with dve.Fori(0, BATCHES - 1) as b:
                    body(b, True)
                body(BATCHES - 1, False)

            def prep2(b, step):
                if step < 17:
                    prep("f2", b, step)
                else:
                    if step == 17:
                        dve.wait_ge(M["xn"], b + 1)
                    ln_step(step - 17, LN_COUNT * b, M["ln2"], lambda t: xn[:, t, :], lambda t: xn[:, t, :], M["xn2"])

            def mlp():
                s = M

                def hidden_step(b, k):
                    if k < 2:
                        dve.wait_ge(s["gelu"], TILES * b + 2 * k + 2)
                    ln_step(k, 15 * b, s["dve"], lambda t: big[:, 1, t, :], None, None, 512, norm_h)

                def hidden_norm(b, t):
                    if t == 0:
                        dve.wait_ge(s["dve"], 15 * (b + 1))
                    ts_(big[:, 0, t, :], big[:, 1, t, :], norm_h["mean"][:, t:t + 1], norm_h["rstd"][:, t:t + 1],
                        ALU.subtract, ALU.mult).then_inc(s["n"], 1)

                def add(b):
                    dve.wait_ge(s["down"], TILES * b + TILES)
                    xs = X[:, bass.ds(TILES * b, TILES), :]
                    tt(xs, pb[7][:, :].rearrange("p (t d) -> p t d", d=P), xs, ALU.add).then_inc(s["x"], 1)

                def statistics(b, ahead, steps):
                    for step in range(4, 15):
                        ahead(step)
                    for k in range(15):
                        hidden_step(b, k)
                        for step in (2 * k + 15, 2 * k + 16):
                            if step < steps:
                                ahead(step)

                def body(b, left):
                    def ahead(step):
                        if left > 1:
                            prep2(b + 2, step)
                        else:
                            prep("a3", 0, step)

                    for t in range(TILES):
                        hidden_norm(b, t)
                        if left:
                            ahead(t)
                        else:
                            prep("a3", 1, t)
                    if not left:
                        prep("a3", 1, *range(4, 15))
                        norm_free("a3", 0)
                        prep("a3", 1, 15, 16)
                    if left:
                        statistics(b + 1, ahead, 34 if left > 1 else 17)
                    add(b)

                for step in range(4):
                    prep2(1, step)
                statistics(0, lambda step: prep2(1, step), 34)
                with dve.Fori(0, BATCHES - 2) as b:
                    body(b, 2)
                body(BATCHES - 2, 1)
                body(BATCHES - 1, 0)

            for n, stage in enumerate((lambda: heads(0), moe0, single, moe1, lambda: heads(2), mlp,
                                       lambda: heads(3), moe3)):
                if n < STAGES:
                    stage()


def layout(i):
    c = np.ascontiguousarray

    def wide(a, chunks):
        return a.reshape(chunks, P, -1).transpose(1, 0, 2).reshape(P, -1)

    ctx = i["ctx_1024"].transpose(2, 0, 1)[:, :, None, :]
    ctx = np.broadcast_to(ctx, (P, BATCHES, QUADS, KEYS))
    kv_w = i["L2_xattn_kv_w"]
    att = [i["L0_xattn_Wq"], i["L0_xattn_Wk"], i["L0_xattn_Wv"], i["L0_xattn_Wo"],
           i["L1_xattn_Wq"].T, i["L1_xattn_Wk"].T, i["L1_xattn_Wv"].T,
           i["L2_xattn_q_w"], kv_w[:, :P], kv_w[:, P:], i["L2_xattn_proj_w"],
           i["L3_xattn_w_q"].T, i["L3_xattn_w_k"].T, i["L3_xattn_w_v"].T, i["L3_xattn_w_o"].T]
    kv_b = i["L2_xattn_kv_b"]
    cols = [i["L0_xattn_bq"][:, None], i["L0_xattn_bk"][:, None], i["L1_xattn_bq"][:, None],
            i["L1_xattn_bk"][:, None], i["L2_xattn_q_b"][:, None], kv_b[:P, None],
            i["L3_xattn_b_q"][:, None], i["L3_xattn_b_k"][:, None],
            i["L2_ffn_ln1_g"][:, None], i["L2_ffn_ln1_b"][:, None],
            i["L2_ffn_ln2_g"].reshape(4, P).T, i["L2_ffn_ln2_b"].reshape(4, P).T,
            i["L3_ffn_bup"].reshape(4 * E3, P).T]
    rows = [i["L0_xattn_bv"], i["L1_xattn_bv"], kv_b[P:], i["L3_xattn_b_v"]]
    biases = [i["L0_xattn_bo"], i["L2_xattn_proj_b"], i["L3_xattn_b_o"], i["L2_ffn_b2"], i["L2_ffn_b1"]]
    router = [i["L0_ffn_w_router"].T, i["L1_ffn_Wg"], i["L3_ffn_Wg"]]

    def experts(shared, routed):
        return np.concatenate([routed, shared[None]], 0)

    w1 = experts(i["L1_ffn_Ws1"], i["L1_ffn_We1"]).transpose(1, 0, 2).reshape(P, -1)
    w3 = experts(i["L1_ffn_Ws3"], i["L1_ffn_We3"]).transpose(1, 0, 2).reshape(P, -1)
    w2 = experts(i["L1_ffn_Ws2"], i["L1_ffn_We2"]).reshape(S1, 2, P, P).transpose(2, 0, 1, 3).reshape(P, -1)
    down0 = i["L0_ffn_w_down"].transpose(2, 0, 1).reshape(2, P, E0, P).transpose(1, 0, 2, 3).reshape(P, -1)
    up3 = i["L3_ffn_Wup"].transpose(1, 0, 2).reshape(P, -1)
    down3 = i["L3_ffn_Wdown"].reshape(E3, 4, P, P).transpose(2, 0, 1, 3).reshape(P, -1)
    moe = [i["L0_ffn_w_gate"].T, down0, w1, w3, w2, up3, down3]
    mlp = [i["L2_ffn_w1"].T, wide(i["L2_ffn_w2"].T, 4)]

    consts = np.zeros((P, K_COLS), np.float32)
    p = np.arange(P)
    consts[p, K_ID + p] = 1.0
    consts[:, K_TRI:K_TRI + P] = p[:, None] <= p[None, :]
    consts[:, K_HEAD:K_HEAD + HEADS] = p[:, None] // DEPTH == np.arange(HEADS)[None, :]
    consts[:, K_QUAD:K_QUAD + QUADS] = p[:, None] // KEYS == np.arange(QUADS)[None, :]
    consts[:, K_IOTA:K_IOTA + 12] = np.arange(12)[None, :]
    return {
        "x": c(i["x"].reshape(BATCHES * SEQ, P)),
        "ctx": c(ctx),
        "attw": c(np.concatenate([a.reshape(P, 1, P) for a in att], 1)),
        "cols": c(np.concatenate(cols, 1)),
        "rows": c(np.concatenate(rows)[None, :]),
        "biases": c(np.concatenate(biases)[None, :]),
        "router": c(np.concatenate(router, 1)),
        "moe_w": c(np.concatenate(moe, 1)),
        "mlp_w": c(np.concatenate([a.reshape(P, 1, 512) for a in mlp], 1)),
        "bdown": c(i["L3_ffn_bdown"]),
        "mask1": c(i["mask_BxSxS2_ik1"].reshape(BATCHES * SEQ, KEYS)),
        "mask2": c(i["mask_BxS2_bk0"].reshape(1, BATCHES, KEYS)),
        "consts": consts,
    }


def kernel(**inputs):
    import concourse.bacc as bacc
    from concourse.bass_utils import run_bass_kernel_spmd as run

    nc = bacc.Bacc("TRN2", target_bir_lowering=False, num_devices=1)
    arrays = layout({k: np.asarray(v) for k, v in inputs.items()})
    args = [nc.dram_tensor(n, a.shape, mybir.dt.from_np(a.dtype), kind="ExternalInput").ap()
            for n, a in arrays.items()]
    out = nc.dram_tensor("out", (BATCHES * SEQ, P), F32, kind="ExternalOutput").ap()
    build(nc, *args, out)
    r = run(nc, [arrays], core_ids=[0])
    return r.results[0]["out"].reshape(BATCHES, SEQ, P)
```
